# Optimizing a Trainium2 kernel written in Bass

```python
import numpy as np
import jax
import jax.numpy as jnp

def _softmax(x, axis=-1):
    return jax.nn.softmax(x, axis=axis)

def _gelu(x):
    return jax.nn.gelu(x, approximate=True)

def _silu(x):
    return jax.nn.silu(x)

def _sigmoid(x):
    return jax.nn.sigmoid(x)

def _layernorm(x, axis=-1, eps=1e-05):
    m = jnp.mean(x, axis=axis, keepdims=True)
    v = jnp.var(x, axis=axis, keepdims=True)
    return (x - m) / jnp.sqrt(v + eps)

def _scatter_add(tgt, idx, src, axis=0):
    return tgt.at[idx].add(src)

def _segment_sum(src, seg, n):
    return jax.ops.segment_sum(src, seg, n)
kernel_name = 'mk_lm_tower_d1_tok_ids768_r4_165505'

def setup_inputs(seed: int=0):
    np.random.seed(seed)
    _w = jnp.asarray

    def _rec_inputs():
        import jax
        import jax.numpy as jnp
        _rk = jax.random.key(seed)
        x = jax.random.randint(jax.random.fold_in(_rk, 1), (1, 2048), 0, 31921, jnp.int32)
        return x
    x = _rec_inputs()

    def _L0_tok_setup():
        import jax, jax.numpy as jnp
        import numpy as np
        B, L, V, D_MODEL = (1, 512, 8000, 192)
        N_LAYER, D_STATE, EXPAND, D_CONV = (2, 16, 2, 4)
        D_INNER = EXPAND * D_MODEL
        DT_RANK = -(-D_MODEL // D_STATE)
        EPS = 1e-05

        def _rmsnorm(x, w):
            return x * jax.lax.rsqrt(jnp.mean(x * x, axis=-1, keepdims=True) + EPS) * w

        def _selective_scan(u, delta, A, Bm, Cm, D):
            deltaA = jnp.exp(delta[..., None] * A)
            dBu = delta[..., None] * Bm[:, :, None, :] * u[..., None]

            def comb(c1, c2):
                a1, b1 = c1
                a2, b2 = c2
                return (a2 * a1, a2 * b1 + b2)
            _, h = jax.lax.associative_scan(comb, (deltaA, dBu), axis=1)
            y = jnp.einsum('bldn,bln->bld', h, Cm)
            return y + u * D

        def _mamba_block(x, in_proj_w, conv_w, conv_b, x_proj_w, dt_proj_w, dt_proj_b, A_log, D, out_proj_w):
            xz = x @ in_proj_w
            xr, res = jnp.split(xz, 2, axis=-1)
            xc = jax.lax.conv_general_dilated(jnp.swapaxes(xr, 1, 2), conv_w, (1,), [(D_CONV - 1, 0)], feature_group_count=D_INNER, dimension_numbers=('NCH', 'OIH', 'NCH'))
            xr = jax.nn.silu(jnp.swapaxes(xc + conv_b[:, None], 1, 2))
            A = -jnp.exp(A_log)
            x_dbl = xr @ x_proj_w
            dt, Bm, Cm = jnp.split(x_dbl, [DT_RANK, DT_RANK + D_STATE], axis=-1)
            delta = jax.nn.softplus(dt @ dt_proj_w + dt_proj_b)
            y = _selective_scan(xr, delta, A, Bm, Cm, D)
            return y * jax.nn.silu(res) @ out_proj_w
        key = jax.random.key(seed)
        ks = jax.random.split(key, 12)
        s = 0.02
        inp = {'input_ids': jax.random.randint(ks[0], (B, L), 0, V), 'emb': jax.random.normal(ks[1], (V, D_MODEL), jnp.float32) * s, 'norm_w': jnp.ones((N_LAYER, D_MODEL), jnp.float32), 'in_proj_w': jax.random.normal(ks[2], (N_LAYER, D_MODEL, 2 * D_INNER), jnp.float32) * s, 'conv_w': jax.random.normal(ks[3], (N_LAYER, D_INNER, 1, D_CONV), jnp.float32) * s, 'conv_b': jnp.zeros((N_LAYER, D_INNER), jnp.float32), 'x_proj_w': jax.random.normal(ks[4], (N_LAYER, D_INNER, DT_RANK + 2 * D_STATE), jnp.float32) * s, 'dt_proj_w': jax.random.normal(ks[5], (N_LAYER, DT_RANK, D_INNER), jnp.float32) * s, 'dt_proj_b': jax.random.normal(ks[6], (N_LAYER, D_INNER), jnp.float32) * s, 'A_log': jnp.tile(jnp.log(jnp.arange(1, D_STATE + 1, dtype=jnp.float32)), (N_LAYER, D_INNER, 1)), 'D': jnp.ones((N_LAYER, D_INNER), jnp.float32), 'out_proj_w': jax.random.normal(ks[7], (N_LAYER, D_INNER, D_MODEL), jnp.float32) * s}
        return inp
    _L0_tok_all = _L0_tok_setup()
    _L0_tok_in = {k: v for k, v in _L0_tok_all.items() if k in ('emb', 'norm_w', 'in_proj_w', 'conv_w', 'conv_b', 'x_proj_w', 'dt_proj_w', 'dt_proj_b', 'A_log', 'D', 'out_proj_w')}
    del _L0_tok_all

    def _L0_attn_setup():
        import jax, jax.numpy as jnp
        import numpy as np
        import math
        B, N, D, H = (2, 512, 192, 12)
        DH = D // H
        M = int(DH * math.log(DH))
        FF = 4 * D
        EPS_KER = 0.0001
        EPS_DEN = 1e-06
        CHUNK = 64

        def layer_norm(x, g, b):
            mu = x.mean(-1, keepdims=True)
            var = ((x - mu) ** 2).mean(-1, keepdims=True)
            return (x - mu) / jnp.sqrt(var + 1e-05) * g + b

        def softmax_kernel(data, proj, is_query):
            dn = data.shape[-1] ** (-0.25)
            ratio = proj.shape[0] ** (-0.5)
            dd = jnp.einsum('bhnd,md->bhnm', data * dn, proj)
            diag = (data ** 2).sum(-1, keepdims=True) * 0.5 * dn ** 2
            if is_query:
                mx = jnp.max(dd, axis=-1, keepdims=True)
            else:
                mx = jnp.max(dd)
            return ratio * (jnp.exp(dd - diag - mx) + EPS_KER)

        def causal_linear_attention(q, k, v, chunk=CHUNK):
            b, h, n, m = q.shape
            e = v.shape[-1]
            nc = n // chunk
            qs = q.reshape(b, h, nc, chunk, m).transpose(2, 0, 1, 3, 4)
            ks = k.reshape(b, h, nc, chunk, m).transpose(2, 0, 1, 3, 4)
            vs = v.reshape(b, h, nc, chunk, e).transpose(2, 0, 1, 3, 4)
            S0 = jnp.zeros((b, h, m, e), q.dtype)
            z0 = jnp.zeros((b, h, m), q.dtype)

            def step(carry, inp):
                S, z = carry
                qc, kc, vc = inp
                k_cum = jnp.cumsum(kc, axis=2) + z[:, :, None, :]
                ctx = jnp.cumsum(jnp.einsum('bhcm,bhce->bhcme', kc, vc), axis=2) + S[:, :, None, :, :]
                den = jnp.einsum('bhcm,bhcm->bhc', qc, k_cum + EPS_DEN)
                out = jnp.einsum('bhcme,bhcm->bhce', ctx, qc) / den[..., None]
                return ((ctx[:, :, -1], k_cum[:, :, -1]), out)
            _, outs = jax.lax.scan(step, (S0, z0), (qs, ks, vs))
            return outs.transpose(1, 2, 0, 3, 4).reshape(b, h, n, e)
        key = jax.random.key(seed)
        ks = jax.random.split(key, 12)
        s = 0.02
        return {'x': jax.random.normal(ks[0], (B, N, D), jnp.float32), 'ln1_g': jnp.ones((D,), jnp.float32), 'ln1_b': jnp.zeros((D,), jnp.float32), 'Wq': jax.random.normal(ks[1], (D, D), jnp.float32) * s, 'bq': jnp.zeros((D,), jnp.float32), 'Wk': jax.random.normal(ks[2], (D, D), jnp.float32) * s, 'bk': jnp.zeros((D,), jnp.float32), 'Wv': jax.random.normal(ks[3], (D, D), jnp.float32) * s, 'bv': jnp.zeros((D,), jnp.float32), 'Wo': jax.random.normal(ks[4], (D, D), jnp.float32) * s, 'bo': jnp.zeros((D,), jnp.float32), 'proj': jax.random.normal(ks[5], (M, DH), jnp.float32), 'ln2_g': jnp.ones((D,), jnp.float32), 'ln2_b': jnp.zeros((D,), jnp.float32), 'W1': jax.random.normal(ks[6], (D, FF), jnp.float32) * s, 'b1': jnp.zeros((FF,), jnp.float32), 'W2': jax.random.normal(ks[7], (FF, D), jnp.float32) * s, 'b2': jnp.zeros((D,), jnp.float32)}
    _L0_attn_all = _L0_attn_setup()
    _L0_attn_in = {k: v for k, v in _L0_attn_all.items() if k in ('ln1_g', 'ln1_b', 'Wq', 'bq', 'Wk', 'bk', 'Wv', 'bv', 'Wo', 'bo', 'proj', 'ln2_g', 'ln2_b', 'W1', 'b1', 'W2', 'b2')}
    del _L0_attn_all

    def _L0_ffn_setup():
        import jax, jax.numpy as jnp
        import numpy as np
        EPS_NORM = 1e-06
        EPS_LN = 1e-05

        def _layernorm(x, g, b):
            mu = jnp.mean(x, axis=-1, keepdims=True)
            var = jnp.mean(jnp.square(x - mu), axis=-1, keepdims=True)
            return (x - mu) * jax.lax.rsqrt(var + EPS_LN) * g + b
        key = jax.random.key(seed)
        ks = jax.random.split(key, 6)
        b, m, d = (8, 256, 192)
        n, p = (64, 16)
        h = 2 * d
        x = jax.random.normal(ks[0], (b, m, d), dtype=jnp.float32)
        phi = jax.random.normal(ks[1], (n, p, d), dtype=jnp.float32)
        ln_g = jnp.ones((n, d), dtype=jnp.float32)
        ln_b = jnp.zeros((n, d), dtype=jnp.float32)
        w1 = jax.random.normal(ks[2], (n, d, h), dtype=jnp.float32) * (1.0 / np.sqrt(d))
        b1 = jax.random.normal(ks[3], (n, h), dtype=jnp.float32) * 0.01
        w2 = jax.random.normal(ks[4], (n, h, d), dtype=jnp.float32) * (1.0 / np.sqrt(h))
        b2 = jax.random.normal(ks[5], (n, d), dtype=jnp.float32) * 0.01
        return {'x': x, 'phi': phi, 'ln_g': ln_g, 'ln_b': ln_b, 'w1': w1, 'b1': b1, 'w2': w2, 'b2': b2}
    _L0_ffn_all = _L0_ffn_setup()
    _L0_ffn_in = {k: v for k, v in _L0_ffn_all.items() if k in ('phi', 'ln_g', 'ln_b', 'w1', 'b1', 'w2', 'b2')}
    del _L0_ffn_all
    return {'x': x, 'L0_tok_emb': _L0_tok_in['emb'], 'L0_tok_norm_w': _L0_tok_in['norm_w'], 'L0_tok_in_proj_w': _L0_tok_in['in_proj_w'], 'L0_tok_conv_w': _L0_tok_in['conv_w'], 'L0_tok_conv_b': _L0_tok_in['conv_b'], 'L0_tok_x_proj_w': _L0_tok_in['x_proj_w'], 'L0_tok_dt_proj_w': _L0_tok_in['dt_proj_w'], 'L0_tok_dt_proj_b': _L0_tok_in['dt_proj_b'], 'L0_tok_A_log': _L0_tok_in['A_log'], 'L0_tok_D': _L0_tok_in['D'], 'L0_tok_out_proj_w': _L0_tok_in['out_proj_w'], 'L0_attn_ln1_g': _L0_attn_in['ln1_g'], 'L0_attn_ln1_b': _L0_attn_in['ln1_b'], 'L0_attn_Wq': _L0_attn_in['Wq'], 'L0_attn_bq': _L0_attn_in['bq'], 'L0_attn_Wk': _L0_attn_in['Wk'], 'L0_attn_bk': _L0_attn_in['bk'], 'L0_attn_Wv': _L0_attn_in['Wv'], 'L0_attn_bv': _L0_attn_in['bv'], 'L0_attn_Wo': _L0_attn_in['Wo'], 'L0_attn_bo': _L0_attn_in['bo'], 'L0_attn_proj': _L0_attn_in['proj'], 'L0_attn_ln2_g': _L0_attn_in['ln2_g'], 'L0_attn_ln2_b': _L0_attn_in['ln2_b'], 'L0_attn_W1': _L0_attn_in['W1'], 'L0_attn_b1': _L0_attn_in['b1'], 'L0_attn_W2': _L0_attn_in['W2'], 'L0_attn_b2': _L0_attn_in['b2'], 'L0_ffn_phi': _L0_ffn_in['phi'], 'L0_ffn_ln_g': _L0_ffn_in['ln_g'], 'L0_ffn_ln_b': _L0_ffn_in['ln_b'], 'L0_ffn_w1': _L0_ffn_in['w1'], 'L0_ffn_b1': _L0_ffn_in['b1'], 'L0_ffn_w2': _L0_ffn_in['w2'], 'L0_ffn_b2': _L0_ffn_in['b2']}

def reference(x, L0_tok_emb, L0_tok_norm_w, L0_tok_in_proj_w, L0_tok_conv_w, L0_tok_conv_b, L0_tok_x_proj_w, L0_tok_dt_proj_w, L0_tok_dt_proj_b, L0_tok_A_log, L0_tok_D, L0_tok_out_proj_w, L0_attn_ln1_g, L0_attn_ln1_b, L0_attn_Wq, L0_attn_bq, L0_attn_Wk, L0_attn_bk, L0_attn_Wv, L0_attn_bv, L0_attn_Wo, L0_attn_bo, L0_attn_proj, L0_attn_ln2_g, L0_attn_ln2_b, L0_attn_W1, L0_attn_b1, L0_attn_W2, L0_attn_b2, L0_ffn_phi, L0_ffn_ln_g, L0_ffn_ln_b, L0_ffn_w1, L0_ffn_b1, L0_ffn_w2, L0_ffn_b2):
    import jax
    import jax.numpy as jnp

    def _L0_tok_ref(input_ids, emb, norm_w, in_proj_w, conv_w, conv_b, x_proj_w, dt_proj_w, dt_proj_b, A_log, D, out_proj_w):
        import jax, jax.numpy as jnp
        import numpy as np
        B, L, V, D_MODEL = (1, 512, 8000, 192)
        N_LAYER, D_STATE, EXPAND, D_CONV = (2, 16, 2, 4)
        D_INNER = EXPAND * D_MODEL
        DT_RANK = -(-D_MODEL // D_STATE)
        EPS = 1e-05

        def _rmsnorm(x, w):
            return x * jax.lax.rsqrt(jnp.mean(x * x, axis=-1, keepdims=True) + EPS) * w

        def _selective_scan(u, delta, A, Bm, Cm, D):
            deltaA = jnp.exp(delta[..., None] * A)
            dBu = delta[..., None] * Bm[:, :, None, :] * u[..., None]

            def comb(c1, c2):
                a1, b1 = c1
                a2, b2 = c2
                return (a2 * a1, a2 * b1 + b2)
            _, h = jax.lax.associative_scan(comb, (deltaA, dBu), axis=1)
            y = jnp.einsum('bldn,bln->bld', h, Cm)
            return y + u * D

        def _mamba_block(x, in_proj_w, conv_w, conv_b, x_proj_w, dt_proj_w, dt_proj_b, A_log, D, out_proj_w):
            xz = x @ in_proj_w
            xr, res = jnp.split(xz, 2, axis=-1)
            xc = jax.lax.conv_general_dilated(jnp.swapaxes(xr, 1, 2), conv_w, (1,), [(D_CONV - 1, 0)], feature_group_count=D_INNER, dimension_numbers=('NCH', 'OIH', 'NCH'))
            xr = jax.nn.silu(jnp.swapaxes(xc + conv_b[:, None], 1, 2))
            A = -jnp.exp(A_log)
            x_dbl = xr @ x_proj_w
            dt, Bm, Cm = jnp.split(x_dbl, [DT_RANK, DT_RANK + D_STATE], axis=-1)
            delta = jax.nn.softplus(dt @ dt_proj_w + dt_proj_b)
            y = _selective_scan(xr, delta, A, Bm, Cm, D)
            return y * jax.nn.silu(res) @ out_proj_w
        x = emb[input_ids]
        for i in range(N_LAYER):
            x = x + _mamba_block(_rmsnorm(x, norm_w[i]), in_proj_w[i], conv_w[i], conv_b[i], x_proj_w[i], dt_proj_w[i], dt_proj_b[i], A_log[i], D[i], out_proj_w[i])
        return x

    def _L0_attn_ref(x, ln1_g, ln1_b, Wq, bq, Wk, bk, Wv, bv, Wo, bo, proj, ln2_g, ln2_b, W1, b1, W2, b2):
        import jax, jax.numpy as jnp
        import numpy as np
        import math
        B, N, D, H = (2, 512, 192, 12)
        DH = D // H
        M = int(DH * math.log(DH))
        FF = 4 * D
        EPS_KER = 0.0001
        EPS_DEN = 1e-06
        CHUNK = 64

        def layer_norm(x, g, b):
            mu = x.mean(-1, keepdims=True)
            var = ((x - mu) ** 2).mean(-1, keepdims=True)
            return (x - mu) / jnp.sqrt(var + 1e-05) * g + b

        def softmax_kernel(data, proj, is_query):
            dn = data.shape[-1] ** (-0.25)
            ratio = proj.shape[0] ** (-0.5)
            dd = jnp.einsum('bhnd,md->bhnm', data * dn, proj)
            diag = (data ** 2).sum(-1, keepdims=True) * 0.5 * dn ** 2
            if is_query:
                mx = jnp.max(dd, axis=-1, keepdims=True)
            else:
                mx = jnp.max(dd)
            return ratio * (jnp.exp(dd - diag - mx) + EPS_KER)

        def causal_linear_attention(q, k, v, chunk=CHUNK):
            b, h, n, m = q.shape
            e = v.shape[-1]
            nc = n // chunk
            qs = q.reshape(b, h, nc, chunk, m).transpose(2, 0, 1, 3, 4)
            ks = k.reshape(b, h, nc, chunk, m).transpose(2, 0, 1, 3, 4)
            vs = v.reshape(b, h, nc, chunk, e).transpose(2, 0, 1, 3, 4)
            S0 = jnp.zeros((b, h, m, e), q.dtype)
            z0 = jnp.zeros((b, h, m), q.dtype)

            def step(carry, inp):
                S, z = carry
                qc, kc, vc = inp
                k_cum = jnp.cumsum(kc, axis=2) + z[:, :, None, :]
                ctx = jnp.cumsum(jnp.einsum('bhcm,bhce->bhcme', kc, vc), axis=2) + S[:, :, None, :, :]
                den = jnp.einsum('bhcm,bhcm->bhc', qc, k_cum + EPS_DEN)
                out = jnp.einsum('bhcme,bhcm->bhce', ctx, qc) / den[..., None]
                return ((ctx[:, :, -1], k_cum[:, :, -1]), out)
            _, outs = jax.lax.scan(step, (S0, z0), (qs, ks, vs))
            return outs.transpose(1, 2, 0, 3, 4).reshape(b, h, n, e)
        b, n, d = x.shape
        h = layer_norm(x, ln1_g, ln1_b)
        q = (h @ Wq + bq).reshape(b, n, H, DH).transpose(0, 2, 1, 3)
        k = (h @ Wk + bk).reshape(b, n, H, DH).transpose(0, 2, 1, 3)
        v = (h @ Wv + bv).reshape(b, n, H, DH).transpose(0, 2, 1, 3)
        qp = softmax_kernel(q, proj, True)
        kp = softmax_kernel(k, proj, False)
        o = causal_linear_attention(qp, kp, v)
        o = o.transpose(0, 2, 1, 3).reshape(b, n, d)
        x = x + o @ Wo + bo
        h2 = layer_norm(x, ln2_g, ln2_b)
        y = jax.nn.gelu(h2 @ W1 + b1, approximate=False) @ W2 + b2
        return x + y

    def _L0_ffn_ref(x, phi, ln_g, ln_b, w1, b1, w2, b2):
        import jax, jax.numpy as jnp
        import numpy as np
        EPS_NORM = 1e-06
        EPS_LN = 1e-05

        def _layernorm(x, g, b):
            mu = jnp.mean(x, axis=-1, keepdims=True)
            var = jnp.mean(jnp.square(x - mu), axis=-1, keepdims=True)
            return (x - mu) * jax.lax.rsqrt(var + EPS_LN) * g + b
        phi_n = phi * jax.lax.rsqrt(jnp.sum(jnp.square(phi), axis=0, keepdims=True) + EPS_NORM)
        bsz, m, d = x.shape
        n, p, _ = phi_n.shape
        logits = jnp.einsum('bmd,npd->bmnp', x, phi_n)
        D = jax.nn.softmax(logits, axis=1)
        C = jax.nn.softmax(logits.reshape(bsz, m, n * p), axis=-1)
        Xs = jnp.einsum('bmd,bmnp->bnpd', x, D)
        hdn = _layernorm(Xs, ln_g[:, None, :], ln_b[:, None, :])
        hdn = jnp.einsum('bnpd,ndh->bnph', hdn, w1) + b1[:, None, :]
        hdn = jax.nn.gelu(hdn, approximate=False)
        Ys = jnp.einsum('bnph,nhd->bnpd', hdn, w2) + b2[:, None, :]
        Ys = Ys.reshape(bsz, n * p, d)
        Y = jnp.einsum('bsd,bms->bmd', Ys, C)
        return Y
    h = _L0_tok_ref(x, L0_tok_emb, L0_tok_norm_w, L0_tok_in_proj_w, L0_tok_conv_w, L0_tok_conv_b, L0_tok_x_proj_w, L0_tok_dt_proj_w, L0_tok_dt_proj_b, L0_tok_A_log, L0_tok_D, L0_tok_out_proj_w)
    h = h + _L0_attn_ref(_layernorm(h, axis=-1), L0_attn_ln1_g, L0_attn_ln1_b, L0_attn_Wq, L0_attn_bq, L0_attn_Wk, L0_attn_bk, L0_attn_Wv, L0_attn_bv, L0_attn_Wo, L0_attn_bo, L0_attn_proj, L0_attn_ln2_g, L0_attn_ln2_b, L0_attn_W1, L0_attn_b1, L0_attn_W2, L0_attn_b2)
    h = h + _L0_ffn_ref(_layernorm(h, axis=-1), L0_ffn_phi, L0_ffn_ln_g, L0_ffn_ln_b, L0_ffn_w1, L0_ffn_b1, L0_ffn_w2, L0_ffn_b2)
    return h

_drawn_inputs = setup_inputs


def setup_inputs(seed=0):
    import zlib

    import numpy as np

    out = dict(_drawn_inputs(seed))
    spreads = {'L0_tok_norm_w': (1.0, 0.2),
     'L0_tok_conv_b': (0.0, 0.1),
     'L0_tok_D': (1.0, 0.2),
     'L0_attn_ln1_g': (1.0, 0.6),
     'L0_attn_ln1_b': (0.0, 0.8),
     'L0_attn_bq': (0.0, 2.0),
     'L0_attn_bk': (0.0, 0.8),
     'L0_attn_bv': (0.0, 0.27),
     'L0_attn_bo': (0.0, 0.1),
     'L0_attn_ln2_g': (1.0, 0.6),
     'L0_attn_ln2_b': (0.0, 0.8),
     'L0_attn_b1': (0.0, 0.1),
     'L0_attn_b2': (0.0, 0.1),
     'L0_ffn_ln_g': (1.0, 0.2),
     'L0_ffn_ln_b': (0.0, 0.51)}
    factors = {'L0_tok_conv_w': 2.717,
     'L0_tok_x_proj_w': 8.0,
     'L0_tok_dt_proj_w': 200.0,
     'L0_tok_dt_proj_b': 200.0,
     'L0_tok_A_log': 200.0,
     'L0_attn_Wq': 64.0,
     'L0_attn_Wk': 8.0,
     'L0_attn_proj': 64.0,
     'L0_ffn_b1': 36.61,
     'L0_ffn_b2': 24.187}
    for name, (base, spread) in spreads.items():
        noise = np.random.default_rng([zlib.crc32(name.encode()), seed]).standard_normal(out[name].shape)
        drawn = base * np.exp(spread * noise) if base else spread * noise
        out[name] = jnp.asarray(drawn.astype(out[name].dtype))
    for name, factor in factors.items():
        out[name] = (out[name] * factor).astype(out[name].dtype)
    return out
```

```python
from contextlib import ExitStack

import numpy as np

import concourse.bass as bass
from concourse import mybir

F32 = mybir.dt.float32
BF16 = mybir.dt.bfloat16
I32 = mybir.dt.int32
ALU = mybir.AluOpType
ACT = mybir.ActivationFunctionType
AX = mybir.AxisListType

P = 128
L = 2048
NT = L // P
D = 192
KD = 2
DP = D // KD
CH = 512
NCH = L // CH
TPC = CH // P
V = 8000
NL = 2
DI = 384
MI = DI // P
NS = 16
RK = 12
NX = 2 * NS
TAPS = 4
H = 12
DH = 16
HK = H // KD
M = 44
MP = 64
HP = H // 2
FF = 768
MF = FF // P
NE = 64
SL = 16
S = NE * SL
ST = S // P
EG = P // SL
HE = 384
MH = HE // P
A_LOG_MAX = 80.0
LN2 = 0.6931471


class Core:
    pass


def sems(nc, g, names):
    made = [nc.alloc_semaphore(name=n) for n in names.split()]
    g.live += made
    return made


def retire_semaphores(nc, g):
    nc.clear_and_free_semaphores(g.live)
    nc.all_engine_barrier()
    g.live = []


def ks(w):
    return w.rearrange("(k p) n -> p k n", p=DP)


def col(v, p):
    return v.rearrange("(k p) -> p k", p=p)


def load_and_gather(nc, g):
    s_ids, g.s_w, s_gather, s_cst, s_idx = sems(nc, g, "ids_in mamba_weights_in rows_in constants_made indices_made")
    with ExitStack() as local, nc.allow_non_contiguous_dma(reason="small weights"):
        ids = local.enter_context(nc.sbuf_tensor("ids", [P, NT], I32))
        wrap = local.enter_context(nc.sbuf_tensor("wrap", [P, NT], F32))
        idsf = local.enter_context(nc.sbuf_tensor("idsf", [P, NT], F32))
        idx = local.enter_context(nc.sbuf_tensor("idx", [P, NT], I32))
        block = local.enter_context(nc.Block())

        @block.sync
        def _(sp):
            sp.dma_start(ids[:, :], g.ids.rearrange("a (i p) -> p (a i)", p=P)).then_inc(s_ids, 16)
            n = 0
            for l in range(NL):
                for dst, src in (
                    (g.w_in[:, l], ks(g.tok["in_proj_w"][l])),
                    (g.norm_w_c[:, l, :], col(g.tok["norm_w"][l], DP)),
                    (g.conv_wc[:, l, :, :], g.tok["conv_w"][l].rearrange("(m p) a k -> p m (a k)", p=P)),
                    (g.conv_bc[:, l, :], col(g.tok["conv_b"][l], P)),
                    (g.w_x[:, l, :, 0:NX], g.tok["x_proj_w"][l].rearrange("(m p) n -> p m n", p=P)[:, :, RK:RK + NX]),
                    (g.w_x[:, l, :, NX:NX + RK], g.tok["x_proj_w"][l].rearrange("(m p) n -> p m n", p=P)[:, :, 0:RK]),
                    (g.w_dt[:, l, :], g.tok["dt_proj_w"][l]),
                    (g.dt_bc[:, l, :], col(g.tok["dt_proj_b"][l], P)),
                    (g.a_neg[:, l, :, :], g.tok["A_log"][l].rearrange("(m p) n -> p m n", p=P)),
                    (g.d_c[:, l, :], col(g.tok["D"][l], P)),
                    (g.w_out[:, l], g.tok["out_proj_w"][l].rearrange("(m p) n -> p m n", p=P)),
                ):
                    sp.dma_start(dst, src).then_inc(g.s_w, 16)
                    n += 16
            g.n_w = n
            sp.wait_ge(s_gather, 16 * NT)
            sp.wait_ge(g.s_w, n)

        @block.vector
        def _(dve):
            dve.wait_ge(s_ids, 16)
            dve.tensor_scalar(wrap[:, :], ids[:, :], 0.0, float(V), ALU.is_lt, ALU.mult).then_inc(s_idx, 1)
            dve.wait_ge(s_idx, 1)
            dve.tensor_tensor(idsf[:, :], ids[:, :], wrap[:, :], ALU.add).then_inc(s_idx, 1)
            dve.wait_ge(s_idx, 2)
            dve.tensor_scalar(idx[:, :], idsf[:, :], 0.0, float(V - 1), ALU.max, ALU.min).then_inc(s_idx, 1)
            dve.wait_ge(g.s_w, g_total_w(g))
            dve.tensor_scalar(g.a_neg[:, :, :, :], g.a_neg[:, :, :, :], A_LOG_MAX, None, ALU.min).then_inc(s_idx, 1)
            dve.wait_ge(s_idx, 5)
            dve.tensor_scalar(g.a_neg[:, :, :, :], g.a_neg[:, :, :, :], -1.0, None, ALU.mult).then_inc(s_idx, 1)

        @block.scalar
        def _(act):
            act.wait_ge(s_idx, 4)
            act.activation(g.a_neg[:, :, :, :], g.a_neg[:, :, :, :], ACT.Exp).then_inc(s_idx, 1)

        @block.gpsimd
        def _(pool):
            pool.memset(g.ident[:, :], 0.0).then_inc(s_cst, 1)
            pool.memset(g.sel[:, :, :], 0.0).then_inc(s_cst, 1)
            pool.memset(g.causal[:, :], 1.0).then_inc(s_cst, 1)
            pool.memset(g.ones[:, :], 1.0).then_inc(s_cst, 1)
            pool.memset(g.slot_of[:, :], 1.0).then_inc(s_cst, 1)
            pool.memset(g.head_of[:, :], 0.5).then_inc(s_cst, 1)
            pool.wait_ge(s_cst, 6)
            pool.affine_select(out=g.ident[:, :], in_=g.ident[:, :], compare_op=ALU.not_equal, fill=1.0,
                               base=0, pattern=[[-1, P]], channel_multiplier=1).then_inc(s_cst, 1)
            pool.affine_select(out=g.causal[:, :], in_=g.causal[:, :], compare_op=ALU.is_ge, fill=0.0,
                               base=0, pattern=[[1, P]], channel_multiplier=-1).then_inc(s_cst, 1)
            for a in range(3):
                pool.affine_select(out=g.sel[:, :, :], in_=g.sel[:, :, :], compare_op=ALU.not_equal, fill=1.0,
                                   base=-NX * a, pattern=[[-1, NX], [0, P]],
                                   channel_multiplier=1).then_inc(s_cst, 1)
                pool.wait_ge(s_cst, 9 + a)
            for out, n, a in ((g.head_of, HK, -DH), (g.slot_of, P, 1)):
                cm = 1 if a < 0 else -SL
                pool.affine_select(out=out[:, :], in_=out[:, :], compare_op=ALU.is_ge, fill=0.0,
                                   base=0, pattern=[[a, n]], channel_multiplier=cm).then_inc(s_cst, 1)
            pool.wait_ge(s_cst, 13)
            for out, n, a in ((g.head_of, HK, DH), (g.slot_of, P, -1)):
                cm = -1 if a > 0 else SL
                pool.affine_select(out=out[:, :], in_=out[:, :], compare_op=ALU.is_ge, fill=0.0,
                                   base=DH - 1, pattern=[[a, n]], channel_multiplier=cm).then_inc(s_cst, 1)
            pool.wait_ge(s_idx, 3)
            for i in range(NT):
                pool.indirect_dma_start(g.x[:, i, :], None, g.tok["emb"],
                                        bass.IndirectOffsetOnAxis(ap=idx[:, i:i + 1], axis=0)).then_inc(s_gather, 16)
            pool.wait_ge(s_cst, 15)


def g_total_w(g):
    return 16 * 11 * NL


def mamba_front(nc, g, l):
    (sumsq, meansq, rms, rstd_done, xs_ready, tr_done, xT_ready, proj_done, xr_ready, res_ready, conv_step,
     conv_done, u_ready, xp_done, bc_ready, dtT_ready, split_step, dt_done, abs_done, exp_done, ln_done,
     sp_step, delta_ready) = sems(nc, g, " ".join(f"{n}{l}" for n in (
        "sumsq meansq rms rstd_done xs_ready transposed xT_ready projected xr_ready res_ready conv_step "
        "conv_done u_ready x_projected bc_ready dtT_ready split_step dt_projected abs_done exp_done ln_done "
        "softplus_step delta_ready").split()))
    with ExitStack() as local:
        def sb(name, shape, dt=F32):
            return local.enter_context(nc.sbuf_tensor(f"{name}{l}", shape, dt))
        ss = sb("ss", [P, NT])
        rstd = sb("rstd", [P, NT])
        ax = sb("ax", [P, 2, MI, CH])
        dd = sb("dd", [P, 2, MI, CH])
        cv = sb("cv", [P, MI, CH])
        bcf = sb("bcf", [NX, 2, CH])
        mid = sb("mid", [NX, 2, CH], BF16)
        dtT = sb("dtT", [RK, 2, CH])
        xs = g.delta[:, :, :].rearrange("p m t -> p (m t)")[:, 0:NT * D].rearrange("p (i d) -> p i d", d=D)
        xT = g.du[0:DP, :, :].rearrange("p m t -> p (m t)")[:, 0:KD * L].rearrange("p (k t) -> p k t", k=KD)
        banks = [local.enter_context(nc.psum_tensor(f"fb{l}_{i}", [P, CH], F32)) for i in range(8)]
        block = local.enter_context(nc.Block())

        @block.scalar
        def _(act):
            for i in range(NT):
                act.activation(xs[:, i, :], g.x[:, i, :], ACT.Square, accum_out=ss[:, i:i + 1]).then_inc(sumsq, 1)
            act.wait_ge(meansq, 1)
            act.activation(ss[:, :], ss[:, :], ACT.Sqrt).then_inc(rms, 1)
            for c in range(NCH):
                for k in range(KD):
                    act.wait_ge(tr_done, KD * c + k + 1)
                    act.activation(xT[:, k, c * CH:(c + 1) * CH], banks[(c % 2) * KD + k][0:DP, :], ACT.Copy,
                                   scale=g.norm_w_c[:, l, k:k + 1]).then_inc(xT_ready, 1)
            for c in range(NCH):
                for m in range(MI):
                    j = c * 2 * MI + 2 * m + 1
                    act.wait_ge(proj_done, j + 1)
                    act.activation(g.sres[:, m, c * CH:(c + 1) * CH], banks[4 + j % 4][:, :],
                                   ACT.Silu).then_inc(res_ready, 1)
                for m in range(MI):
                    act.wait_ge(conv_done, MI * c + m + 1)
                    act.activation(g.u[:, m, c * CH:(c + 1) * CH], cv[:, m, :], ACT.Silu,
                                   bias=g.conv_bc[:, l, m:m + 1]).then_inc(u_ready, 1)
            for c in range(NCH):
                act.wait_ge(xp_done, c + 1)
                if c >= 2:
                    act.wait_ge(split_step, 5 * (c - 1))
                    act.wait_ge(dt_done, MI * (c - 1))
                act.activation(bcf[:, c % 2, :], banks[c % 2][0:NX, :], ACT.Copy).then_inc(bc_ready, 1)
                act.activation(dtT[:, c % 2, :], banks[c % 2][NX:NX + RK, :], ACT.Copy).then_inc(dtT_ready, 1)
                for m in range(MI):
                    j = MI * c + m
                    act.wait_ge(dt_done, j + 1)
                    if m == 0 and c >= 2:
                        act.wait_ge(delta_ready, MI * (c - 1))
                    act.activation(ax[:, c % 2, m, :], banks[2 + j % 4][:, :], ACT.Abs,
                                   bias=g.dt_bc[:, l, m:m + 1]).then_inc(abs_done, 1)
                    act.activation(g.delta[:, m, c * CH:(c + 1) * CH], banks[2 + j % 4][:, :], ACT.Relu,
                                   bias=g.dt_bc[:, l, m:m + 1]).then_inc(abs_done, 1)
                act.wait_ge(abs_done, 2 * MI * (c + 1))
                act.activation(ax[:, c % 2, :, :], ax[:, c % 2, :, :], ACT.Exp, scale=-1.0).then_inc(exp_done, 1)
                act.wait_ge(exp_done, c + 1)
                if c >= 2:
                    act.wait_ge(delta_ready, MI * (c - 1))
                act.activation(dd[:, c % 2, :, :], ax[:, c % 2, :, :], ACT.Ln, bias=1.0).then_inc(ln_done, 1)

        @block.vector
        def _(dve):
            dve.wait_ge(sumsq, NT)
            dve.tensor_scalar(ss[:, :], ss[:, :], 1.0 / D, 1e-5, ALU.mult, ALU.add).then_inc(meansq, 1)
            dve.wait_ge(rms, 1)
            dve.reciprocal(rstd[:, :], ss[:, :]).then_inc(rstd_done, 1)
            dve.wait_ge(rstd_done, 1)
            for i in range(NT):
                dve.tensor_scalar(xs[:, i, :], g.x[:, i, :], rstd[:, i:i + 1], None, ALU.mult).then_inc(xs_ready, 1)
            dve.memset(g.xr[:, :, 0:TAPS - 1], 0.0).then_inc(conv_step, 1)
            steps = 1
            for c in range(NCH):
                for m in range(MI):
                    j = c * 2 * MI + 2 * m
                    dve.wait_ge(proj_done, j + 1)
                    dve.tensor_copy(g.xr[:, m, TAPS - 1 + c * CH:TAPS - 1 + (c + 1) * CH],
                                    banks[4 + j % 4][:, :]).then_inc(xr_ready, 1)
                dve.wait_ge(xr_ready, MI * (c + 1))
                if c:
                    dve.wait_ge(u_ready, MI * c)
                for k in range(TAPS):
                    dve.wait_ge(conv_step, steps)
                    for m in range(MI):
                        src = g.xr[:, m, c * CH + k:c * CH + k + CH]
                        w = g.conv_wc[:, l, m, k:k + 1]
                        if k == 0:
                            ins = dve.tensor_scalar(cv[:, m, :], src, w, None, ALU.mult)
                        else:
                            ins = dve.scalar_tensor_tensor(out=cv[:, m, :], in0=src, scalar=w, in1=cv[:, m, :],
                                                           op0=ALU.mult, op1=ALU.add)
                        if k < TAPS - 1:
                            ins.then_inc(conv_step, 1)
                            steps += 1
                        else:
                            ins.then_inc(conv_done, 1)
            n = 0
            for c in range(NCH):
                cc = slice(c * CH, (c + 1) * CH)
                dve.wait_ge(bc_ready, c + 1)
                b = bcf[:, c % 2, :]
                for out, i0, i1 in ((g.bcp[0:NX, cc], b, None), (b, b, g.bcp[0:NX, cc]),
                                    (mid[:, c % 2, :], b, None), (g.bcp[NX:2 * NX, cc], mid[:, c % 2, :], None),
                                    (g.bcp[2 * NX:3 * NX, cc], b, mid[:, c % 2, :])):
                    if i1 is None:
                        ins = dve.tensor_copy(out, i0)
                    else:
                        ins = dve.tensor_tensor(out, i0, i1, ALU.subtract)
                    ins.then_inc(split_step, 1)
                    n += 1
                    dve.wait_ge(split_step, n)
                dve.wait_ge(ln_done, c + 1)
                e, ln = ax[:, c % 2, :, :], dd[:, c % 2, :, :]
                r = cv
                k0 = 6 * c
                dve.tensor_scalar(r[:, :, :], e, 1.0, -1.0, ALU.add, ALU.add).then_inc(sp_step, 1)
                dve.wait_ge(sp_step, k0 + 1)
                dve.tensor_tensor(r[:, :, :], e, r[:, :, :], ALU.subtract).then_inc(sp_step, 1)
                dve.wait_ge(sp_step, k0 + 2)
                dve.tensor_tensor(r[:, :, :], r[:, :, :], ln, ALU.add).then_inc(sp_step, 1)
                dve.wait_ge(sp_step, k0 + 3)
                dve.scalar_tensor_tensor(out=r[:, :, :], in0=e, scalar=LN2, in1=r[:, :, :], op0=ALU.mult,
                                         op1=ALU.max).then_inc(sp_step, 1)
                dve.wait_ge(sp_step, k0 + 4)
                dve.tensor_tensor(g.delta[:, :, cc], g.delta[:, :, cc], r[:, :, :], ALU.add).then_inc(sp_step, 1)
                dve.wait_ge(sp_step, k0 + 5)
                dve.tensor_tensor(g.du[:, :, cc], g.delta[:, :, cc], g.u[:, :, cc],
                                  ALU.mult).then_inc(sp_step, 1)
                dve.wait_ge(sp_step, k0 + 6)
                dve.sem_inc(delta_ready, MI)

        @block.tensor
        def _(pe):
            for c in range(NCH):
                pe.wait_ge(xs_ready, TPC * (c + 1))
                for k in range(KD):
                    if c >= 2:
                        pe.wait_ge(xT_ready, KD * (c - 2) + k + 1)
                    for i in range(TPC):
                        ins = pe.transpose(banks[(c % 2) * KD + k][0:DP, i * P:(i + 1) * P],
                                           xs[:, c * TPC + i, k * DP:(k + 1) * DP], g.ident[:, :])
                    ins.then_inc(tr_done, 1)
            for c in range(NCH):
                pe.wait_ge(xT_ready, KD * (c + 1))
                for j6 in range(2 * MI):
                    j = c * 2 * MI + j6
                    m = j6 // 2 + MI * (j6 % 2)
                    if j >= 4:
                        pe.wait_ge(res_ready if j % 2 else xr_ready, (j - 4) // 2 + 1)
                    for k in range(KD):
                        ins = pe.matmul(banks[4 + j % 4][:, :], g.w_in[:, l, k, m * P:(m + 1) * P],
                                        xT[:, k, c * CH:(c + 1) * CH], start=(k == 0), stop=(k == KD - 1))
                    ins.then_inc(proj_done, 1)
            pe.wait_ge(xr_ready, MI * NCH)
            pe.wait_ge(res_ready, MI * NCH)
            for c in range(NCH):
                pe.wait_ge(u_ready, MI * (c + 1))
                if c >= 2:
                    pe.wait_ge(dtT_ready, c - 1)
                for m in range(MI):
                    ins = pe.matmul(banks[c % 2][0:NX + RK, :], g.w_x[:, l, m, :], g.u[:, m, c * CH:(c + 1) * CH],
                                    start=(m == 0), stop=(m == MI - 1))
                ins.then_inc(xp_done, 1)
                pe.wait_ge(dtT_ready, c + 1)
                for m in range(MI):
                    j = MI * c + m
                    if j >= 4:
                        pe.wait_ge(abs_done, 2 * (j - 3))
                    pe.matmul(banks[2 + j % 4][:, :], g.w_dt[:, l, m * P:(m + 1) * P], dtT[:, c % 2, :],
                              start=True, stop=True).then_inc(dt_done, 1)


def mamba_scan(nc, g, l):
    JP = 2 * MI
    NP2 = NS // 2
    (b_rep, c_rep, b_copied, decay_ready, decay_free, in_ready, in_free, scanned, carried, weighted, hc_free,
     y_done, gated, diag_made, out_done, added, pool_turns) = sems(nc, g, " ".join(f"{n}{l}" for n in (
        "b_replicated c_replicated b_copied decay_ready decay_free input_ready input_free scanned carried "
        "weighted hc_free y_done gated diag_made out_projected x_added pool_turns").split()))
    with ExitStack() as local:
        def sb(name, shape, dt=F32):
            return local.enter_context(nc.sbuf_tensor(f"{name}{l}", shape, dt))
        brep = sb("brep", [P, 2, CH])
        inp = sb("inp", [P, MI, CH])
        hst = sb("hst", [P, JP, CH])
        hc = sb("hc", [P, MI, CH])
        carry = sb("carry", [P, NS * MI])
        diag = sb("diag", [P, MI, P])
        psy = [local.enter_context(nc.psum_tensor(f"psy{l}_{m}", [P, CH], F32)) for m in range(MI)]
        psa = [local.enter_context(nc.psum_tensor(f"psa{l}_{m}", [P, CH], F32)) for m in range(2)]
        psc = [local.enter_context(nc.psum_tensor(f"psc{l}_{m}", [P, CH], F32)) for m in range(2)]
        psb = local.enter_context(nc.psum_tensor(f"psb{l}", [P, CH], F32))
        y = g.xr
        block = local.enter_context(nc.Block())

        @block.tensor
        def _(pe):
            def replicate(c, n, e, seen):
                if seen is not None:
                    pe.wait_ge(b_copied, seen)
                pe.matmul(psb[:, :], g.sel[:, n, :], g.bcp[:, bass.ds(c * CH, CH)], start=True,
                          stop=True).then_inc(b_rep, 1)
                pe.matmul(psc[e][:, :], g.sel[:, n + NS, :], g.bcp[:, bass.ds(c * CH, CH)], start=True,
                          stop=True).then_inc(c_rep, 1)

            def accumulate(seen, stop):
                for m in range(MI):
                    pe.wait_ge(weighted, seen + m + 1)
                    pe.matmul(psy[m][:, :], g.ident[:, :], hc[:, m, :], start=False, stop=stop,
                              skip_group_check=True).then_inc(hc_free, 1)

            pe.wait_ge(diag_made, MI)
            with pe.Fori(0, NCH) as c:
                pe.wait_ge(gated, MI * c + MI)
                pe.wait_ge(weighted, c * NS * MI + 1)
                for m in range(MI):
                    pe.matmul(psy[m][:, :], diag[:, m, :], g.u[:, m, bass.ds(c * CH, CH)], start=True, stop=False,
                              skip_group_check=True)
                for e in range(2):
                    replicate(c, e, e, c * NS + e + 1)
                with pe.Fori(0, NP2 - 1) as p:
                    for e in range(2):
                        accumulate(c * (NS * MI) + p * JP + MI * e + 1, False)
                        replicate(c, p * 2 + (e + 2), e, c * NS + p * 2 + e + 3)
                for e in range(2):
                    accumulate(c * (NS * MI) + (NP2 - 1) * JP + MI * e + 1, e == 1)
                pe.matmul(psb[0:1, 0:2], g.ident[:, 0:1], g.ident[:, 0:2], start=True,
                          stop=True).then_inc(y_done, 1)
            for i in range(NT):
                pe.wait_ge(gated, MI * (2 + i // TPC))
                if i >= 2:
                    pe.wait_ge(added, i - 1)
                for m in range(MI):
                    ins = pe.matmul(psa[i % 2][:, 0:D], y[:, m, i * P:(i + 1) * P], g.w_out[:, l, m, :],
                                    start=(m == 0), stop=(m == MI - 1))
                ins.then_inc(out_done, 1)

        @block.scalar
        def _(act):
            with act.Fori(0, NCH) as c:
                with act.Fori(0, NP2) as p:
                    for e in range(2):
                        act.wait_ge(b_rep, c * NS + p * 2 + e + 1)
                        act.wait_ge(in_free, (c * NS + p * 2 + e) * MI + 1)
                        act.activation(brep[:, e, :], psb[:, :], ACT.Copy).then_inc(b_copied, 1)
                        for m in range(MI):
                            j = MI * e + m
                            act.wait_ge(decay_free, (c * NP2 + p) * JP + j + 1)
                            act.activation(psa[j % 2][:, :], g.delta[:, m, bass.ds(c * CH, CH)], ACT.Exp,
                                           scale=g.a_neg[:, l, m, bass.ds(p * 2 + e, 1)]).then_inc(decay_ready, 1)

        @block.gpsimd
        def _(pool):
            with pool.Fori(0, NCH) as c:
                with pool.Fori(0, NP2) as p:
                    for e in range(2):
                        pool.wait_ge(b_copied, c * NS + p * 2 + e + 2)
                        for m in range(MI):
                            j = MI * e + m
                            pool.wait_ge(in_free, (c * NP2 + p) * JP + j + 1)
                            pool.sem_inc(pool_turns, 1)
                            pool.tensor_tensor(inp[:, m, :], g.du[:, m, bass.ds(c * CH, CH)], brep[:, e, :],
                                               ALU.mult).then_inc(in_ready, 1)

        @block.vector
        def _(dve):
            dve.sem_inc(gated, MI)
            dve.sem_inc(weighted, 1)
            dve.sem_inc(b_copied, 1)
            dve.sem_inc(decay_free, 2)
            dve.sem_inc(in_free, MI)
            dve.sem_inc(hc_free, MI)
            dve.memset(carry[:, :], 0.0).then_inc(carried, 1)
            for m in range(MI):
                dve.tensor_scalar(diag[:, m, :], g.ident[:, :], g.d_c[:, l, m:m + 1], None,
                                  ALU.mult).then_inc(diag_made, 1)

            with dve.Fori(0, NCH) as c:
                with dve.Fori(0, NP2) as p:
                    base = (c * NP2 + p) * JP

                    def scan(j):
                        m, e = j % MI, j // MI
                        dve.wait_ge(decay_ready, base + j + 1)
                        dve.wait_ge(in_ready, base + j + 1)
                        if j == 0:
                            dve.wait_ge(carried, (c * NP2 + p) * 2 + 1)
                        dve.tensor_tensor_scan(hst[:, j, :], psa[j % 2][:, :], inp[:, m, :],
                                               carry[:, bass.ds(p * JP + j, 1)], ALU.mult,
                                               ALU.add).then_inc(scanned, 1)

                    def weight(j):
                        m, e = j % MI, j // MI
                        dve.wait_ge(scanned, base + j + 1)
                        dve.sem_inc(decay_free, 1)
                        dve.sem_inc(in_free, 1)
                        if m == 0:
                            dve.wait_ge(c_rep, c * NS + p * 2 + e + 1)
                        dve.wait_ge(hc_free, base + j + 1)
                        dve.tensor_tensor(hc[:, m, :], hst[:, j, :], psc[e][:, :], ALU.mult).then_inc(weighted, 1)

                    scan(0)
                    for j in range(1, JP):
                        scan(j)
                        weight(j - 1)
                        if j % MI == 0:
                            e = j // MI - 1
                            dve.tensor_copy(carry[:, bass.ds(p * JP + MI * e, MI)],
                                            hst[:, MI * e:MI * e + MI, CH - 1]).then_inc(carried, 1)
                    weight(JP - 1)
                    dve.tensor_copy(carry[:, bass.ds(p * JP + MI, MI)],
                                    hst[:, MI:JP, CH - 1]).then_inc(carried, 1)
                dve.wait_ge(y_done, c + 1)
                for m in range(MI):
                    dve.tensor_tensor(y[:, m, bass.ds(c * CH, CH)], g.sres[:, m, bass.ds(c * CH, CH)],
                                      psy[m][:, :], ALU.mult).then_inc(gated, 1)
            for i in range(NT):
                dve.wait_ge(out_done, i + 1)
                dve.tensor_tensor(g.x[:, i, :], g.x[:, i, :], psa[i % 2][:, 0:D], ALU.add).then_inc(added, 1)
            dve.wait_ge(added, NT)


def normalize_rows(nc, g, name, src, dst, eps, then=None):
    stats, mean_var, root, recip, rows = sems(nc, g, " ".join(
        f"{name}_{n}" for n in "stats mean_var root reciprocal rows".split()))
    n = src.shape[1]
    with ExitStack() as local:
        st = local.enter_context(nc.sbuf_tensor(f"{name}_st", [P, n, 6], F32))
        mv = local.enter_context(nc.sbuf_tensor(f"{name}_mv", [P, n, 2], F32))
        rs = local.enter_context(nc.sbuf_tensor(f"{name}_rs", [P, n], F32))
        block = local.enter_context(nc.Block())

        @block.vector
        def _(dve):
            for i in range(n):
                dve.bn_stats(st[:, i, :], src[:, i, 0:D]).then_inc(stats, 1)
            for i in range(n):
                dve.wait_ge(stats, i + 1)
                dve.bn_aggr(mv[:, i, :], st[:, i, :]).then_inc(mean_var, 1)
            dve.wait_ge(mean_var, n)
            dve.tensor_scalar(rs[:, :], mv[:, :, 1], eps, None, ALU.add).then_inc(mean_var, 1)
            dve.wait_ge(root, 1)
            dve.reciprocal(rs[:, :], rs[:, :]).then_inc(recip, 1)
            dve.wait_ge(recip, 1)
            for i in range(n):
                dve.tensor_scalar(dst[:, i, 0:D], src[:, i, 0:D], mv[:, i, 0:1], rs[:, i:i + 1],
                                  ALU.subtract, ALU.mult).then_inc(rows, 1)
            dve.wait_ge(rows, n)

        @block.scalar
        def _(act):
            act.wait_ge(mean_var, n + 1)
            act.activation(rs[:, :], rs[:, :], ACT.Sqrt).then_inc(root, 1)


def transpose_rows(pe, g, banks, src, c, k, done, ready=None, seen=0):
    for i in range(TPC):
        ins = pe.transpose(banks[(c % 2) * KD + k][0:DP, i * P:(i + 1) * P],
                           src[:, c * TPC + i, k * DP:(k + 1) * DP], g.ident[:, :])
    ins.then_inc(done, 1)


def attn_project(nc, g, a):
    w_in, tr_done, hT_ready, qk_done, qk_ready, v_done, v_ready, halved, ones_set, bias_in = sems(
        nc, g, "attn_w_in attn_transposed attn_hT_ready qk_projected qk_ready v_projected v_ready "
        "biases_scaled v_ones_set xa_biased")
    with ExitStack() as local, nc.allow_non_contiguous_dma(reason="small weights"):
        def sb(name, shape, dt=F32):
            return local.enter_context(nc.sbuf_tensor(name, shape, dt))
        hT = sb("hT", [DP, KD, L])
        w = sb("w_qkv", [DP, 3, KD, D])
        gb = sb("ln1_gb", [DP, 2, KD])
        qkb = sb("qk_bias", [DP, 2, KD])
        bv = sb("bv_rows", [P, D])
        bo = sb("bo_rows", [P, D])
        banks = [local.enter_context(nc.psum_tensor(f"pb{i}", [P, CH], F32)) for i in range(8)]
        block = local.enter_context(nc.Block())
        I = g.attn

        @block.sync
        def _(sp):
            for dst, src in ((w[:, 0], ks(I["Wq"])), (w[:, 1], ks(I["Wk"])), (w[:, 2], ks(I["Wv"])),
                             (gb[:, 0, :], col(I["ln1_g"], DP)), (gb[:, 1, :], col(I["ln1_b"], DP)),
                             (qkb[:, 0, :], col(I["bq"], DP)), (qkb[:, 1, :], col(I["bk"], DP)),
                             (bv[:, :], I["bv"].partition_broadcast(P)), (bo[:, :], I["bo"].partition_broadcast(P)),
                             (a.w_o[:, :, :], ks(I["Wo"]))):
                sp.dma_start(dst, src).then_inc(w_in, 16)
            for j in range(HK):
                sp.dma_start(a.proj_blocks[DH * j:DH * (j + 1), j, :],
                             I["proj"].rearrange("m d -> d m")).then_inc(w_in, 16)
            sp.wait_ge(w_in, 16 * (10 + HK))

        @block.gpsimd
        def _(pool):
            pool.memset(a.v1[:, :, :, DH:DH + 1], 1.0).then_inc(ones_set, 1)
            pool.wait_ge(w_in, 16 * (10 + HK))
            for i in range(NT):
                pool.tensor_tensor(a.xa[:, i, :], a.xa[:, i, :], bo[:, :], ALU.add).then_inc(bias_in, 1)
            pool.wait_ge(bias_in, NT)

        @block.tensor
        def _(pe):
            for c in range(NCH):
                for k in range(KD):
                    if c >= 2:
                        pe.wait_ge(hT_ready, KD * (c - 2) + k + 1)
                    transpose_rows(pe, g, banks, a.xs, c, k, tr_done)
            pe.wait_ge(w_in, 16 * (10 + HK))
            for c in range(NCH):
                pe.wait_ge(hT_ready, KD * (c + 1))
                for qk in range(2):
                    for m in range(KD):
                        j = (c * 2 + qk) * KD + m
                        if j >= 2:
                            pe.wait_ge(qk_ready, 2 * (j - 1))
                        for k in range(KD):
                            ins = pe.matmul(banks[4 + j % 2][0:DP, :], w[:, qk, k, m * DP:(m + 1) * DP],
                                            hT[:, k, c * CH:(c + 1) * CH], start=(k == 0), stop=(k == KD - 1))
                        ins.then_inc(qk_done, 1)
                for i in range(c * TPC, (c + 1) * TPC):
                    if i >= 2:
                        pe.wait_ge(v_ready, i - 1)
                    for k in range(KD):
                        ins = pe.matmul(banks[6 + i % 2][:, 0:D], hT[:, k, i * P:(i + 1) * P], w[:, 2, k, :],
                                        start=(k == 0), stop=(k == KD - 1))
                    ins.then_inc(v_done, 1)

        @block.scalar
        def _(act):
            act.wait_ge(w_in, 16 * (10 + HK))
            for c in range(NCH):
                for k in range(KD):
                    act.wait_ge(tr_done, KD * c + k + 1)
                    act.activation(hT[:, k, c * CH:(c + 1) * CH], banks[(c % 2) * KD + k][0:DP, :], ACT.Identity,
                                   scale=gb[:, 0, k:k + 1], bias=gb[:, 1, k:k + 1]).then_inc(hT_ready, 1)
            act.wait_ge(halved, 1)
            for c in range(NCH):
                for qk in range(2):
                    for m in range(KD):
                        j = (c * 2 + qk) * KD + m
                        act.wait_ge(qk_done, j + 1)
                        for out, f in ((a.qk[:, qk, m, c * CH:(c + 1) * CH], ACT.Identity),
                                       (a.qk2[:, qk, m, c * CH:(c + 1) * CH], ACT.Square)):
                            act.activation(out, banks[4 + j % 2][0:DP, :], f, scale=DH ** -0.25,
                                           bias=qkb[:, qk, m:m + 1]).then_inc(qk_ready, 1)

        @block.vector
        def _(dve):
            dve.wait_ge(w_in, 16 * (10 + HK))
            dve.tensor_scalar(qkb[:, :, :], qkb[:, :, :], DH ** -0.25, None, ALU.mult).then_inc(halved, 1)
            for i in range(NT):
                dve.wait_ge(v_done, i + 1)
                dve.tensor_tensor(a.v1[:, i, :, 0:DH], banks[6 + i % 2][:, 0:D].rearrange("p (h e) -> p h e", e=DH),
                                  bv[:, :].rearrange("p (h e) -> p h e", e=DH), ALU.add).then_inc(v_ready, 1)


def attn_key_logits(nc, g, a):
    dd_done, diag_copied, kdd_ready, kmax_ready, gmax = sems(
        nc, g, "k_dd_done k_diag_copied k_dd_ready k_max_ready k_global_max")
    with ExitStack() as local:
        def sb(name, shape, dt=F32):
            return local.enter_context(nc.sbuf_tensor(name, shape, dt))
        kd = sb("k_diag", [P, NT, KD, HK])
        km = sb("k_max", [P, NT, KD])
        km1 = sb("k_max1", [P, 1])
        row = sb("k_max_row", [1, 2])
        banks = [local.enter_context(nc.psum_tensor(f"kb{i}", [P, CH], F32)) for i in range(8)]
        block = local.enter_context(nc.Block())
        W = HK * M

        @block.tensor
        def _(pe):
            for i in range(NT):
                if i >= 4:
                    pe.wait_ge(kdd_ready, KD * (i - 3))
                    pe.wait_ge(kmax_ready, KD * (i - 3))
                for k in range(KD):
                    b = banks[(i % 4) * KD + k]
                    t = slice(i * P, (i + 1) * P)
                    pe.matmul(b[:, 0:W], a.qk[:, 1, k, t], a.proj_blocks[:, :, :], start=True, stop=True)
                    pe.matmul(b[:, W:W + HK], a.qk2[:, 1, k, t], g.head_of[:, :], start=True,
                              stop=True).then_inc(dd_done, 1)
            pe.wait_ge(gmax, 1)
            pe.transpose(banks[0][0:1, 0:P], km1[:, :], g.ident[:, :]).then_inc(gmax, 1)
            pe.wait_ge(gmax, 3)
            pe.matmul(banks[1][:, 0:1], g.ones[0:1, :], row[:, 0:1], start=True, stop=True).then_inc(gmax, 1)

        @block.scalar
        def _(act):
            for i in range(NT):
                for k in range(KD):
                    act.wait_ge(dd_done, KD * i + k + 1)
                    act.activation(kd[:, i, k, :], banks[(i % 4) * KD + k][:, W:W + HK],
                                   ACT.Copy).then_inc(diag_copied, 1)

        @block.vector
        def _(dve):
            for i in range(NT):
                for k in range(KD):
                    dd = banks[(i % 4) * KD + k][:, 0:W]
                    dve.wait_ge(diag_copied, KD * i + k + 1)
                    dve.tensor_reduce(km[:, i, k:k + 1], dd, AX.X, ALU.max).then_inc(kmax_ready, 1)
                    dve.tensor_tensor(a.kdd[:, i, k, :, :], dd.rearrange("p (h m) -> p h m", m=M),
                                      kd[:, i, k, :].unsqueeze(2).broadcast_to([P, HK, M]),
                                      ALU.subtract).then_inc(kdd_ready, 1)
            dve.wait_ge(kmax_ready, KD * NT)
            dve.tensor_reduce(km1[:, :], km[:, :, :], AX.XY, ALU.max).then_inc(gmax, 1)
            dve.wait_ge(gmax, 2)
            dve.tensor_reduce(row[:, 0:1], banks[0][0:1, 0:P], AX.X, ALU.max).then_inc(gmax, 1)
            dve.wait_ge(gmax, 4)
            dve.tensor_scalar(a.neg_kmax[:, :], banks[1][:, 0:1], -1.0, None, ALU.mult).then_inc(gmax, 1)


def attention(nc, g, a):
    (qdd_done, qdiag_ready, qmax_ready, qbias_ready, qarg_ready, qexp_ready, qp_ready, kexp_ready, kp_ready,
     turned, turned_copied, at_done, masked, out_done, state_done, state_ready, recip, o_ready, oT_done, oT_ready,
     wo_done, xa_ready, padded) = sems(nc, g, " ".join("at_" + n for n in (
        "qdd_done qdiag_ready qmax_ready qbias_ready qarg_ready qexp_ready qp_ready kexp_ready kp_ready "
        "turned turned_copied products_done masked out_done state_done state_ready recip o_ready oT_done "
        "oT_ready wo_done xa_ready padded").split()))
    with ExitStack() as local:
        def sb(name, shape, dt=F32):
            return local.enter_context(nc.sbuf_tensor(name, shape, dt))
        qd = sb("q_diag", [P, 2, H])
        qm = sb("q_max", [P, 2, H])
        qarg = sb("q_arg", [P, 2, H, M])
        kexp = sb("k_exp", [P, 2, H, M])
        qp = sb("q_feat", [P, 2, H, MP])
        kp = sb("k_feat", [P, 2, H, MP])
        qkT = sb("qk_feat_T", [P, 2, 2 * HP, P])
        am = sb("masked_products", [P, H, P])
        st = sb("state", [P, HP, 2 * (DH + 1)])
        rc = sb("recip_den", [P, 2, H])
        o = sb("o_rows", [P, 2, D])
        oT = sb("o_T", [DP, KD, P])
        banks = [local.enter_context(nc.psum_tensor(f"ab{i}", [P, CH], F32)) for i in range(8)]
        block = local.enter_context(nc.Block())
        W = HK * M
        E1 = DH + 1
        SC = HP * 2 * E1
        ratio = M ** -0.5

        @block.gpsimd
        def _(pool):
            pool.memset(qp[:, :, :, M:MP], 0.0).then_inc(padded, 1)
            pool.memset(kp[:, :, :, M:MP], 0.0).then_inc(padded, 1)
            pool.memset(st[:, :, :], 0.0).then_inc(padded, 1)
            pool.wait_ge(padded, 3)
            pool.memset(st[0:MP, :, DH:E1], 1e-6).then_inc(padded, 1)
            pool.memset(st[MP:P, :, E1 + DH:2 * E1], 1e-6).then_inc(padded, 1)
            for i in range(NT):
                if i >= 2:
                    pool.wait_ge(turned, 3 * (i - 1))
                    pool.wait_ge(state_done, i - 1)
                pool.wait_ge(qexp_ready, i + 1)
                pool.tensor_scalar(qp[:, i % 2, :, 0:M], qarg[:, i % 2, :, :], 1e-4, ratio, ALU.add,
                                   ALU.mult).then_inc(qp_ready, 1)
                pool.wait_ge(kexp_ready, i + 1)
                pool.tensor_scalar(kp[:, i % 2, :, 0:M], kexp[:, i % 2, :, :], 1e-4, ratio, ALU.add,
                                   ALU.mult).then_inc(kp_ready, 1)

        @block.scalar
        def _(act):
            def features(i):
                for k in range(KD):
                    act.wait_ge(qdd_done, KD * i + k + 1)
                    if i >= 2 and k == 0:
                        act.wait_ge(qbias_ready, i - 1)
                    act.activation(qd[:, i % 2, k * HK:(k + 1) * HK], banks[k][:, W:W + HK],
                                   ACT.Copy).then_inc(qdiag_ready, 1)
                if i >= 2:
                    act.wait_ge(kp_ready, i - 1)
                act.activation(kexp[:, i % 2, :, :], a.kdd[:, i, :, :, :].rearrange("p k h m -> p (k h) m"), ACT.Exp,
                               bias=a.neg_kmax[:, :]).then_inc(kexp_ready, 1)
                act.wait_ge(qarg_ready, KD * (i + 1))
                act.activation(qarg[:, i % 2, :, :], qarg[:, i % 2, :, :], ACT.Exp).then_inc(qexp_ready, 1)

            features(0)
            for i in range(NT):
                for b in range(3):
                    act.wait_ge(turned, 3 * i + b + 1)
                    if i >= 2 and b == 0:
                        act.wait_ge(out_done, i - 1)
                    act.activation(qkT[:, i % 2, 4 * b:4 * b + 4, :],
                                   banks[2 + b][:, :].rearrange("p (s t) -> p s t", t=P),
                                   ACT.Copy).then_inc(turned_copied, 1)
                if i + 1 < NT:
                    features(i + 1)
                act.wait_ge(oT_done, i + 1)
                if i >= 1:
                    act.wait_ge(wo_done, i)
                act.activation(oT[:, :, :], banks[5][0:DP, 0:KD * P].rearrange("p (k t) -> p k t", t=P),
                               ACT.Copy).then_inc(oT_ready, 1)

        @block.vector
        def _(dve):
            def features(i):
                for k in range(KD):
                    dve.wait_ge(qdiag_ready, KD * i + k + 1)
                    dve.tensor_reduce(qm[:, i % 2, k * HK:(k + 1) * HK],
                                      banks[k][:, 0:W].rearrange("p (h m) -> p h m", m=M), AX.X,
                                      ALU.max).then_inc(qmax_ready, 1)
                dve.wait_ge(qmax_ready, KD * (i + 1))
                dve.tensor_tensor(qm[:, i % 2, :], qm[:, i % 2, :], qd[:, i % 2, :], ALU.add).then_inc(qbias_ready, 1)
                dve.wait_ge(qbias_ready, i + 1)
                if i >= 2:
                    dve.wait_ge(qp_ready, i - 1)
                for k in range(KD):
                    dve.tensor_tensor(qarg[:, i % 2, k * HK:(k + 1) * HK, :],
                                      banks[k][:, 0:W].rearrange("p (h m) -> p h m", m=M),
                                      qm[:, i % 2, k * HK:(k + 1) * HK].unsqueeze(2).broadcast_to([P, HK, M]),
                                      ALU.subtract).then_inc(qarg_ready, 1)

            features(0)
            for i in range(NT):
                if i + 1 < NT:
                    features(i + 1)
                for r in range(2):
                    for s in range(2):
                        dve.wait_ge(at_done, 4 * i + 2 * r + s + 1)
                        if i and r == 0 and s == 0:
                            dve.wait_ge(out_done, i)
                        h = 2 * 3 * r + s
                        dve.tensor_tensor(am[:, h:h + 5:2, :],
                                          banks[5 + s][:, 0:3 * P].rearrange("p (j t) -> p j t", t=P),
                                          g.causal[:, :].unsqueeze(1).broadcast_to([P, 3, P]),
                                          ALU.mult).then_inc(masked, 1)
                dve.wait_ge(state_done, i + 1)
                ob = banks[7][:, 0:SC].rearrange("p (h e) -> p h e", e=E1)
                dve.reciprocal(rc[:, i % 2, :], ob[:, :, DH]).then_inc(recip, 1)
                dve.wait_ge(state_done, i + 1)
                sp = banks[7][:, SC:2 * SC].rearrange("p (j e) -> p j e", e=2 * E1)
                if i == 0:
                    dve.wait_ge(padded, 5)
                else:
                    dve.wait_ge(state_ready, 2 * i)
                for s in range(2):
                    q, e = slice(MP * s, MP * (s + 1)), slice(E1 * s, E1 * (s + 1))
                    dve.tensor_tensor(st[q, :, e], st[q, :, e], sp[q, :, e], ALU.add).then_inc(state_ready, 1)
                dve.wait_ge(recip, i + 1)
                if i >= 2:
                    dve.wait_ge(oT_done, i - 1)
                dve.tensor_tensor(o[:, i % 2, :].rearrange("p (h e) -> p h e", e=DH), ob[:, :, 0:DH],
                                  rc[:, i % 2, :].unsqueeze(2).broadcast_to([P, H, DH]),
                                  ALU.mult).then_inc(o_ready, 1)
                dve.wait_ge(wo_done, i + 1)
                dve.tensor_tensor(a.xa[:, i, :], a.xa[:, i, :], banks[6][:, 0:D], ALU.add).then_inc(xa_ready, 1)
            dve.wait_ge(xa_ready, NT)

        @block.tensor
        def _(pe):
            def logits(i):
                if i:
                    pe.wait_ge(qarg_ready, KD * i)
                    pe.wait_ge(qdiag_ready, KD * i)
                for k in range(KD):
                    t = slice(i * P, (i + 1) * P)
                    pe.matmul(banks[k][:, 0:W], a.qk[:, 0, k, t], a.proj_blocks[:, :, :], start=True, stop=True)
                    pe.matmul(banks[k][:, W:W + HK], a.qk2[:, 0, k, t], g.head_of[:, :], start=True,
                              stop=True).then_inc(qdd_done, 1)

            pe.wait_ge(padded, 5)
            logits(0)
            for i in range(NT):
                for s in range(2 * HP):
                    f, j = (qp, s) if s < HP else (kp, s - HP)
                    if s == 0:
                        pe.wait_ge(qp_ready, i + 1)
                        if i:
                            pe.wait_ge(turned_copied, 3 * i)
                    if s == HP:
                        pe.wait_ge(kp_ready, i + 1)
                    ins = pe.transpose(banks[2 + s // 4][:, (s % 4) * P:(s % 4 + 1) * P],
                                       f[:, i % 2, 2 * j:2 * j + 2, :].rearrange("p h m -> p (h m)"), g.ident[:, :])
                    if s % 4 == 3:
                        ins.then_inc(turned, 1)
                if i + 1 < NT:
                    logits(i + 1)
                pe.wait_ge(turned_copied, 3 * (i + 1))
                for r in range(2):
                    if r:
                        pe.wait_ge(masked, 4 * i + 2)
                    elif i:
                        pe.wait_ge(xa_ready, i)
                        pe.wait_ge(oT_ready, i)
                    for s in range(2):
                        q = slice(MP * s, MP * s + M)
                        for jj in range(3):
                            j = 3 * r + jj
                            ins = pe.matmul(banks[5 + s][:, jj * P:(jj + 1) * P], qkT[q, i % 2, HP + j, :],
                                            qkT[q, i % 2, j, :], start=True, stop=True)
                        ins.then_inc(at_done, 1)
                if i:
                    pe.wait_ge(state_ready, 2 * i)
                    pe.wait_ge(o_ready, i)
                for j in range(HP):
                    pe.wait_ge(masked, 4 * i + 2 * (j // 3) + 2)
                    pe.matmul(banks[7][:, 2 * E1 * j:2 * E1 * (j + 1)], qkT[:, i % 2, j, :], st[:, j, :], start=True,
                              stop=False, skip_group_check=True)
                    for s in range(2):
                        h = 2 * j + s
                        ins = pe.matmul(banks[7][:, E1 * h:E1 * (h + 1)], am[:, h, :], a.v1[:, i, h, :], start=False,
                                        stop=True, skip_group_check=True)
                for j in range(HP):
                    st_ins = pe.matmul(banks[7][:, SC + 2 * E1 * j:SC + 2 * E1 * (j + 1)],
                                       kp[:, i % 2, 2 * j:2 * j + 2, :].rearrange("p h m -> p (h m)"),
                                       a.v1[:, i, 2 * j:2 * j + 2, :].rearrange("p h e -> p (h e)"), start=True, stop=True)
                ins.then_inc(out_done, 1)
                st_ins.then_inc(state_done, 1)
                pe.wait_ge(o_ready, i + 1)
                for k in range(KD):
                    ins = pe.transpose(banks[5][0:DP, k * P:(k + 1) * P], o[:, i % 2, k * DP:(k + 1) * DP], g.ident[:, :])
                ins.then_inc(oT_done, 1)
                pe.wait_ge(oT_ready, i + 1)
                for k in range(KD):
                    ins = pe.matmul(banks[6][:, 0:D], oT[:, k, :], a.w_o[:, k, :], start=(k == 0), stop=(k == KD - 1))
                ins.then_inc(wo_done, 1)


def attn_mlp(nc, g, a):
    w_in, tr_done, hT_ready, up_done, gelu_ready, down_done, biased, added = sems(
        nc, g, "mlp_w_in mlp_transposed mlp_hT_ready mlp_up_done gelu_ready mlp_down_done mlp_biased mlp_added")
    with ExitStack() as local, nc.allow_non_contiguous_dma(reason="small weights"):
        def sb(name, shape, dt=F32):
            return local.enter_context(nc.sbuf_tensor(name, shape, dt))
        hT = sb("mlp_hT", [DP, KD, L])
        gT = sb("gelu_T", [P, MF, L])
        w1 = sb("mlp_w1", [DP, KD, FF])
        w2 = sb("mlp_w2", [P, MF, D])
        gb = sb("ln2_gb", [DP, 2, KD])
        b1 = sb("mlp_b1", [P, MF])
        b2 = sb("mlp_b2_rows", [P, D])
        banks = [local.enter_context(nc.psum_tensor(f"mb{i}", [P, CH], F32)) for i in range(8)]
        block = local.enter_context(nc.Block())
        I = g.attn
        NW = 16 * 6

        @block.sync
        def _(sp):
            for dst, src in ((w1[:, :, :], ks(I["W1"])), (w2[:, :, :], I["W2"].rearrange("(m p) n -> p m n", p=P)),
                             (gb[:, 0, :], col(I["ln2_g"], DP)), (gb[:, 1, :], col(I["ln2_b"], DP)),
                             (b1[:, :], col(I["b1"], P)), (b2[:, :], I["b2"].partition_broadcast(P))):
                sp.dma_start(dst, src).then_inc(w_in, 16)

        @block.gpsimd
        def _(pool):
            pool.wait_ge(w_in, NW)
            for i in range(NT):
                pool.tensor_tensor(a.xa[:, i, :], a.xa[:, i, :], b2[:, :], ALU.add).then_inc(biased, 1)
                pool.wait_ge(biased, 2 * i + 1)
                pool.tensor_tensor(g.x[:, i, :], g.x[:, i, :], a.xa[:, i, :], ALU.add).then_inc(biased, 1)

        @block.tensor
        def _(pe):
            for c in range(NCH):
                for k in range(KD):
                    if c >= 2:
                        pe.wait_ge(hT_ready, KD * (c - 2) + k + 1)
                    transpose_rows(pe, g, banks, a.xs, c, k, tr_done)
            pe.wait_ge(w_in, NW)
            for c in range(NCH):
                pe.wait_ge(hT_ready, KD * (c + 1))
                for m in range(MF):
                    j = c * MF + m
                    if j >= 2:
                        pe.wait_ge(gelu_ready, j - 1)
                    for k in range(KD):
                        ins = pe.matmul(banks[4 + j % 2][:, :], w1[:, k, m * P:(m + 1) * P],
                                        hT[:, k, c * CH:(c + 1) * CH], start=(k == 0), stop=(k == KD - 1))
                    ins.then_inc(up_done, 1)
                pe.wait_ge(gelu_ready, MF * (c + 1))
                for i in range(c * TPC, (c + 1) * TPC):
                    if i >= 2:
                        pe.wait_ge(added, i - 1)
                    for m in range(MF):
                        ins = pe.matmul(banks[6 + i % 2][:, 0:D], gT[:, m, i * P:(i + 1) * P], w2[:, m, :],
                                        start=(m == 0), stop=(m == MF - 1))
                    ins.then_inc(down_done, 1)

        @block.scalar
        def _(act):
            act.wait_ge(w_in, NW)
            for c in range(NCH):
                for k in range(KD):
                    act.wait_ge(tr_done, KD * c + k + 1)
                    act.activation(hT[:, k, c * CH:(c + 1) * CH], banks[(c % 2) * KD + k][0:DP, :], ACT.Identity,
                                   scale=gb[:, 0, k:k + 1], bias=gb[:, 1, k:k + 1]).then_inc(hT_ready, 1)
            for j in range(NCH * MF):
                c, m = j // MF, j % MF
                act.wait_ge(up_done, j + 1)
                act.activation(gT[:, m, c * CH:(c + 1) * CH], banks[4 + j % 2][:, :], ACT.Gelu,
                               bias=b1[:, m:m + 1]).then_inc(gelu_ready, 1)

        @block.vector
        def _(dve):
            for i in range(NT):
                dve.wait_ge(down_done, i + 1)
                dve.wait_ge(biased, 2 * (i + 1))
                dve.tensor_tensor(g.x[:, i, :], g.x[:, i, :], banks[6 + i % 2][:, 0:D], ALU.add).then_inc(added, 1)
            dve.wait_ge(added, NT)


def moe_logits(nc, g, e):
    (phi_in, phi_turned, phi_ready, square_ready, norm_step, phiT_ready, x_turned, xT_ready, lg_done, lg_ready,
     rmax_ready, cmax_step, cmax_turned, cmax_col, cmax_diag, cmax_rep, cmax_ready, wT_turned, wT_ready) = sems(
         nc, g, " ".join("moe_" + n for n in (
             "phi_in phi_turned phi_ready square_ready norm_step phiT_ready x_turned xT_ready logits_done "
             "logits_ready rmax_ready cmax_step cmax_turned cmax_col cmax_diag cmax_replicated cmax_ready "
             "ln_turned ln_ready").split()))
    with ExitStack() as local, nc.allow_non_contiguous_dma(reason="small weights"):
        def sb(name, shape, dt=F32):
            return local.enter_context(nc.sbuf_tensor(name, shape, dt))
        phi = sb("phi_rows", [P, ST, D])
        phiT = sb("phi_T", [DP, KD, S])
        sq = sb("phi_squares", [DP, KD, S])
        rn = sb("phi_norm", [DP, KD, SL])
        xT = sb("moe_x_T", [DP, KD, L])
        cm = sb("tile_cmax", [P, S])
        cc = sb("cmax_cols", [P, ST])
        dg = sb("cmax_diag", [P, ST, P])
        lng = sb("expert_ln", [NE, 2, D])
        banks = [local.enter_context(nc.psum_tensor(f"eb{i}", [P, CH], F32)) for i in range(8)]
        block = local.enter_context(nc.Block())
        I = g.ffn

        @block.sync
        def _(sp):
            sp.dma_start(phi[:, :, :], I["phi"].rearrange("(a b) q d -> (b q) a d", b=EG)).then_inc(phi_in, 16)
            sp.dma_start(lng[:, 0, :], I["ln_g"]).then_inc(phi_in, 16)
            sp.dma_start(lng[:, 1, :], I["ln_b"]).then_inc(phi_in, 16)

        @block.tensor
        def _(pe):
            pe.wait_ge(phi_in, 48)
            for k in range(KD):
                for f in range(2):
                    for s in range(ST // 2):
                        ins = pe.transpose(banks[2 * k + f][0:DP, s * P:(s + 1) * P],
                                           phi[:, f * ST // 2 + s, k * DP:(k + 1) * DP], g.ident[:, :])
                    ins.then_inc(phi_turned, 1)
            for v in range(2):
                for k in range(KD):
                    ins = pe.transpose(banks[4][0:DP, (2 * v + k) * NE:(2 * v + k + 1) * NE],
                                       lng[:, v, k * DP:(k + 1) * DP], g.ident[0:NE, 0:NE])
            ins.then_inc(wT_turned, 1)
            pe.wait_ge(square_ready, 2 * KD)
            pe.wait_ge(phi_ready, 2 * KD)
            for c in range(NCH):
                for k in range(KD):
                    if c >= 2:
                        pe.wait_ge(xT_ready, KD * (c - 2) + k + 1)
                    transpose_rows(pe, g, banks, e.xm, c, k, x_turned)
            pe.wait_ge(phiT_ready, KD)
            pe.wait_ge(wT_ready, 1)
            for j in range(2 * NT):
                i, f = j // 2, j % 2
                pe.wait_ge(xT_ready, KD * (i // TPC + 1))
                if j >= 4:
                    pe.wait_ge(lg_ready, j - 3)
                for k in range(KD):
                    ins = pe.matmul(banks[4 + j % 4][:, :], xT[:, k, i * P:(i + 1) * P],
                                    phiT[:, k, f * CH:(f + 1) * CH], start=(k == 0), stop=(k == KD - 1))
                ins.then_inc(lg_done, 1)
            pe.wait_ge(cmax_step, NT)
            for s in range(ST):
                ins = pe.transpose(banks[s // 4][:, (s % 4) * P:(s % 4 + 1) * P], cm[:, s * P:(s + 1) * P], g.ident[:, :])
            ins.then_inc(cmax_turned, 1)
            for s in range(ST):
                pe.wait_ge(cmax_diag, s + 1)
                ins = pe.matmul(banks[2 + s // 4][:, (s % 4) * P:(s % 4 + 1) * P], g.ones[:, :], dg[:, s, :],
                                start=True, stop=True)
            ins.then_inc(cmax_rep, 1)

        @block.scalar
        def _(act):
            for k in range(KD):
                for f in range(2):
                    act.wait_ge(phi_turned, 2 * k + f + 1)
                    src = banks[2 * k + f][0:DP, :]
                    act.activation(sq[:, k, f * CH:(f + 1) * CH], src, ACT.Square).then_inc(square_ready, 1)
                    act.activation(phiT[:, k, f * CH:(f + 1) * CH], src, ACT.Copy).then_inc(phi_ready, 1)
            act.wait_ge(wT_turned, 1)
            act.activation(e.lnT[:, :, :, :], banks[4][0:DP, 0:4 * NE].rearrange("p (v k n) -> p v k n", v=2, k=KD),
                           ACT.Copy).then_inc(wT_ready, 1)
            act.wait_ge(norm_step, KD + 1)
            act.activation(rn[:, :, :], rn[:, :, :], ACT.Sqrt).then_inc(norm_step, 1)
            for c in range(NCH):
                for k in range(KD):
                    act.wait_ge(x_turned, KD * c + k + 1)
                    act.activation(xT[:, k, c * CH:(c + 1) * CH], banks[(c % 2) * KD + k][0:DP, :],
                                   ACT.Copy).then_inc(xT_ready, 1)
            for j in range(2 * NT):
                act.wait_ge(lg_done, j + 1)
                act.activation(e.lg[:, j // 2, (j % 2) * CH:(j % 2 + 1) * CH], banks[4 + j % 4][:, :],
                               ACT.Copy).then_inc(lg_ready, 1)
            act.wait_ge(cmax_rep, 1)
            for f in range(2):
                act.activation(e.cmax[:, f * CH:(f + 1) * CH], banks[2 + f][:, :], ACT.Copy).then_inc(cmax_ready, 1)

        @block.vector
        def _(dve):
            dve.wait_ge(square_ready, 2 * KD)
            for k in range(KD):
                dve.tensor_reduce(rn[:, k, :], sq[:, k, :].rearrange("p (n q) -> p q n", q=SL), AX.X,
                                  ALU.add).then_inc(norm_step, 1)
            dve.wait_ge(norm_step, KD)
            dve.tensor_scalar(rn[:, :, :], rn[:, :, :], 1e-6, None, ALU.add).then_inc(norm_step, 1)
            dve.wait_ge(norm_step, KD + 2)
            dve.reciprocal(rn[:, :, :], rn[:, :, :]).then_inc(norm_step, 1)
            dve.wait_ge(norm_step, KD + 3)
            dve.wait_ge(phi_ready, 2 * KD)
            for k in range(KD):
                v = phiT[:, k, :].rearrange("p (n q) -> p n q", q=SL)
                dve.tensor_tensor(v, v, rn[:, k, :].unsqueeze(1).broadcast_to([DP, NE, SL]),
                                  ALU.mult).then_inc(phiT_ready, 1)
            for i in range(NT):
                dve.wait_ge(lg_ready, 2 * (i + 1))
                dve.tensor_reduce(e.rmax[:, i:i + 1], e.lg[:, i, :], AX.X, ALU.max,
                                  negate=True).then_inc(rmax_ready, 1)
                if i:
                    dve.wait_ge(cmax_step, i)
                    dve.tensor_tensor(cm[:, :], cm[:, :], e.lg[:, i, :], ALU.max).then_inc(cmax_step, 1)
                else:
                    dve.tensor_copy(cm[:, :], e.lg[:, i, :]).then_inc(cmax_step, 1)
            dve.wait_ge(cmax_turned, 1)
            for f in range(2):
                dve.tensor_reduce(cc[:, 4 * f:4 * f + 4], banks[f][:, :].rearrange("p (s t) -> p s t", t=P), AX.X,
                                  ALU.max).then_inc(cmax_col, 1)
            dve.wait_ge(cmax_col, 2)
            for s in range(ST):
                dve.tensor_scalar(dg[:, s, :], g.ident[:, :], cc[:, s:s + 1], None, ALU.mult).then_inc(cmax_diag, 1)
            dve.wait_ge(cmax_ready, 2)
            dve.wait_ge(rmax_ready, NT)


def moe_gather_slots(nc, g, e):
    arg_ready, exp_ready, used, sum_done, recip, rows_ready = sems(
        nc, g, "slot_arg_ready slot_exp_ready slot_exp_used slot_sum_done slot_recip slot_rows_ready")
    with ExitStack() as local:
        def sb(name, shape, dt=F32):
            return local.enter_context(nc.sbuf_tensor(name, shape, dt))
        ed = sb("dispatch", [P, 3, S])
        rc = sb("dispatch_recip", [P, ST])
        banks = [local.enter_context(nc.psum_tensor(f"db{i}", [P, CH], F32)) for i in range(4)]
        block = local.enter_context(nc.Block())
        D1 = D + 1

        @block.vector
        def _(dve):
            for i in range(NT):
                if i >= 3:
                    dve.wait_ge(used, i - 2)
                dve.tensor_tensor(ed[:, i % 3, :], e.lg[:, i, :], e.cmax[:, :], ALU.subtract).then_inc(arg_ready, 1)
            dve.wait_ge(sum_done, 1)
            for s in range(ST):
                b = banks[s // 2][:, (s % 2) * D1:(s % 2 + 1) * D1]
                dve.reciprocal(rc[:, s:s + 1], b[:, D:D1]).then_inc(recip, 1)
            for s in range(ST):
                b = banks[s // 2][:, (s % 2) * D1:(s % 2 + 1) * D1]
                dve.wait_ge(recip, s + 1)
                dve.tensor_scalar(e.xs[:, s, :], b[:, 0:D], rc[:, s:s + 1], None, ALU.mult).then_inc(rows_ready, 1)
            dve.wait_ge(rows_ready, ST)

        @block.scalar
        def _(act):
            for i in range(NT):
                act.wait_ge(arg_ready, i + 1)
                act.activation(ed[:, i % 3, :], ed[:, i % 3, :], ACT.Exp).then_inc(exp_ready, 1)

        @block.tensor
        def _(pe):
            for i in range(NT):
                pe.wait_ge(exp_ready, i + 1)
                for s in range(ST):
                    ins = pe.matmul(banks[s // 2][:, (s % 2) * D1:(s % 2 + 1) * D1], ed[:, i % 3, s * P:(s + 1) * P],
                                    e.xm[:, i, :], start=(i == 0 and s % 2 == 0), stop=(i == NT - 1),
                                    skip_group_check=True)
                ins.then_inc(used, 1)
            pe.matmul(banks[3][0:1, 2 * D1:2 * D1 + 2], g.ident[:, 0:1], g.ident[:, 0:2], start=False, stop=True,
                      skip_group_check=True).then_inc(sum_done, 1)


def moe_experts(nc, g, e):
    PR = EG // 2
    RING = 2 * PR
    (zeroed, turned, scaled, slots_ready, up_done, gelu_ready, h_turned, hT_ready, down_done, ys_ready,
     c_exp, c_turned, c_ready, y_done, c_recip, added, s_out) = sems(nc, g, " ".join("ex_" + n for n in (
         "zeroed slots_turned slots_scaled slots_ready up_done gelu_ready h_turned hT_ready "
         "down_done results_ready combine_exp combine_turned combine_ready y_done combine_recip added "
         "rows_out").split()))
    w_in = sems(nc, g, " ".join(f"ex_w_in{r}" for r in range(RING)))
    b_in = sems(nc, g, "ex_biases_in0 ex_biases_in1")
    with ExitStack() as local, nc.allow_non_contiguous_dma(reason="small weights"):
        def sb(name, shape, dt=F32):
            return local.enter_context(nc.sbuf_tensor(name, shape, dt))
        w1 = sb("ex_w1", [DP, RING, 2, KD, HE])
        w2 = sb("ex_w2", [P, RING, 2, MH, D])
        b1 = sb("ex_b1", [EG, 2, HE])
        b2 = sb("ex_b2", [EG, 2, D])
        xT = [sb(f"slots_T{v}", [DP, KD, S]) for v in range(2)]
        tmp = sb("slots_scaled", [DP, 2, CH])
        hg = sb("gelu_rows", [P, 2, HE])
        hT = [sb(f"gelu_T{v}", [P, MH, P]) for v in range(2)]
        ys = sb("slot_results", [P, ST, D])
        rs = sb("combine_sum", [P, NT])
        rr = sb("combine_recip", [P, NT])
        banks = [local.enter_context(nc.psum_tensor(f"xb{i}", [P, CH], F32)) for i in range(8)]
        block = local.enter_context(nc.Block())
        I = g.ffn

        @block.sync
        def _(sp):
            for q in range(NE // 2):
                if q >= RING:
                    sp.wait_ge(down_done, q // PR - 1)
                if q % PR == 0:
                    t = q // PR
                    sp.dma_start(b1[:, t % 2, :], I["b1"][EG * t:EG * (t + 1), :]).then_inc(b_in[t % 2], 16)
                    sp.dma_start(b2[:, t % 2, :], I["b2"][EG * t:EG * (t + 1), :]).then_inc(b_in[t % 2], 16)
                sp.dma_start(w1[:, q % RING], I["w1"][2 * q:2 * q + 2].rearrange("e (k p) h -> p e k h", p=DP)) \
                  .then_inc(w_in[q % RING], 16)
                sp.dma_start(w2[:, q % RING], I["w2"][2 * q:2 * q + 2].rearrange("e (p m) d -> p e m d", m=MH)) \
                  .then_inc(w_in[q % RING], 16)
            for i in range(NT):
                sp.wait_ge(added, i + 1)
                sp.dma_start(g.out[0, i * P:(i + 1) * P, :], g.x[:, i, :]).then_inc(s_out, 16)
            sp.wait_ge(s_out, 16 * NT)

        @block.gpsimd
        def _(pool):
            for v in range(2):
                pool.memset(xT[v][:, :, :], 0.0).then_inc(zeroed, 1)
                pool.memset(hT[v][:, :, :], 0.0).then_inc(zeroed, 1)

        @block.tensor
        def _(pe):
            def combine_transposes(i):
                pe.wait_ge(c_exp, i + 1)
                if i:
                    pe.wait_ge(c_ready, 2 * i)
                for s in range(ST):
                    ins = pe.transpose(banks[6 + s // 4][:, (s % 4) * P:(s % 4 + 1) * P],
                                       e.lg[:, i, s * P:(s + 1) * P], g.ident[:, :])
                ins.then_inc(c_turned, 1)

            for k in range(KD):
                for f in range(2):
                    for s in range(ST // 2):
                        ins = pe.transpose(banks[2 * k + f][0:DP, s * P:(s + 1) * P],
                                           e.xs[:, f * ST // 2 + s, k * DP:(k + 1) * DP], g.ident[:, :])
                    ins.then_inc(turned, 1)
            pe.wait_ge(zeroed, 4)
            pe.wait_ge(slots_ready, 4 * KD)
            for t in range(ST):
                up, down = banks[t % 2], banks[2 + t % 2]
                pe.wait_ge(b_in[t % 2], 32 * (t // 2 + 1))
                pe.matmul(up[:, 0:HE], g.slot_of[:, :], b1[:, t % 2, :], start=True, stop=False, skip_group_check=True)
                for q in range(PR):
                    r = (t * PR + q) % RING
                    pe.wait_ge(w_in[r], 32 * (t * PR // RING + 1))
                for v in range(2):
                    for k in range(KD):
                        for q in range(PR):
                            ins = pe.matmul(up[32 * q:32 * q + 32, 0:HE],
                                            xT[v][:, k, t * P + 32 * q:t * P + 32 * q + 32],
                                            w1[:, (t * PR + q) % RING, v, k, :], start=False,
                                            stop=(v == 1 and k == KD - 1), skip_group_check=True)
                ins.then_inc(up_done, 1)
                combine_transposes(2 * t)
                pe.wait_ge(gelu_ready, t + 1)
                if t:
                    pe.wait_ge(hT_ready, 2 * t)
                for m in range(MH):
                    ins = pe.transpose(banks[4][:, m * P:(m + 1) * P], hg[:, t % 2, m:HE:MH], g.ident[:, :])
                ins.then_inc(h_turned, 1)
                combine_transposes(2 * t + 1)
                pe.wait_ge(hT_ready, 2 * (t + 1))
                if t >= 2:
                    pe.wait_ge(ys_ready, t - 1)
                pe.matmul(down[:, 0:D], g.slot_of[:, :], b2[:, t % 2, :], start=True, stop=False, skip_group_check=True)
                for v in range(2):
                    for m in range(MH):
                        for q in range(PR):
                            ins = pe.matmul(down[32 * q:32 * q + 32, 0:D], hT[v][:, m, 32 * q:32 * q + 32],
                                            w2[:, (t * PR + q) % RING, v, m, :], start=False,
                                            stop=(v == 1 and m == MH - 1), skip_group_check=True)
                ins.then_inc(down_done, 1)
            pe.wait_ge(ys_ready, ST)
            for i in range(NT):
                pe.wait_ge(c_ready, 2 * (i + 1))
                if i >= 2:
                    pe.wait_ge(added, i - 1)
                for s in range(ST):
                    ins = pe.matmul(banks[i % 2][:, 0:D], e.lg[:, i, s * P:(s + 1) * P], ys[:, s, :],
                                    start=(s == 0), stop=(s == ST - 1))
                ins.then_inc(y_done, 1)

        @block.scalar
        def _(act):
            def combine_exp(i):
                act.activation(e.lg[:, i, :], e.lg[:, i, :], ACT.Exp, bias=e.rmax[:, i:i + 1],
                               accum_out=rs[:, i:i + 1]).then_inc(c_exp, 1)
            for i in range(NT):
                combine_exp(i)
            for t in range(ST):
                act.wait_ge(up_done, t + 1)
                if t >= 2:
                    act.wait_ge(h_turned, t - 1)
                act.activation(hg[:, t % 2, :], banks[t % 2][:, 0:HE], ACT.Gelu).then_inc(gelu_ready, 1)
                act.wait_ge(down_done, t + 1)
                act.activation(ys[:, t, :], banks[2 + t % 2][:, 0:D], ACT.Copy).then_inc(ys_ready, 1)

        @block.vector
        def _(dve):
            dve.wait_ge(zeroed, 4)
            n = 0
            for k in range(KD):
                for f in range(2):
                    dve.wait_ge(turned, 2 * k + f + 1)
                    if n >= 2:
                        dve.wait_ge(slots_ready, 2 * (n - 1))
                    tv = tmp[:, n % 2, :].rearrange("p (n q) -> p n q", q=SL)
                    gn = slice(f * NE // 2, (f + 1) * NE // 2)
                    dve.tensor_tensor(tv, banks[2 * k + f][0:DP, :].rearrange("p (n q) -> p n q", q=SL),
                                      e.lnT[:, 0, k, gn].unsqueeze(2).broadcast_to([DP, NE // 2, SL]),
                                      ALU.mult).then_inc(scaled, 1)
                    dve.wait_ge(scaled, n + 1)
                    for v in range(2):
                        xv = xT[v][:, k, f * CH:(f + 1) * CH].rearrange("p (n q) -> p n q", q=SL)[:, v:NE // 2:2, :]
                        bn = e.lnT[:, 1, k, f * NE // 2 + v:(f + 1) * NE // 2:2]
                        dve.tensor_tensor(xv, tv[:, v:NE // 2:2, :],
                                          bn.unsqueeze(2).broadcast_to([DP, NE // 4, SL]),
                                          ALU.add).then_inc(slots_ready, 1)
                    n += 1

            def combine_copy(i):
                dve.wait_ge(c_turned, i + 1)
                for f in range(2):
                    dve.tensor_copy(e.lg[:, i, f * CH:(f + 1) * CH], banks[6 + f][:, :]).then_inc(c_ready, 1)

            for t in range(ST):
                combine_copy(2 * t)
                dve.wait_ge(h_turned, t + 1)
                if t:
                    dve.wait_ge(down_done, t)
                src = banks[4][:, 0:MH * P].rearrange("p (m q v s) -> p m q v s", m=MH, v=2, s=SL)
                for v in range(2):
                    for_v = hT[v][:, :, :].rearrange("p m (q v s) -> p m q v s", v=2, s=SL)
                    dve.tensor_copy(for_v[:, :, :, v, :], src[:, :, :, v, :]).then_inc(hT_ready, 1)
                combine_copy(2 * t + 1)
            dve.wait_ge(c_exp, NT)
            dve.reciprocal(rr[:, :], rs[:, :]).then_inc(c_recip, 1)
            dve.wait_ge(c_recip, 1)
            for i in range(NT):
                dve.wait_ge(y_done, i + 1)
                dve.scalar_tensor_tensor(out=g.x[:, i, :], in0=banks[i % 2][:, 0:D], scalar=rr[:, i:i + 1],
                                         in1=g.x[:, i, :], op0=ALU.mult, op1=ALU.add).then_inc(added, 1)


def store_out(nc, g, src):
    s_out, = sems(nc, g, "rows_out")
    with nc.Block() as block:
        @block.sync
        def _(sp):
            sp.dma_start(g.out.rearrange("a (i p) d -> p (a i) d", p=P), src[:, :, :]).then_inc(s_out, 16)
            sp.wait_ge(s_out, 16)


def lm_tower(nc, ins, out, upto=9):
    g = Core()
    g.live = []
    g.out = out
    g.ids = ins["x"]
    g.tok = {k[7:]: v for k, v in ins.items() if k.startswith("L0_tok_")}
    g.attn = {k[8:]: v for k, v in ins.items() if k.startswith("L0_attn_")}
    g.ffn = {k[7:]: v for k, v in ins.items() if k.startswith("L0_ffn_")}
    g.ctx = ExitStack()
    with g.ctx as ctx:
        def sb(name, shape, dt=F32):
            return ctx.enter_context(nc.sbuf_tensor(name, shape, dt))
        g.x = sb("x_rows", [P, NT, D])
        g.ident = sb("ident", [P, P])
        g.causal = sb("causal", [P, P])
        g.ones = sb("ones", [P, P])
        g.slot_of = sb("slot_of", [EG, P])
        g.head_of = sb("head_of", [DP, HK])
        with ExitStack() as mamba:
            def mb(name, shape, dt=F32):
                return mamba.enter_context(nc.sbuf_tensor(name, shape, dt))
            g.sel = mb("sel", [3 * NX, NX, P], BF16)
            g.w_in = mb("w_in", [DP, NL, KD, 2 * DI])
            g.norm_w_c = mb("norm_w_c", [DP, NL, KD])
            g.conv_wc = mb("conv_wc", [P, NL, MI, TAPS])
            g.conv_bc = mb("conv_bc", [P, NL, MI])
            g.w_x = mb("w_x", [P, NL, MI, NX + RK])
            g.w_dt = mb("w_dt", [RK, NL, DI])
            g.dt_bc = mb("dt_bc", [P, NL, MI])
            g.a_neg = mb("a_neg", [P, NL, MI, NS])
            g.d_c = mb("d_c", [P, NL, MI])
            g.w_out = mb("w_out", [P, NL, MI, D])
            g.xr = mb("xr", [P, MI, L + TAPS - 1])
            g.sres = mb("sres", [P, MI, L])
            g.u = mb("u", [P, MI, L])
            g.delta = mb("delta", [P, MI, L])
            g.du = mb("du", [P, MI, L])
            g.bcp = mb("bcp", [3 * NX, L], BF16)
            load_and_gather(nc, g)
            for l in range(NL if upto > 1 else upto):
                mamba_front(nc, g, l)
                mamba_scan(nc, g, l)
                retire_semaphores(nc, g)
        if upto > 2:
            with ExitStack() as attn:
                a = Core()
                def ab(name, shape, dt=F32):
                    return attn.enter_context(nc.sbuf_tensor(name, shape, dt))
                a.xa = ab("xa", [P, NT, D])
                a.xs = ab("xs_attn", [P, NT, D])
                a.w_o = ab("w_o", [DP, KD, D])
                a.proj_blocks = ab("proj_blocks", [DP, HK, M])
                a.neg_kmax = ab("neg_kmax", [P, 1])
                normalize_rows(nc, g, "norm0", g.x, a.xa, 1e-5)
                with ExitStack() as qkv:
                    def qb(name, shape, dt=F32):
                        return qkv.enter_context(nc.sbuf_tensor(name, shape, dt))
                    a.qk = qb("qk_T", [DP, 2, KD, L])
                    a.qk2 = qb("qk_squares_T", [DP, 2, KD, L])
                    a.v1 = qb("v_rows", [P, NT, H, DH + 1])
                    with nc.Block() as block:
                        @block.gpsimd
                        def _(pool):
                            pool.memset(a.proj_blocks[:, :, :], 0.0)
                    normalize_rows(nc, g, "norm1", a.xa, a.xs, 1e-5)
                    attn_project(nc, g, a)
                    a.kdd = qb("k_dd", [P, NT, KD, HK, M])
                    attn_key_logits(nc, g, a)
                    attention(nc, g, a)
                normalize_rows(nc, g, "norm2", a.xa, a.xs, 1e-5)
                attn_mlp(nc, g, a)
                retire_semaphores(nc, g)
        if upto > 3:
            with ExitStack() as moe:
                e = Core()
                def eb(name, shape, dt=F32):
                    return moe.enter_context(nc.sbuf_tensor(name, shape, dt))
                e.lg = eb("logits", [P, NT, S])
                e.rmax = eb("neg_rmax", [P, NT])
                e.lnT = eb("expert_ln_T", [DP, 2, KD, NE])
                e.xs = eb("slot_rows", [P, ST, D])
                with ExitStack() as rows:
                    e.xm = rows.enter_context(nc.sbuf_tensor("moe_rows", [P, NT, D + 1], F32))
                    e.cmax = rows.enter_context(nc.sbuf_tensor("cmax", [P, S], F32))
                    with nc.Block() as block:
                        @block.gpsimd
                        def _(pool):
                            pool.memset(e.xm[:, :, D:D + 1], 1.0)
                    normalize_rows(nc, g, "norm3", g.x, e.xm, 1e-5)
                    moe_logits(nc, g, e)
                    moe_gather_slots(nc, g, e)
                normalize_rows(nc, g, "norm4", e.xs, e.xs, 1e-5)
                moe_experts(nc, g, e)
        else:
            store_out(nc, g, g.x)


_INS = ["x"] + ["L0_tok_" + n for n in (
    "emb", "norm_w", "in_proj_w", "conv_w", "conv_b", "x_proj_w", "dt_proj_w", "dt_proj_b", "A_log", "D",
    "out_proj_w")] + ["L0_attn_" + n for n in (
        "ln1_g", "ln1_b", "Wq", "bq", "Wk", "bk", "Wv", "bv", "Wo", "bo", "proj", "ln2_g", "ln2_b", "W1", "b1",
        "W2", "b2")] + ["L0_ffn_" + n for n in ("phi", "ln_g", "ln_b", "w1", "b1", "w2", "b2")]


def kernel(**inputs):
    import numpy as _np
    import concourse.bacc as _bacc
    from concourse import mybir as _mybir
    from concourse.bass_utils import run_bass_kernel_spmd as _run

    nc = _bacc.Bacc("TRN2", target_bir_lowering=False, num_devices=1)
    arrays, ins = {}, {}
    for name in _INS:
        a = _np.ascontiguousarray(inputs[name])
        arrays[f"in_{name}_dram"] = a
        ins[name] = nc.dram_tensor(f"in_{name}_dram", a.shape, _mybir.dt.from_np(a.dtype), kind="ExternalInput").ap()
    out = nc.dram_tensor("out_0_dram", (1, L, D), _mybir.dt.float32, kind="ExternalOutput").ap()
    lm_tower(nc, ins, out)
    r = _run(nc, [arrays], core_ids=[0])
    return r.results[0]["out_0_dram"]
```

```python
from contextlib import ExitStack

import numpy as np

import concourse.bass as bass
from concourse import mybir

F32 = mybir.dt.float32
BF16 = mybir.dt.bfloat16
I32 = mybir.dt.int32
ALU = mybir.AluOpType
ACT = mybir.ActivationFunctionType
AX = mybir.AxisListType

P = 128
L = 2048
NT = L // P
D = 192
KD = 2
DP = D // KD
CH = 512
NCH = L // CH
TPC = CH // P
V = 8000
NL = 2
DI = 384
MI = DI // P
NS = 16
RK = 12
NX = 2 * NS
TAPS = 4
H = 12
DH = 16
HK = H // KD
M = 44
MP = 64
HP = H // 2
FF = 768
MF = FF // P
NE = 64
SL = 16
S = NE * SL
ST = S // P
EG = P // SL
HE = 384
MH = HE // P
PR = EG // 2
W1C = PR * 2 * KD * HE
W2C = PR * 2 * MH * D
A_LOG_MAX = 80.0
LN2 = 0.6931471


class Core:
    pass


def sems(nc, g, names):
    made = [nc.alloc_semaphore(name=n) for n in names.split()]
    g.live += made
    return made


def retire_semaphores(nc, g):
    nc.clear_and_free_semaphores(g.live)
    nc.all_engine_barrier()
    g.live = []


def ks(w):
    return w.rearrange("(k p) n -> p k n", p=DP)


def col(v, p):
    return v.rearrange("(k p) -> p k", p=p)


def load_and_gather(nc, g):
    s_ids, g.s_w, s_gather, s_cst, s_idx = sems(nc, g, "ids_in mamba_weights_in rows_in constants_made indices_made")
    with ExitStack() as local, nc.allow_non_contiguous_dma(reason="small weights"):
        ids = local.enter_context(nc.sbuf_tensor("ids", [P, NT], I32))
        wrap = local.enter_context(nc.sbuf_tensor("wrap", [P, NT], F32))
        idsf = local.enter_context(nc.sbuf_tensor("idsf", [P, NT], F32))
        idx = local.enter_context(nc.sbuf_tensor("idx", [P, NT], I32))
        block = local.enter_context(nc.Block())

        @block.sync
        def _(sp):
            sp.dma_start(ids[:, :], g.ids.rearrange("a (i p) -> p (a i)", p=P)).then_inc(s_ids, 16)
            sp.dma_start(g.w_in[:, :, :], ks(g.tok["in_proj_w"][0])).then_inc(g.s_w, 16)
            n = 16
            for l in range(NL):
                for dst, src in (
                    (g.norm_w_c[:, l, :], col(g.tok["norm_w"][l], DP)),
                    (g.conv_wc[:, l, :, :], g.tok["conv_w"][l].rearrange("(m p) a k -> p m (a k)", p=P)),
                    (g.conv_bc[:, l, :], col(g.tok["conv_b"][l], P)),
                    (g.w_x[:, l, :, 0:NX], g.tok["x_proj_w"][l].rearrange("(m p) n -> p m n", p=P)[:, :, RK:RK + NX]),
                    (g.w_x[:, l, :, NX:NX + RK], g.tok["x_proj_w"][l].rearrange("(m p) n -> p m n", p=P)[:, :, 0:RK]),
                    (g.w_dt[:, l, :], g.tok["dt_proj_w"][l]),
                    (g.dt_bc[:, l, :], col(g.tok["dt_proj_b"][l], P)),
                    (g.a_neg[:, l, :, :], g.tok["A_log"][l].rearrange("(m p) n -> p m n", p=P)),
                    (g.d_c[:, l, :], col(g.tok["D"][l], P)),
                    (g.w_out[:, l], g.tok["out_proj_w"][l].rearrange("(m p) n -> p m n", p=P)),
                ):
                    sp.dma_start(dst, src).then_inc(g.s_w, 16)
                    n += 16
            g.n_w = n
            sp.wait_ge(s_gather, 16 * NT)
            sp.wait_ge(g.s_w, n)

        @block.vector
        def _(dve):
            dve.wait_ge(s_ids, 16)
            dve.tensor_scalar(wrap[:, :], ids[:, :], 0.0, float(V), ALU.is_lt, ALU.mult).then_inc(s_idx, 1)
            dve.wait_ge(s_idx, 1)
            dve.tensor_tensor(idsf[:, :], ids[:, :], wrap[:, :], ALU.add).then_inc(s_idx, 1)
            dve.wait_ge(s_idx, 2)
            dve.tensor_scalar(idx[:, :], idsf[:, :], 0.0, float(V - 1), ALU.max, ALU.min).then_inc(s_idx, 1)
            dve.wait_ge(g.s_w, g_total_w(g))
            dve.tensor_scalar(g.a_neg[:, :, :, :], g.a_neg[:, :, :, :], A_LOG_MAX, None, ALU.min).then_inc(s_idx, 1)
            dve.wait_ge(s_idx, 5)
            dve.tensor_scalar(g.a_neg[:, :, :, :], g.a_neg[:, :, :, :], -1.0, None, ALU.mult).then_inc(s_idx, 1)

        @block.scalar
        def _(act):
            act.wait_ge(s_idx, 4)
            act.activation(g.a_neg[:, :, :, :], g.a_neg[:, :, :, :], ACT.Exp).then_inc(s_idx, 1)

        @block.gpsimd
        def _(pool):
            pool.memset(g.ident[:, :], 0.0).then_inc(s_cst, 1)
            pool.memset(g.sel[:, :, :], 0.0).then_inc(s_cst, 1)
            pool.memset(g.causal[:, :], 1.0).then_inc(s_cst, 1)
            pool.memset(g.ones[:, :], 1.0).then_inc(s_cst, 1)
            pool.memset(g.slot_of[:, :], 1.0).then_inc(s_cst, 1)
            pool.memset(g.head_of[:, :], 0.5).then_inc(s_cst, 1)
            pool.memset(g.bcp[:, L:L + CH], 0.0).then_inc(s_cst, 1)
            pool.wait_ge(s_cst, 7)
            pool.affine_select(out=g.ident[:, :], in_=g.ident[:, :], compare_op=ALU.not_equal, fill=1.0,
                               base=0, pattern=[[-1, P]], channel_multiplier=1).then_inc(s_cst, 1)
            pool.affine_select(out=g.causal[:, :], in_=g.causal[:, :], compare_op=ALU.is_ge, fill=0.0,
                               base=0, pattern=[[1, P]], channel_multiplier=-1).then_inc(s_cst, 1)
            for a in range(3):
                pool.affine_select(out=g.sel[:, :, :], in_=g.sel[:, :, :], compare_op=ALU.not_equal, fill=1.0,
                                   base=-NX * a, pattern=[[-1, NX], [0, P]],
                                   channel_multiplier=1).then_inc(s_cst, 1)
                pool.wait_ge(s_cst, 10 + a)
            for out, n, a in ((g.head_of, HK, -DH), (g.slot_of, P, 1)):
                cm = 1 if a < 0 else -SL
                pool.affine_select(out=out[:, :], in_=out[:, :], compare_op=ALU.is_ge, fill=0.0,
                                   base=0, pattern=[[a, n]], channel_multiplier=cm).then_inc(s_cst, 1)
            pool.wait_ge(s_cst, 14)
            for out, n, a in ((g.head_of, HK, DH), (g.slot_of, P, -1)):
                cm = -1 if a > 0 else SL
                pool.affine_select(out=out[:, :], in_=out[:, :], compare_op=ALU.is_ge, fill=0.0,
                                   base=DH - 1, pattern=[[a, n]], channel_multiplier=cm).then_inc(s_cst, 1)
            pool.wait_ge(s_idx, 3)
            for i in range(NT):
                pool.indirect_dma_start(g.x[:, i, :], None, g.tok["emb"],
                                        bass.IndirectOffsetOnAxis(ap=idx[:, i:i + 1], axis=0)).then_inc(s_gather, 16)
            pool.wait_ge(s_cst, 16)


def g_total_w(g):
    return 16 * (10 * NL + 1)


def mamba_front(nc, g, l):
    (sumsq, meansq, rms, rstd_done, xs_ready, tr_done, xT_ready, proj_done, xr_ready, res_ready, conv_step,
     conv_done, u_ready, xp_done, bc_ready, dtT_ready, split_step, dt_done, abs_done, exp_done, ln_done,
     sp_step, delta_ready) = sems(nc, g, " ".join(f"{n}{l}" for n in (
        "sumsq meansq rms rstd_done xs_ready transposed xT_ready projected xr_ready res_ready conv_step "
        "conv_done u_ready x_projected bc_ready dtT_ready split_step dt_projected abs_done exp_done ln_done "
        "softplus_step delta_ready").split()))
    with ExitStack() as local:
        def sb(name, shape, dt=F32):
            return local.enter_context(nc.sbuf_tensor(f"{name}{l}", shape, dt))
        ss = sb("ss", [P, NT])
        rstd = sb("rstd", [P, NT])
        ax = sb("ax", [P, 2, MI, CH])
        dd = sb("dd", [P, 2, MI, CH])
        cv = sb("cv", [P, MI, CH])
        bcf = sb("bcf", [NX, 2, CH])
        mid = sb("mid", [NX, CH], BF16)
        dtT = sb("dtT", [RK, 2, CH])
        xs = g.delta[:, :, :].rearrange("p m t -> p (m t)")[:, 0:NT * D].rearrange("p (i d) -> p i d", d=D)
        xT = g.du[0:DP, :, :].rearrange("p m t -> p (m t)")[:, 0:KD * L].rearrange("p (k t) -> p k t", k=KD)
        banks = [local.enter_context(nc.psum_tensor(f"fb{l}_{i}", [P, CH], F32)) for i in range(8)]
        block = local.enter_context(nc.Block())

        @block.scalar
        def _(act):
            for i in range(NT):
                act.activation(xs[:, i, :], g.x[:, i, :], ACT.Square, accum_out=ss[:, i:i + 1]).then_inc(sumsq, 1)
            act.wait_ge(meansq, 1)
            act.activation(ss[:, :], ss[:, :], ACT.Sqrt).then_inc(rms, 1)
            for c in range(NCH):
                for k in range(KD):
                    act.wait_ge(tr_done, KD * c + k + 1)
                    act.activation(xT[:, k, c * CH:(c + 1) * CH], banks[(c % 2) * KD + k][0:DP, :], ACT.Copy,
                                   scale=g.norm_w_c[:, l, k:k + 1]).then_inc(xT_ready, 1)
            for c in range(NCH):
                for m in range(MI):
                    j = c * 2 * MI + 2 * m + 1
                    act.wait_ge(proj_done, j + 1)
                    act.activation(g.sres[:, m, c * CH:(c + 1) * CH], banks[4 + j % 4][:, :],
                                   ACT.Silu).then_inc(res_ready, 1)
                for m in range(MI):
                    act.wait_ge(conv_done, MI * c + m + 1)
                    act.activation(g.u[:, m, c * CH:(c + 1) * CH], cv[:, m, :], ACT.Silu,
                                   bias=g.conv_bc[:, l, m:m + 1]).then_inc(u_ready, 1)
            for c in range(NCH):
                act.wait_ge(xp_done, c + 1)
                if c >= 2:
                    act.wait_ge(split_step, 5 * (c - 1))
                    act.wait_ge(dt_done, MI * (c - 1))
                act.activation(bcf[:, c % 2, :], banks[c % 2][0:NX, :], ACT.Copy).then_inc(bc_ready, 1)
                act.activation(dtT[:, c % 2, :], banks[c % 2][NX:NX + RK, :], ACT.Copy).then_inc(dtT_ready, 1)
                for m in range(MI):
                    j = MI * c + m
                    act.wait_ge(dt_done, j + 1)
                    if m == 0 and c >= 2:
                        act.wait_ge(delta_ready, MI * (c - 1))
                    act.activation(ax[:, c % 2, m, :], banks[2 + j % 4][:, :], ACT.Abs,
                                   bias=g.dt_bc[:, l, m:m + 1]).then_inc(abs_done, 1)
                    act.activation(g.delta[:, m, c * CH:(c + 1) * CH], banks[2 + j % 4][:, :], ACT.Relu,
                                   bias=g.dt_bc[:, l, m:m + 1]).then_inc(abs_done, 1)
                act.wait_ge(abs_done, 2 * MI * (c + 1))
                act.activation(ax[:, c % 2, :, :], ax[:, c % 2, :, :], ACT.Exp, scale=-1.0).then_inc(exp_done, 1)
                act.wait_ge(exp_done, c + 1)
                if c >= 2:
                    act.wait_ge(delta_ready, MI * (c - 1))
                act.activation(dd[:, c % 2, :, :], ax[:, c % 2, :, :], ACT.Ln, bias=1.0).then_inc(ln_done, 1)

        @block.vector
        def _(dve):
            dve.wait_ge(sumsq, NT)
            dve.tensor_scalar(ss[:, :], ss[:, :], 1.0 / D, 1e-5, ALU.mult, ALU.add).then_inc(meansq, 1)
            dve.wait_ge(rms, 1)
            dve.reciprocal(rstd[:, :], ss[:, :]).then_inc(rstd_done, 1)
            dve.wait_ge(rstd_done, 1)
            for i in range(NT):
                dve.tensor_scalar(xs[:, i, :], g.x[:, i, :], rstd[:, i:i + 1], None, ALU.mult).then_inc(xs_ready, 1)
            dve.memset(g.xr[:, :, 0:TAPS - 1], 0.0).then_inc(conv_step, 1)
            steps = 1
            for c in range(NCH):
                for m in range(MI):
                    j = c * 2 * MI + 2 * m
                    dve.wait_ge(proj_done, j + 1)
                    dve.tensor_copy(g.xr[:, m, TAPS - 1 + c * CH:TAPS - 1 + (c + 1) * CH],
                                    banks[4 + j % 4][:, :]).then_inc(xr_ready, 1)
                dve.wait_ge(xr_ready, MI * (c + 1))
                if c:
                    dve.wait_ge(u_ready, MI * c)
                for k in range(TAPS):
                    dve.wait_ge(conv_step, steps)
                    for m in range(MI):
                        src = g.xr[:, m, c * CH + k:c * CH + k + CH]
                        w = g.conv_wc[:, l, m, k:k + 1]
                        if k == 0:
                            ins = dve.tensor_scalar(cv[:, m, :], src, w, None, ALU.mult)
                        else:
                            ins = dve.scalar_tensor_tensor(out=cv[:, m, :], in0=src, scalar=w, in1=cv[:, m, :],
                                                           op0=ALU.mult, op1=ALU.add)
                        if k < TAPS - 1:
                            ins.then_inc(conv_step, 1)
                            steps += 1
                        else:
                            ins.then_inc(conv_done, 1)
            n = 0
            for c in range(NCH):
                cc = slice(c * CH, (c + 1) * CH)
                dve.wait_ge(bc_ready, c + 1)
                b = bcf[:, c % 2, :]
                for out, i0, i1 in ((g.bcp[0:NX, cc], b, None), (b, b, g.bcp[0:NX, cc]),
                                    (mid[:, :], b, None), (g.bcp[NX:2 * NX, cc], mid[:, :], None),
                                    (g.bcp[2 * NX:3 * NX, cc], b, mid[:, :])):
                    if i1 is None:
                        ins = dve.tensor_copy(out, i0)
                    else:
                        ins = dve.tensor_tensor(out, i0, i1, ALU.subtract)
                    ins.then_inc(split_step, 1)
                    n += 1
                    dve.wait_ge(split_step, n)
                dve.wait_ge(ln_done, c + 1)
                e, ln = ax[:, c % 2, :, :], dd[:, c % 2, :, :]
                r = cv
                k0 = 6 * c
                dve.tensor_scalar(r[:, :, :], e, 1.0, -1.0, ALU.add, ALU.add).then_inc(sp_step, 1)
                dve.wait_ge(sp_step, k0 + 1)
                dve.tensor_tensor(r[:, :, :], e, r[:, :, :], ALU.subtract).then_inc(sp_step, 1)
                dve.wait_ge(sp_step, k0 + 2)
                dve.tensor_tensor(r[:, :, :], r[:, :, :], ln, ALU.add).then_inc(sp_step, 1)
                dve.wait_ge(sp_step, k0 + 3)
                dve.scalar_tensor_tensor(out=r[:, :, :], in0=e, scalar=LN2, in1=r[:, :, :], op0=ALU.mult,
                                         op1=ALU.max).then_inc(sp_step, 1)
                dve.wait_ge(sp_step, k0 + 4)
                dve.tensor_tensor(g.delta[:, :, cc], g.delta[:, :, cc], r[:, :, :], ALU.add).then_inc(sp_step, 1)
                dve.wait_ge(sp_step, k0 + 5)
                dve.tensor_tensor(g.du[:, :, cc], g.delta[:, :, cc], g.u[:, :, cc],
                                  ALU.mult).then_inc(sp_step, 1)
                dve.wait_ge(sp_step, k0 + 6)
                dve.sem_inc(delta_ready, MI)

        @block.tensor
        def _(pe):
            for c in range(NCH):
                pe.wait_ge(xs_ready, TPC * (c + 1))
                for k in range(KD):
                    if c >= 2:
                        pe.wait_ge(xT_ready, KD * (c - 2) + k + 1)
                    for i in range(TPC):
                        ins = pe.transpose(banks[(c % 2) * KD + k][0:DP, i * P:(i + 1) * P],
                                           xs[:, c * TPC + i, k * DP:(k + 1) * DP], g.ident[:, :])
                    ins.then_inc(tr_done, 1)
            for c in range(NCH):
                pe.wait_ge(xT_ready, KD * (c + 1))
                for j6 in range(2 * MI):
                    j = c * 2 * MI + j6
                    m = j6 // 2 + MI * (j6 % 2)
                    if j >= 4:
                        pe.wait_ge(res_ready if j % 2 else xr_ready, (j - 4) // 2 + 1)
                    for k in range(KD):
                        ins = pe.matmul(banks[4 + j % 4][:, :], g.w_in[:, k, m * P:(m + 1) * P],
                                        xT[:, k, c * CH:(c + 1) * CH], start=(k == 0), stop=(k == KD - 1))
                    ins.then_inc(proj_done, 1)
            pe.wait_ge(xr_ready, MI * NCH)
            pe.wait_ge(res_ready, MI * NCH)
            for c in range(NCH):
                pe.wait_ge(u_ready, MI * (c + 1))
                if c >= 2:
                    pe.wait_ge(dtT_ready, c - 1)
                for m in range(MI):
                    ins = pe.matmul(banks[c % 2][0:NX + RK, :], g.w_x[:, l, m, :], g.u[:, m, c * CH:(c + 1) * CH],
                                    start=(m == 0), stop=(m == MI - 1))
                ins.then_inc(xp_done, 1)
                pe.wait_ge(dtT_ready, c + 1)
                for m in range(MI):
                    j = MI * c + m
                    if j >= 4:
                        pe.wait_ge(abs_done, 2 * (j - 3))
                    pe.matmul(banks[2 + j % 4][:, :], g.w_dt[:, l, m * P:(m + 1) * P], dtT[:, c % 2, :],
                              start=True, stop=True).then_inc(dt_done, 1)


def mamba_scan(nc, g, l):
    JP = 2 * MI
    NP2 = NS // 2
    (b_rep, c_rep, b_copied, decay_ready, decay_free, in_ready, in_free, scanned, carried, weighted, hc_free,
     gated, diag_made, out_done, added, pool_turns, w_in_loaded) = sems(nc, g, " ".join(f"{n}{l}" for n in (
        "b_replicated c_replicated b_copied decay_ready decay_free input_ready input_free scanned carried "
        "weighted hc_free gated diag_made out_projected x_added pool_turns w_in_loaded").split()))
    with ExitStack() as local:
        def sb(name, shape, dt=F32):
            return local.enter_context(nc.sbuf_tensor(f"{name}{l}", shape, dt))
        brep = sb("brep", [P, 2, CH])
        inp = sb("inp", [P, JP, CH])
        hst = sb("hst", [P, JP, CH])
        hc = sb("hc", [P, MI, CH])
        carry = sb("carry", [P, NS * MI])
        diag = sb("diag", [P, MI, P])
        psy = [local.enter_context(nc.psum_tensor(f"psy{l}_{m}", [P, CH], F32)) for m in range(MI)]
        psa = [local.enter_context(nc.psum_tensor(f"psa{l}_{m}", [P, CH], F32)) for m in range(2)]
        psc = [local.enter_context(nc.psum_tensor(f"psc{l}_{m}", [P, CH], F32)) for m in range(2)]
        psb = local.enter_context(nc.psum_tensor(f"psb{l}", [P, CH], F32))
        y = g.xr
        block = local.enter_context(nc.Block())

        @block.sync
        def _(sp):
            if l + 1 < NL:
                sp.dma_start(g.w_in[:, :, :], ks(g.tok["in_proj_w"][l + 1])).then_inc(w_in_loaded, 16)
                sp.wait_ge(w_in_loaded, 16)

        @block.tensor
        def _(pe):
            def replicate_b(c, n, q):
                pe.wait_ge(b_copied, q + 1)
                pe.matmul(psb[:, :], g.sel[:, n, :], g.bcp[:, bass.ds(c * CH, CH)], start=True,
                          stop=True).then_inc(b_rep, 1)

            def replicate_c(c, n, e):
                pe.matmul(psc[e][:, :], g.sel[:, n + NS, :], g.bcp[:, bass.ds(c * CH, CH)], start=True,
                          stop=True).then_inc(c_rep, 1)

            def accumulate(seen, stop):
                for m in range(MI):
                    pe.wait_ge(weighted, seen + m + 1)
                    pe.matmul(psy[m][:, :], g.ident[:, :], hc[:, m, :], start=False, stop=stop,
                              skip_group_check=True).then_inc(hc_free, 1)

            pe.sem_inc(hc_free, MI)
            for e in range(2):
                pe.wait_ge(b_copied, e + 1)
                pe.matmul(psb[:, :], g.sel[:, e, :], g.bcp[:, 0:CH], start=True, stop=True).then_inc(b_rep, 1)
                pe.matmul(psc[e][:, :], g.sel[:, e + NS, :], g.bcp[:, 0:CH], start=True, stop=True).then_inc(c_rep, 1)
            pe.wait_ge(diag_made, MI)
            with pe.Fori(0, NCH) as c:
                pe.wait_ge(gated, MI * c + MI)
                for m in range(MI):
                    pe.matmul(psy[m][:, :], diag[:, m, :], g.u[:, m, bass.ds(c * CH, CH)], start=True, stop=False,
                              skip_group_check=True)
                with pe.Fori(0, NP2 - 1) as p:
                    for e in range(2):
                        replicate_b(c, p * 2 + (e + 2), c * NS + p * 2 + (e + 2))
                        accumulate(c * (NS * MI) + p * JP + MI * e, False)
                        replicate_c(c, p * 2 + (e + 2), e)
                for e in range(2):
                    replicate_b(c + 1, e, c * NS + NS + e)
                    accumulate(c * (NS * MI) + (NP2 - 1) * JP + MI * e, e == 1)
                    replicate_c(c + 1, e, e)
            for i in range(NT):
                pe.wait_ge(gated, MI * (2 + i // TPC))
                if i >= 2:
                    pe.wait_ge(added, i - 1)
                for m in range(MI):
                    ins = pe.matmul(psa[i % 2][:, 0:D], y[:, m, i * P:(i + 1) * P], g.w_out[:, l, m, :],
                                    start=(m == 0), stop=(m == MI - 1))
                ins.then_inc(out_done, 1)

        @block.scalar
        def _(act):
            act.preload_act_table(ACT.Exp)
            act.sem_inc(b_copied, 1)

            def copy_b(e, q):
                act.wait_ge(b_rep, q + 1)
                act.wait_ge(in_ready, q * MI)
                act.activation(brep[:, e, :], psb[:, :], ACT.Copy).then_inc(b_copied, 1)

            act.wait_ge(b_rep, 1)
            act.activation(brep[:, 0, :], psb[:, :], ACT.Copy).then_inc(b_copied, 1)
            with act.Fori(0, NCH) as c:
                with act.Fori(0, NP2) as p:
                    for e in range(2):
                        for m in range(MI):
                            j = MI * e + m
                            act.wait_ge(decay_free, (c * NP2 + p) * JP + j + 1)
                            act.activation(psa[j % 2][:, :], g.delta[:, m, bass.ds(c * CH, CH)], ACT.Exp,
                                           scale=g.a_neg[:, l, m, bass.ds(p * 2 + e, 1)]).then_inc(decay_ready, 1)
                            if m == 0:
                                copy_b(1 - e, c * NS + p * 2 + (e + 1))

        @block.gpsimd
        def _(pool):
            pool.sem_inc(in_ready, MI)
            with pool.Fori(0, NCH) as c:
                with pool.Fori(0, NP2) as p:
                    for e in range(2):
                        pool.wait_ge(b_copied, c * NS + p * 2 + e + 2)
                        for m in range(MI):
                            j = MI * e + m
                            pool.wait_ge(in_free, (c * NP2 + p) * JP + j + 1)
                            pool.sem_inc(pool_turns, 1)
                            pool.tensor_tensor(inp[:, j, :], g.du[:, m, bass.ds(c * CH, CH)], brep[:, e, :],
                                               ALU.mult).then_inc(in_ready, 1)

        @block.vector
        def _(dve):
            dve.sem_inc(gated, MI)
            dve.sem_inc(decay_free, 2)
            dve.sem_inc(in_free, JP)
            dve.memset(carry[:, :], 0.0).then_inc(carried, 1)
            for m in range(MI):
                dve.tensor_scalar(diag[:, m, :], g.ident[:, :], g.d_c[:, l, m:m + 1], None,
                                  ALU.mult).then_inc(diag_made, 1)

            with dve.Fori(0, NCH) as c:
                with dve.Fori(0, NP2) as p:
                    base = (c * NP2 + p) * JP

                    def scan(j):
                        m, e = j % MI, j // MI
                        dve.wait_ge(decay_ready, base + j + 1)
                        dve.wait_ge(in_ready, base + (MI + j + 1))
                        if j == 0:
                            dve.wait_ge(carried, (c * NP2 + p) * 2 + 1)
                        dve.tensor_tensor_scan(hst[:, j, :], psa[j % 2][:, :], inp[:, j, :],
                                               carry[:, bass.ds(p * JP + j, 1)], ALU.mult,
                                               ALU.add).then_inc(scanned, 1)

                    def weight(j):
                        m, e = j % MI, j // MI
                        dve.wait_ge(scanned, base + j + 1)
                        dve.sem_inc(decay_free, 1)
                        dve.sem_inc(in_free, 1)
                        if m == 0:
                            dve.wait_ge(c_rep, c * NS + p * 2 + e + 1)
                        dve.wait_ge(hc_free, base + j + 1)
                        dve.tensor_tensor(hc[:, m, :], hst[:, j, :], psc[e][:, :], ALU.mult).then_inc(weighted, 1)

                    scan(0)
                    for j in range(1, JP):
                        scan(j)
                        weight(j - 1)
                        if j % MI == 0:
                            e = j // MI - 1
                            dve.tensor_copy(carry[:, bass.ds(p * JP + MI * e, MI)],
                                            hst[:, MI * e:MI * e + MI, CH - 1]).then_inc(carried, 1)
                    weight(JP - 1)
                    dve.tensor_copy(carry[:, bass.ds(p * JP + MI, MI)],
                                    hst[:, MI:JP, CH - 1]).then_inc(carried, 1)
                for m in range(MI):
                    dve.wait_ge(hc_free, c * (NS * MI) + (NS * MI + m + 1))
                    dve.tensor_tensor(y[:, m, bass.ds(c * CH, CH)], g.sres[:, m, bass.ds(c * CH, CH)],
                                      psy[m][:, :], ALU.mult).then_inc(gated, 1)
            for i in range(NT):
                dve.wait_ge(out_done, i + 1)
                dve.tensor_tensor(g.x[:, i, :], g.x[:, i, :], psa[i % 2][:, 0:D], ALU.add).then_inc(added, 1)
            dve.wait_ge(added, NT)


def normalize_rows(nc, g, name, src, dst, eps, then=None):
    stats, mean_var, root, recip, rows = sems(nc, g, " ".join(
        f"{name}_{n}" for n in "stats mean_var root reciprocal rows".split()))
    n = src.shape[1]
    with ExitStack() as local:
        st = local.enter_context(nc.sbuf_tensor(f"{name}_st", [P, n, 6], F32))
        mv = local.enter_context(nc.sbuf_tensor(f"{name}_mv", [P, n, 2], F32))
        rs = local.enter_context(nc.sbuf_tensor(f"{name}_rs", [P, n], F32))
        block = local.enter_context(nc.Block())

        @block.vector
        def _(dve):
            for i in range(n):
                dve.bn_stats(st[:, i, :], src[:, i, 0:D]).then_inc(stats, 1)
            for i in range(n):
                dve.wait_ge(stats, i + 1)
                dve.bn_aggr(mv[:, i, :], st[:, i, :]).then_inc(mean_var, 1)
            dve.wait_ge(mean_var, n)
            dve.tensor_scalar(rs[:, :], mv[:, :, 1], eps, None, ALU.add).then_inc(mean_var, 1)
            dve.wait_ge(root, 1)
            dve.reciprocal(rs[:, :], rs[:, :]).then_inc(recip, 1)
            dve.wait_ge(recip, 1)
            for i in range(n):
                dve.tensor_scalar(dst[:, i, 0:D], src[:, i, 0:D], mv[:, i, 0:1], rs[:, i:i + 1],
                                  ALU.subtract, ALU.mult).then_inc(rows, 1)
            dve.wait_ge(rows, n)

        @block.scalar
        def _(act):
            act.wait_ge(mean_var, n + 1)
            act.activation(rs[:, :], rs[:, :], ACT.Sqrt).then_inc(root, 1)


def transpose_rows(pe, g, banks, src, c, k, done, ready=None, seen=0):
    for i in range(TPC):
        ins = pe.transpose(banks[(c % 2) * KD + k][0:DP, i * P:(i + 1) * P],
                           src[:, c * TPC + i, k * DP:(k + 1) * DP], g.ident[:, :])
    ins.then_inc(done, 1)


def attn_project(nc, g, a):
    w_in, tr_done, hT_ready, qk_done, qk_ready, v_done, v_ready, halved, ones_set, bias_in = sems(
        nc, g, "attn_w_in attn_transposed attn_hT_ready qk_projected qk_ready v_projected v_ready "
        "biases_scaled v_ones_set xa_biased")
    with ExitStack() as local, nc.allow_non_contiguous_dma(reason="small weights"):
        def sb(name, shape, dt=F32):
            return local.enter_context(nc.sbuf_tensor(name, shape, dt))
        hT = sb("hT", [DP, KD, L])
        w = sb("w_qkv", [DP, 3, KD, D])
        gb = sb("ln1_gb", [DP, 2, KD])
        qkb = sb("qk_bias", [DP, 2, KD])
        bv = sb("bv_rows", [P, D])
        bo = sb("bo_rows", [P, D])
        banks = [local.enter_context(nc.psum_tensor(f"pb{i}", [P, CH], F32)) for i in range(8)]
        block = local.enter_context(nc.Block())
        I = g.attn

        @block.sync
        def _(sp):
            for dst, src in ((w[:, 0], ks(I["Wq"])), (w[:, 1], ks(I["Wk"])), (w[:, 2], ks(I["Wv"])),
                             (gb[:, 0, :], col(I["ln1_g"], DP)), (gb[:, 1, :], col(I["ln1_b"], DP)),
                             (qkb[:, 0, :], col(I["bq"], DP)), (qkb[:, 1, :], col(I["bk"], DP)),
                             (bv[:, :], I["bv"].partition_broadcast(P)), (bo[:, :], I["bo"].partition_broadcast(P)),
                             (a.w_o[:, :, :], ks(I["Wo"]))):
                sp.dma_start(dst, src).then_inc(w_in, 16)
            for j in range(HK):
                sp.dma_start(a.proj_blocks[DH * j:DH * (j + 1), j, :],
                             I["proj"].rearrange("m d -> d m")).then_inc(w_in, 16)
            sp.wait_ge(w_in, 16 * (10 + HK))

        @block.gpsimd
        def _(pool):
            pool.memset(a.v1[:, :, :, DH:DH + 1], 1.0).then_inc(ones_set, 1)
            pool.wait_ge(w_in, 16 * (10 + HK))
            for i in range(NT):
                pool.tensor_tensor(a.xa[:, i, :], a.xa[:, i, :], bo[:, :], ALU.add).then_inc(bias_in, 1)
            pool.wait_ge(bias_in, NT)

        @block.tensor
        def _(pe):
            for c in range(NCH):
                for k in range(KD):
                    if c >= 2:
                        pe.wait_ge(hT_ready, KD * (c - 2) + k + 1)
                    transpose_rows(pe, g, banks, a.xs, c, k, tr_done)
            pe.wait_ge(w_in, 16 * (10 + HK))
            for c in range(NCH):
                pe.wait_ge(hT_ready, KD * (c + 1))
                for qk in range(2):
                    for m in range(KD):
                        j = (c * 2 + qk) * KD + m
                        if j >= 2:
                            pe.wait_ge(qk_ready, 2 * (j - 1))
                        for k in range(KD):
                            ins = pe.matmul(banks[4 + j % 2][0:DP, :], w[:, qk, k, m * DP:(m + 1) * DP],
                                            hT[:, k, c * CH:(c + 1) * CH], start=(k == 0), stop=(k == KD - 1))
                        ins.then_inc(qk_done, 1)
                for i in range(c * TPC, (c + 1) * TPC):
                    if i >= 2:
                        pe.wait_ge(v_ready, i - 1)
                    for k in range(KD):
                        ins = pe.matmul(banks[6 + i % 2][:, 0:D], hT[:, k, i * P:(i + 1) * P], w[:, 2, k, :],
                                        start=(k == 0), stop=(k == KD - 1))
                    ins.then_inc(v_done, 1)

        @block.scalar
        def _(act):
            act.wait_ge(w_in, 16 * (10 + HK))
            for c in range(NCH):
                for k in range(KD):
                    act.wait_ge(tr_done, KD * c + k + 1)
                    act.activation(hT[:, k, c * CH:(c + 1) * CH], banks[(c % 2) * KD + k][0:DP, :], ACT.Identity,
                                   scale=gb[:, 0, k:k + 1], bias=gb[:, 1, k:k + 1]).then_inc(hT_ready, 1)
            act.wait_ge(halved, 1)
            for c in range(NCH):
                for qk in range(2):
                    for m in range(KD):
                        j = (c * 2 + qk) * KD + m
                        act.wait_ge(qk_done, j + 1)
                        for out, f in ((a.qk[:, qk, m, c * CH:(c + 1) * CH], ACT.Identity),
                                       (a.qk2[:, qk, m, c * CH:(c + 1) * CH], ACT.Square)):
                            act.activation(out, banks[4 + j % 2][0:DP, :], f, scale=DH ** -0.25,
                                           bias=qkb[:, qk, m:m + 1]).then_inc(qk_ready, 1)

        @block.vector
        def _(dve):
            dve.wait_ge(w_in, 16 * (10 + HK))
            dve.tensor_scalar(qkb[:, :, :], qkb[:, :, :], DH ** -0.25, None, ALU.mult).then_inc(halved, 1)
            for i in range(NT):
                dve.wait_ge(v_done, i + 1)
                dve.tensor_tensor(a.v1[:, i, :, 0:DH], banks[6 + i % 2][:, 0:D].rearrange("p (h e) -> p h e", e=DH),
                                  bv[:, :].rearrange("p (h e) -> p h e", e=DH), ALU.add).then_inc(v_ready, 1)


def attn_key_logits(nc, g, a):
    dd_done, diag_copied, kdd_ready, kmax_ready, gmax = sems(
        nc, g, "k_dd_done k_diag_copied k_dd_ready k_max_ready k_global_max")
    with ExitStack() as local:
        def sb(name, shape, dt=F32):
            return local.enter_context(nc.sbuf_tensor(name, shape, dt))
        kd = sb("k_diag", [P, NT, KD, HK])
        km = sb("k_max", [P, NT, KD])
        km1 = sb("k_max1", [P, 1])
        row = sb("k_max_row", [1, 2])
        banks = [local.enter_context(nc.psum_tensor(f"kb{i}", [P, CH], F32)) for i in range(8)]
        block = local.enter_context(nc.Block())
        W = HK * M

        @block.tensor
        def _(pe):
            for i in range(NT):
                if i >= 4:
                    pe.wait_ge(kdd_ready, KD * (i - 3))
                    pe.wait_ge(kmax_ready, KD * (i - 3))
                for k in range(KD):
                    b = banks[(i % 4) * KD + k]
                    t = slice(i * P, (i + 1) * P)
                    pe.matmul(b[:, 0:W], a.qk[:, 1, k, t], a.proj_blocks[:, :, :], start=True, stop=True)
                    pe.matmul(b[:, W:W + HK], a.qk2[:, 1, k, t], g.head_of[:, :], start=True,
                              stop=True).then_inc(dd_done, 1)
            pe.wait_ge(gmax, 1)
            pe.transpose(banks[0][0:1, 0:P], km1[:, :], g.ident[:, :]).then_inc(gmax, 1)
            pe.wait_ge(gmax, 3)
            pe.matmul(banks[1][:, 0:1], g.ones[0:1, :], row[:, 0:1], start=True, stop=True).then_inc(gmax, 1)

        @block.scalar
        def _(act):
            for i in range(NT):
                for k in range(KD):
                    act.wait_ge(dd_done, KD * i + k + 1)
                    act.activation(kd[:, i, k, :], banks[(i % 4) * KD + k][:, W:W + HK],
                                   ACT.Copy).then_inc(diag_copied, 1)

        @block.vector
        def _(dve):
            for i in range(NT):
                for k in range(KD):
                    dd = banks[(i % 4) * KD + k][:, 0:W]
                    dve.wait_ge(diag_copied, KD * i + k + 1)
                    dve.tensor_reduce(km[:, i, k:k + 1], dd, AX.X, ALU.max).then_inc(kmax_ready, 1)
                    dve.tensor_tensor(a.kdd[:, i, k, :, :], dd.rearrange("p (h m) -> p h m", m=M),
                                      kd[:, i, k, :].unsqueeze(2).broadcast_to([P, HK, M]),
                                      ALU.subtract).then_inc(kdd_ready, 1)
            dve.wait_ge(kmax_ready, KD * NT)
            dve.tensor_reduce(km1[:, :], km[:, :, :], AX.XY, ALU.max).then_inc(gmax, 1)
            dve.wait_ge(gmax, 2)
            dve.tensor_reduce(row[:, 0:1], banks[0][0:1, 0:P], AX.X, ALU.max).then_inc(gmax, 1)
            dve.wait_ge(gmax, 4)
            dve.tensor_scalar(a.neg_kmax[:, :], banks[1][:, 0:1], -1.0, None, ALU.mult).then_inc(gmax, 1)


def attention(nc, g, a):
    (qdd_done, qdiag_ready, qmax_ready, qbias_ready, qarg_ready, qexp_ready, qp_ready, kexp_ready, kp_ready,
     turned, turned_copied, at_done, masked, out_done, state_ready, recip, o_ready, padded) = sems(
         nc, g, " ".join("at_" + n for n in (
             "qdd_done qdiag_ready qmax_ready qbias_ready qarg_ready qexp_ready qp_ready kexp_ready kp_ready "
             "turned turned_copied products_done masked out_done state_ready recip o_ready padded").split()))
    with ExitStack() as local:
        def sb(name, shape, dt=F32):
            return local.enter_context(nc.sbuf_tensor(name, shape, dt))
        qd = sb("q_diag", [P, 2, H])
        qm = sb("q_max", [P, 2, H])
        qarg = sb("q_arg", [P, 2, H, M])
        kexp = sb("k_exp", [P, 2, H, M])
        qp = sb("q_feat", [P, 2, H, MP])
        kp = sb("k_feat", [P, 3, H, MP])
        qkT = sb("qk_feat_T", [P, 2, 2 * HP, P])
        am = sb("masked_products", [P, H, P])
        st = sb("state", [P, HP, 2 * (DH + 1)])
        rc = sb("recip_den", [P, 2, H])
        banks = [local.enter_context(nc.psum_tensor(f"ab{i}", [P, CH], F32)) for i in range(8)]
        block = local.enter_context(nc.Block())
        W = HK * M
        E1 = DH + 1
        SC = HP * 2 * E1
        ratio = M ** -0.5

        @block.gpsimd
        def _(pool):
            pool.memset(qp[:, :, :, M:MP], 0.0).then_inc(padded, 1)
            pool.memset(kp[:, :, :, M:MP], 0.0).then_inc(padded, 1)
            pool.memset(st[:, :, :], 0.0).then_inc(padded, 1)
            pool.wait_ge(padded, 3)
            pool.memset(st[0:MP, :, DH:E1], 1e-6).then_inc(padded, 1)
            pool.wait_ge(padded, 4)
            pool.memset(st[MP:P, :, E1 + DH:2 * E1], 1e-6).then_inc(padded, 1)
            pool.wait_ge(padded, 5)
            for i in range(NT):
                if i >= 3:
                    pool.wait_ge(out_done, i - 2)
                pool.wait_ge(kexp_ready, i + 1)
                pool.tensor_scalar(kp[:, i % 3, :, 0:M], kexp[:, i % 2, :, :], 1e-4, ratio, ALU.add,
                                   ALU.mult).then_inc(kp_ready, 1)
                if i >= 2:
                    pool.wait_ge(turned, 3 * (i - 1))
                pool.wait_ge(qexp_ready, i + 1)
                pool.tensor_scalar(qp[:, i % 2, :, 0:M], qarg[:, i % 2, :, :], 1e-4, ratio, ALU.add,
                                   ALU.mult).then_inc(qp_ready, 1)

        @block.scalar
        def _(act):
            def features(i):
                if i >= 2:
                    act.wait_ge(kp_ready, i - 1)
                act.activation(kexp[:, i % 2, :, :], a.kdd[:, i, :, :, :].rearrange("p k h m -> p (k h) m"), ACT.Exp,
                               bias=a.neg_kmax[:, :]).then_inc(kexp_ready, 1)
                for k in range(KD):
                    act.wait_ge(qdd_done, KD * i + k + 1)
                    if i >= 2 and k == 0:
                        act.wait_ge(qbias_ready, i - 1)
                    act.activation(qd[:, i % 2, k * HK:(k + 1) * HK], banks[k][:, W:W + HK],
                                   ACT.Identity).then_inc(qdiag_ready, 1)
                act.wait_ge(qarg_ready, KD * (i + 1))
                act.activation(qarg[:, i % 2, :, :], qarg[:, i % 2, :, :], ACT.Exp).then_inc(qexp_ready, 1)

            def copy_turned(i):
                if i >= 2:
                    act.wait_ge(out_done, i - 1)
                for b in range(3):
                    act.wait_ge(turned, 3 * i + b + 1)
                    act.activation(qkT[:, i % 2, 4 * b:4 * b + 4, :],
                                   banks[2 + b][:, :].rearrange("p (s t) -> p s t", t=P),
                                   ACT.Identity).then_inc(turned_copied, 1)

            features(0)
            features(1)
            copy_turned(0)
            for i in range(NT):
                if i + 1 < NT:
                    copy_turned(i + 1)
                if i + 2 < NT:
                    features(i + 2)

        @block.vector
        def _(dve):
            def features(i):
                for k in range(KD):
                    dve.wait_ge(qdiag_ready, KD * i + k + 1)
                    dve.tensor_reduce(qm[:, i % 2, k * HK:(k + 1) * HK],
                                      banks[k][:, 0:W].rearrange("p (h m) -> p h m", m=M), AX.X,
                                      ALU.max).then_inc(qmax_ready, 1)
                dve.wait_ge(qmax_ready, KD * (i + 1))
                dve.tensor_tensor(qm[:, i % 2, :], qm[:, i % 2, :], qd[:, i % 2, :], ALU.add).then_inc(qbias_ready, 1)
                dve.wait_ge(qbias_ready, i + 1)
                if i >= 2:
                    dve.wait_ge(qp_ready, i - 1)
                for k in range(KD):
                    dve.tensor_tensor(qarg[:, i % 2, k * HK:(k + 1) * HK, :],
                                      banks[k][:, 0:W].rearrange("p (h m) -> p h m", m=M),
                                      qm[:, i % 2, k * HK:(k + 1) * HK].unsqueeze(2).broadcast_to([P, HK, M]),
                                      ALU.subtract).then_inc(qarg_ready, 1)

            def mask(i, r):
                for s in range(2):
                    dve.wait_ge(at_done, 4 * i + 2 * r + s + 1)
                    h = 2 * 3 * r + s
                    dve.tensor_tensor(am[:, h:h + 5:2, :],
                                      banks[5 + s][:, 0:3 * P].rearrange("p (j t) -> p j t", t=P),
                                      g.causal[:, :].unsqueeze(1).broadcast_to([P, 3, P]),
                                      ALU.mult).then_inc(masked, 1)

            features(0)
            features(1)
            for i in range(NT):
                if i:
                    dve.wait_ge(out_done, i)
                mask(i, 0)
                mask(i, 1)
                if i + 2 < NT:
                    features(i + 2)
                dve.wait_ge(out_done, i + 1)
                ob = banks[7][:, 0:SC].rearrange("p (h e) -> p h e", e=E1)
                dve.reciprocal(rc[:, i % 2, :], ob[:, :, DH]).then_inc(recip, 1)
                sp = banks[7][:, SC:2 * SC].rearrange("p (j e) -> p j e", e=2 * E1)
                if i == 0:
                    dve.wait_ge(padded, 5)
                else:
                    dve.wait_ge(state_ready, 2 * i)
                for s in range(2):
                    q, e = slice(MP * s, MP * (s + 1)), slice(E1 * s, E1 * (s + 1))
                    dve.tensor_tensor(st[q, :, e], st[q, :, e], sp[q, :, e], ALU.add).then_inc(state_ready, 1)
                dve.wait_ge(recip, i + 1)
                dve.tensor_tensor(a.o[:, i, :].rearrange("p (h e) -> p h e", e=DH), ob[:, :, 0:DH],
                                  rc[:, i % 2, :].unsqueeze(2).broadcast_to([P, H, DH]),
                                  ALU.mult).then_inc(o_ready, 1)

        @block.tensor
        def _(pe):
            def logits(i):
                if i:
                    pe.wait_ge(qarg_ready, KD * i)
                for k in range(KD):
                    t = slice(i * P, (i + 1) * P)
                    pe.matmul(banks[k][:, 0:W], a.qk[:, 0, k, t], a.proj_blocks[:, :, :], start=True, stop=True)
                    pe.matmul(banks[k][:, W:W + HK], a.qk2[:, 0, k, t], g.head_of[:, :], start=True,
                              stop=True).then_inc(qdd_done, 1)

            def turn(i):
                for s in range(2 * HP):
                    f, n, j = (kp, 3, s) if s < HP else (qp, 2, s - HP)
                    if s % 4 == 0 and i:
                        pe.wait_ge(turned_copied, 3 * (i - 1) + s // 4 + 1)
                    if s == 0:
                        pe.wait_ge(kp_ready, i + 1)
                    if s == HP:
                        pe.wait_ge(qp_ready, i + 1)
                    ins = pe.transpose(banks[2 + s // 4][:, (s % 4) * P:(s % 4 + 1) * P],
                                       f[:, i % n, 2 * j:2 * j + 2, :].rearrange("p h m -> p (h m)"), g.ident[:, :])
                    if s % 4 == 3:
                        ins.then_inc(turned, 1)

            def products(i, r):
                if r:
                    pe.wait_ge(masked, 4 * i + 2)
                else:
                    pe.wait_ge(turned_copied, 3 * (i + 1))
                    if i:
                        pe.wait_ge(masked, 4 * i)
                for s in range(2):
                    q = slice(MP * s, MP * s + M)
                    for j in range(3 * r, 3 * r + 3):
                        ins = pe.matmul(banks[5 + s][:, (j % 3) * P:(j % 3 + 1) * P], qkT[q, i % 2, j, :],
                                        qkT[q, i % 2, HP + j, :], start=True, stop=True)
                    ins.then_inc(at_done, 1)

            def outputs(i, r):
                pe.wait_ge(masked, 4 * i + 2 * r + 2)
                for j in range(3 * r, 3 * r + 3):
                    pe.matmul(banks[7][:, 2 * E1 * j:2 * E1 * (j + 1)], qkT[:, i % 2, HP + j, :], st[:, j, :], start=True,
                              stop=False, skip_group_check=True)
                    for h in (2 * j, 2 * j + 1):
                        ins = pe.matmul(banks[7][:, E1 * h:E1 * (h + 1)], am[:, h, :], a.v1[:, i, h, :], start=False,
                                        stop=True, skip_group_check=True)
                return ins

            pe.wait_ge(padded, 5)
            logits(0)
            logits(1)
            turn(0)
            for i in range(NT):
                products(i, 0)
                if i + 1 < NT:
                    turn(i + 1)
                products(i, 1)
                if i + 2 < NT:
                    logits(i + 2)
                if i:
                    pe.wait_ge(state_ready, 2 * i)
                    pe.wait_ge(o_ready, i)
                outputs(i, 0)
                for j in range(HP):
                    pe.matmul(banks[7][:, SC + 2 * E1 * j:SC + 2 * E1 * (j + 1)],
                              kp[:, i % 3, 2 * j:2 * j + 2, :].rearrange("p h m -> p (h m)"),
                              a.v1[:, i, 2 * j:2 * j + 2, :].rearrange("p h e -> p (h e)"), start=True, stop=True)
                outputs(i, 1).then_inc(out_done, 1)


def attn_output(nc, g, a):
    oT_done, oT_ready, wo_done, xa_ready = sems(nc, g, "oT_done oT_ready wo_done xa_ready")
    with ExitStack() as local:
        oT = local.enter_context(nc.sbuf_tensor("o_T", [DP, KD, L], F32))
        banks = [local.enter_context(nc.psum_tensor(f"ob{i}", [P, CH], F32)) for i in range(8)]
        block = local.enter_context(nc.Block())

        @block.tensor
        def _(pe):
            for c in range(NCH):
                for k in range(KD):
                    if c >= 2:
                        pe.wait_ge(oT_ready, KD * (c - 2) + k + 1)
                    transpose_rows(pe, g, banks, a.o, c, k, oT_done)
            for i in range(NT):
                pe.wait_ge(oT_ready, KD * (i // TPC + 1))
                if i >= 4:
                    pe.wait_ge(xa_ready, i - 3)
                for k in range(KD):
                    ins = pe.matmul(banks[4 + i % 4][:, 0:D], oT[:, k, i * P:(i + 1) * P], a.w_o[:, k, :],
                                    start=(k == 0), stop=(k == KD - 1))
                ins.then_inc(wo_done, 1)

        @block.scalar
        def _(act):
            for c in range(NCH):
                for k in range(KD):
                    act.wait_ge(oT_done, KD * c + k + 1)
                    act.activation(oT[:, k, c * CH:(c + 1) * CH], banks[(c % 2) * KD + k][0:DP, :],
                                   ACT.Copy).then_inc(oT_ready, 1)

        @block.vector
        def _(dve):
            for i in range(NT):
                dve.wait_ge(wo_done, i + 1)
                dve.tensor_tensor(a.xa[:, i, :], a.xa[:, i, :], banks[4 + i % 4][:, 0:D], ALU.add).then_inc(xa_ready, 1)
            dve.wait_ge(xa_ready, NT)


def attn_mlp(nc, g, a):
    w_in, tr_done, hT_ready, up_done, gelu_ready, down_done, biased, added = sems(
        nc, g, "mlp_w_in mlp_transposed mlp_hT_ready mlp_up_done gelu_ready mlp_down_done mlp_biased mlp_added")
    with ExitStack() as local, nc.allow_non_contiguous_dma(reason="small weights"):
        def sb(name, shape, dt=F32):
            return local.enter_context(nc.sbuf_tensor(name, shape, dt))
        hT = sb("mlp_hT", [DP, KD, L])
        gT = sb("gelu_T", [P, MF, L])
        w1 = sb("mlp_w1", [DP, KD, FF])
        w2 = sb("mlp_w2", [P, MF, D])
        gb = sb("ln2_gb", [DP, 2, KD])
        b1 = sb("mlp_b1", [P, MF])
        b2 = sb("mlp_b2_rows", [P, D])
        banks = [local.enter_context(nc.psum_tensor(f"mb{i}", [P, CH], F32)) for i in range(8)]
        block = local.enter_context(nc.Block())
        I = g.attn
        NW = 16 * 6

        @block.sync
        def _(sp):
            for dst, src in ((w1[:, :, :], ks(I["W1"])), (w2[:, :, :], I["W2"].rearrange("(m p) n -> p m n", p=P)),
                             (gb[:, 0, :], col(I["ln2_g"], DP)), (gb[:, 1, :], col(I["ln2_b"], DP)),
                             (b1[:, :], col(I["b1"], P)), (b2[:, :], I["b2"].partition_broadcast(P))):
                sp.dma_start(dst, src).then_inc(w_in, 16)

        @block.gpsimd
        def _(pool):
            pool.wait_ge(w_in, NW)
            for i in range(NT):
                pool.tensor_tensor(a.xa[:, i, :], a.xa[:, i, :], b2[:, :], ALU.add).then_inc(biased, 1)
                pool.wait_ge(biased, 2 * i + 1)
                pool.tensor_tensor(g.x[:, i, :], g.x[:, i, :], a.xa[:, i, :], ALU.add).then_inc(biased, 1)

        @block.tensor
        def _(pe):
            for c in range(NCH):
                for k in range(KD):
                    if c >= 2:
                        pe.wait_ge(hT_ready, KD * (c - 2) + k + 1)
                    transpose_rows(pe, g, banks, a.xs, c, k, tr_done)
            pe.wait_ge(w_in, NW)
            for c in range(NCH):
                pe.wait_ge(hT_ready, KD * (c + 1))
                for m in range(MF):
                    j = c * MF + m
                    if j >= 2:
                        pe.wait_ge(gelu_ready, j - 1)
                    for k in range(KD):
                        ins = pe.matmul(banks[4 + j % 2][:, :], w1[:, k, m * P:(m + 1) * P],
                                        hT[:, k, c * CH:(c + 1) * CH], start=(k == 0), stop=(k == KD - 1))
                    ins.then_inc(up_done, 1)
                pe.wait_ge(gelu_ready, MF * (c + 1))
                for i in range(c * TPC, (c + 1) * TPC):
                    if i >= 2:
                        pe.wait_ge(added, i - 1)
                    for m in range(MF):
                        ins = pe.matmul(banks[6 + i % 2][:, 0:D], gT[:, m, i * P:(i + 1) * P], w2[:, m, :],
                                        start=(m == 0), stop=(m == MF - 1))
                    ins.then_inc(down_done, 1)

        @block.scalar
        def _(act):
            act.wait_ge(w_in, NW)
            for c in range(NCH):
                for k in range(KD):
                    act.wait_ge(tr_done, KD * c + k + 1)
                    act.activation(hT[:, k, c * CH:(c + 1) * CH], banks[(c % 2) * KD + k][0:DP, :], ACT.Identity,
                                   scale=gb[:, 0, k:k + 1], bias=gb[:, 1, k:k + 1]).then_inc(hT_ready, 1)
            for j in range(NCH * MF):
                c, m = j // MF, j % MF
                act.wait_ge(up_done, j + 1)
                act.activation(gT[:, m, c * CH:(c + 1) * CH], banks[4 + j % 2][:, :], ACT.Gelu,
                               bias=b1[:, m:m + 1]).then_inc(gelu_ready, 1)

        @block.vector
        def _(dve):
            for i in range(NT):
                dve.wait_ge(down_done, i + 1)
                dve.wait_ge(biased, 2 * (i + 1))
                dve.tensor_tensor(g.x[:, i, :], g.x[:, i, :], banks[6 + i % 2][:, 0:D], ALU.add).then_inc(added, 1)
            dve.wait_ge(added, NT)


def moe_logits(nc, g, e):
    (phi_in, phi_turned, phi_ready, square_ready, norm_step, phiT_ready, x_turned, xT_ready, lg_done, lg_ready,
     rmax_ready, cmax_step, cmax_turned, cmax_col, cmax_diag, cmax_rep, cmax_ready, wT_turned, wT_ready) = sems(
         nc, g, " ".join("moe_" + n for n in (
             "phi_in phi_turned phi_ready square_ready norm_step phiT_ready x_turned xT_ready logits_done "
             "logits_ready rmax_ready cmax_step cmax_turned cmax_col cmax_diag cmax_replicated cmax_ready "
             "ln_turned ln_ready").split()))
    with ExitStack() as local, nc.allow_non_contiguous_dma(reason="small weights"):
        def sb(name, shape, dt=F32):
            return local.enter_context(nc.sbuf_tensor(name, shape, dt))
        phi = e.w_place[:, 0:ST * D].rearrange("p (a d) -> p a d", d=D)
        n0 = ST * D
        phiT, sq = (e.w_place[0:DP, n0 + v * KD * S:n0 + (v + 1) * KD * S].rearrange("p (k s) -> p k s", k=KD)
                    for v in range(2))
        n0 += 2 * KD * S
        xT = e.w_place[0:DP, n0:n0 + KD * L].rearrange("p (k t) -> p k t", k=KD)
        rn = sb("phi_norm", [DP, KD, SL])
        cm = sb("tile_cmax", [P, S])
        cc = sb("cmax_cols", [P, ST])
        dg = sb("cmax_diag", [P, ST, P])
        lng = sb("expert_ln", [NE, 2, D])
        banks = [local.enter_context(nc.psum_tensor(f"eb{i}", [P, CH], F32)) for i in range(8)]
        block = local.enter_context(nc.Block())
        I = g.ffn

        @block.sync
        def _(sp):
            sp.dma_start(phi[:, :, :], I["phi"].rearrange("(a b) q d -> (b q) a d", b=EG)).then_inc(phi_in, 16)
            sp.dma_start(lng[:, 0, :], I["ln_g"]).then_inc(phi_in, 16)
            sp.dma_start(lng[:, 1, :], I["ln_b"]).then_inc(phi_in, 16)
            load_up(sp, g, e, 0)
            load_down(sp, g, e, 0)

        @block.tensor
        def _(pe):
            pe.wait_ge(phi_in, 48)
            for k in range(KD):
                for f in range(2):
                    for s in range(ST // 2):
                        ins = pe.transpose(banks[2 * k + f][0:DP, s * P:(s + 1) * P],
                                           phi[:, f * ST // 2 + s, k * DP:(k + 1) * DP], g.ident[:, :])
                    ins.then_inc(phi_turned, 1)
            for v in range(2):
                for k in range(KD):
                    ins = pe.transpose(banks[4][0:DP, (2 * v + k) * NE:(2 * v + k + 1) * NE],
                                       lng[:, v, k * DP:(k + 1) * DP], g.ident[0:NE, 0:NE])
            ins.then_inc(wT_turned, 1)
            pe.wait_ge(square_ready, 2 * KD)
            pe.wait_ge(phi_ready, 2 * KD)
            for c in range(NCH):
                for k in range(KD):
                    if c >= 2:
                        pe.wait_ge(xT_ready, KD * (c - 2) + k + 1)
                    transpose_rows(pe, g, banks, e.xm, c, k, x_turned)
            pe.wait_ge(phiT_ready, KD)
            pe.wait_ge(wT_ready, 1)
            for j in range(2 * NT):
                i, f = j // 2, j % 2
                pe.wait_ge(xT_ready, KD * (i // TPC + 1))
                if j >= 4:
                    pe.wait_ge(lg_ready, j - 3)
                for k in range(KD):
                    ins = pe.matmul(banks[4 + j % 4][:, :], xT[:, k, i * P:(i + 1) * P],
                                    phiT[:, k, f * CH:(f + 1) * CH], start=(k == 0), stop=(k == KD - 1))
                ins.then_inc(lg_done, 1)
            pe.wait_ge(cmax_step, NT)
            for s in range(ST):
                ins = pe.transpose(banks[s // 4][:, (s % 4) * P:(s % 4 + 1) * P], cm[:, s * P:(s + 1) * P], g.ident[:, :])
            ins.then_inc(cmax_turned, 1)
            for s in range(ST):
                pe.wait_ge(cmax_diag, s + 1)
                ins = pe.matmul(banks[2 + s // 4][:, (s % 4) * P:(s % 4 + 1) * P], g.ones[:, :], dg[:, s, :],
                                start=True, stop=True)
            ins.then_inc(cmax_rep, 1)

        @block.scalar
        def _(act):
            for k in range(KD):
                for f in range(2):
                    act.wait_ge(phi_turned, 2 * k + f + 1)
                    src = banks[2 * k + f][0:DP, :]
                    act.activation(sq[:, k, f * CH:(f + 1) * CH], src, ACT.Square).then_inc(square_ready, 1)
                    act.activation(phiT[:, k, f * CH:(f + 1) * CH], src, ACT.Copy).then_inc(phi_ready, 1)
            act.wait_ge(wT_turned, 1)
            act.activation(e.lnT[:, :, :, :], banks[4][0:DP, 0:4 * NE].rearrange("p (v k n) -> p v k n", v=2, k=KD),
                           ACT.Copy).then_inc(wT_ready, 1)
            act.wait_ge(norm_step, KD + 1)
            act.activation(rn[:, :, :], rn[:, :, :], ACT.Sqrt).then_inc(norm_step, 1)
            for c in range(NCH):
                for k in range(KD):
                    act.wait_ge(x_turned, KD * c + k + 1)
                    act.activation(xT[:, k, c * CH:(c + 1) * CH], banks[(c % 2) * KD + k][0:DP, :],
                                   ACT.Copy).then_inc(xT_ready, 1)
            for j in range(2 * NT):
                act.wait_ge(lg_done, j + 1)
                act.activation(e.lg[:, j // 2, (j % 2) * CH:(j % 2 + 1) * CH], banks[4 + j % 4][:, :],
                               ACT.Copy).then_inc(lg_ready, 1)
            act.wait_ge(cmax_rep, 1)
            for f in range(2):
                act.activation(e.cmax[:, f * CH:(f + 1) * CH], banks[2 + f][:, :], ACT.Copy).then_inc(cmax_ready, 1)

        @block.vector
        def _(dve):
            dve.wait_ge(square_ready, 2 * KD)
            for k in range(KD):
                dve.tensor_reduce(rn[:, k, :], sq[:, k, :].rearrange("p (n q) -> p q n", q=SL), AX.X,
                                  ALU.add).then_inc(norm_step, 1)
            dve.wait_ge(norm_step, KD)
            dve.tensor_scalar(rn[:, :, :], rn[:, :, :], 1e-6, None, ALU.add).then_inc(norm_step, 1)
            dve.wait_ge(norm_step, KD + 2)
            dve.reciprocal(rn[:, :, :], rn[:, :, :]).then_inc(norm_step, 1)
            dve.wait_ge(norm_step, KD + 3)
            dve.wait_ge(phi_ready, 2 * KD)
            for k in range(KD):
                v = phiT[:, k, :].rearrange("p (n q) -> p n q", q=SL)
                dve.tensor_tensor(v, v, rn[:, k, :].unsqueeze(1).broadcast_to([DP, NE, SL]),
                                  ALU.mult).then_inc(phiT_ready, 1)
            for i in range(NT):
                dve.wait_ge(lg_ready, 2 * (i + 1))
                dve.tensor_reduce(e.rmax[:, i:i + 1], e.lg[:, i, :], AX.X, ALU.max,
                                  negate=True).then_inc(rmax_ready, 1)
                if i:
                    dve.wait_ge(cmax_step, i)
                    dve.tensor_tensor(cm[:, :], cm[:, :], e.lg[:, i, :], ALU.max).then_inc(cmax_step, 1)
                else:
                    dve.tensor_copy(cm[:, :], e.lg[:, i, :]).then_inc(cmax_step, 1)
            dve.wait_ge(cmax_turned, 1)
            for f in range(2):
                dve.tensor_reduce(cc[:, 4 * f:4 * f + 4], banks[f][:, :].rearrange("p (s t) -> p s t", t=P), AX.X,
                                  ALU.max).then_inc(cmax_col, 1)
            dve.wait_ge(cmax_col, 2)
            for s in range(ST):
                dve.tensor_scalar(dg[:, s, :], g.ident[:, :], cc[:, s:s + 1], None, ALU.mult).then_inc(cmax_diag, 1)
            dve.wait_ge(cmax_ready, 2)
            dve.wait_ge(rmax_ready, NT)


def moe_gather_slots(nc, g, e):
    arg_ready, exp_ready, used, sum_done, recip, rows_ready, c_exp = sems(
        nc, g, "slot_arg_ready slot_exp_ready slot_exp_used slot_sum_done slot_recip slot_rows_ready combine_exp")
    with ExitStack() as local:
        def sb(name, shape, dt=F32):
            return local.enter_context(nc.sbuf_tensor(name, shape, dt))
        ed = sb("dispatch", [P, 3, S])
        rc = sb("dispatch_recip", [P, ST])
        banks = [local.enter_context(nc.psum_tensor(f"db{i}", [P, CH], F32)) for i in range(4)]
        block = local.enter_context(nc.Block())
        D1 = D + 1

        @block.sync
        def _(sp):
            load_up(sp, g, e, 1)
            load_down(sp, g, e, 1)

        @block.vector
        def _(dve):
            for i in range(NT):
                if i >= 3:
                    dve.wait_ge(used, i - 2)
                dve.tensor_tensor(ed[:, i % 3, :], e.lg[:, i, :], e.cmax[:, :], ALU.subtract).then_inc(arg_ready, 1)
            dve.wait_ge(sum_done, 1)
            for s in range(ST):
                b = banks[s // 2][:, (s % 2) * D1:(s % 2 + 1) * D1]
                dve.reciprocal(rc[:, s:s + 1], b[:, D:D1]).then_inc(recip, 1)
            for s in range(ST):
                b = banks[s // 2][:, (s % 2) * D1:(s % 2 + 1) * D1]
                dve.wait_ge(recip, s + 1)
                dve.tensor_scalar(e.xs[:, s, :], b[:, 0:D], rc[:, s:s + 1], None, ALU.mult).then_inc(rows_ready, 1)
            dve.wait_ge(rows_ready, ST)

        @block.scalar
        def _(act):
            for i in range(NT):
                act.wait_ge(arg_ready, i + 1)
                act.activation(ed[:, i % 3, :], ed[:, i % 3, :], ACT.Exp).then_inc(exp_ready, 1)
                act.activation(e.lg[:, i, :], e.lg[:, i, :], ACT.Exp, bias=e.rmax[:, i:i + 1],
                               accum_out=e.csum[:, i:i + 1]).then_inc(c_exp, 1)
            act.wait_ge(c_exp, NT)

        @block.tensor
        def _(pe):
            for i in range(NT):
                pe.wait_ge(exp_ready, i + 1)
                for s in range(ST):
                    ins = pe.matmul(banks[s // 2][:, (s % 2) * D1:(s % 2 + 1) * D1], ed[:, i % 3, s * P:(s + 1) * P],
                                    e.xm[:, i, :], start=(i == 0 and s % 2 == 0), stop=(i == NT - 1),
                                    skip_group_check=True)
                ins.then_inc(used, 1)
            pe.matmul(banks[3][0:1, 2 * D1:2 * D1 + 2], g.ident[:, 0:1], g.ident[:, 0:2], start=False, stop=True,
                      skip_group_check=True).then_inc(sum_done, 1)


def load_up(sp, g, e, t):
    for q in range(PR):
        n = EG * t + 2 * q
        sp.dma_start(e.w1[t % 2][:, q], g.ffn["w1"][n:n + 2].rearrange("e (k p) h -> p e k h", p=DP)) \
          .then_inc(e.w1_in[t % 2], 16)


def load_down(sp, g, e, t):
    for q in range(PR):
        n = EG * t + 2 * q
        sp.dma_start(e.w2[t % 2][:, q], g.ffn["w2"][n:n + 2].rearrange("e (p m) d -> p e m d", m=MH)) \
          .then_inc(e.w2_in[t % 2], 16)


def moe_experts(nc, g, e):
    (zeroed, turned, scaled, slots_ready, up_done, gelu_ready, h_turned, hT_ready, down_done, ys_ready,
     c_turned, c_ready, y_done, c_recip, added, s_out) = sems(nc, g, " ".join("ex_" + n for n in (
         "zeroed slots_turned slots_scaled slots_ready up_done gelu_ready h_turned hT_ready "
         "down_done results_ready combine_turned combine_ready y_done combine_recip added "
         "rows_out").split()))
    b1_in = sems(nc, g, "ex_b1_in_even ex_b1_in_odd")
    b2_in = sems(nc, g, "ex_b2_in_even ex_b2_in_odd")
    with ExitStack() as local, nc.allow_non_contiguous_dma(reason="small weights"):
        def sb(name, shape, dt=F32):
            return local.enter_context(nc.sbuf_tensor(name, shape, dt))
        w1, w2 = e.w1, e.w2
        b1 = sb("ex_b1", [EG, 2, HE])
        b2 = sb("ex_b2", [EG, 2, D])
        xT = [sb(f"slots_T{v}", [DP, KD, S]) for v in range(2)]
        tmp = sb("slots_scaled", [DP, 2, CH])
        hg = sb("gelu_rows", [P, 2, HE])
        hT = [sb(f"gelu_T{v}", [P, MH, P]) for v in range(2)]
        ys = sb("slot_results", [P, ST, D])
        rr = sb("combine_recip", [P, NT])
        banks = [local.enter_context(nc.psum_tensor(f"xb{i}", [P, CH], F32)) for i in range(8)]
        block = local.enter_context(nc.Block())
        I = g.ffn
        PARTS = ((0, ST // 2), (ST // 2, ST))
        order = [(i, f) for f in range(len(PARTS)) for i in range(NT)]
        cuts = (0, 5, 10, 14)
        sums = {5 + k: order[cuts[k]:cuts[k + 1]] for k in range(3)}
        sums[ST] = order[cuts[-1]:]

        @block.sync
        def _(sp):
            for t in range(ST):
                if t >= 2:
                    sp.wait_ge(up_done, t - 1)
                sp.dma_start(b1[:, t % 2, :], I["b1"][EG * t:EG * (t + 1), :]).then_inc(b1_in[t % 2], 16)
                if t >= 2:
                    load_up(sp, g, e, t)
                    sp.wait_ge(down_done, t - 1)
                sp.dma_start(b2[:, t % 2, :], I["b2"][EG * t:EG * (t + 1), :]).then_inc(b2_in[t % 2], 16)
                if t >= 2:
                    load_down(sp, g, e, t)
            for i in range(NT):
                sp.wait_ge(added, (len(PARTS) - 1) * NT + i + 1)
                sp.dma_start(g.out[0, i * P:(i + 1) * P, :], g.x[:, i, :]).then_inc(s_out, 16)
            sp.wait_ge(s_out, 16 * NT)

        @block.gpsimd
        def _(pool):
            for v in range(2):
                pool.memset(xT[v][:, :, :], 0.0).then_inc(zeroed, 1)
                pool.memset(hT[v][:, :, :], 0.0).then_inc(zeroed, 1)

        @block.tensor
        def _(pe):
            def combine_transposes(i):
                if i:
                    pe.wait_ge(c_ready, 2 * i)
                for s in range(ST):
                    ins = pe.transpose(banks[6 + s // 4][:, (s % 4) * P:(s % 4 + 1) * P],
                                       e.lg[:, i, s * P:(s + 1) * P], g.ident[:, :])
                ins.then_inc(c_turned, 1)

            def combine(i, f):
                n = order.index((i, f))
                s0, s1 = PARTS[f]
                pe.wait_ge(c_ready, 2 * (i + 1))
                pe.wait_ge(ys_ready, s1)
                if n >= 2:
                    pe.wait_ge(added, n - 1)
                for s in range(s0, s1):
                    ins = pe.matmul(banks[1 + 4 * (n % 2)][:, 0:D], e.lg[:, i, s * P:(s + 1) * P], ys[:, s, :],
                                    start=(s == s0), stop=(s == s1 - 1))
                ins.then_inc(y_done, 1)

            for k in range(KD):
                for f in range(2):
                    for s in range(ST // 2):
                        ins = pe.transpose(banks[2 * k + f][0:DP, s * P:(s + 1) * P],
                                           e.xs[:, f * ST // 2 + s, k * DP:(k + 1) * DP], g.ident[:, :])
                    ins.then_inc(turned, 1)
            pe.wait_ge(zeroed, 4)
            pe.wait_ge(slots_ready, 4 * KD)
            for t in range(ST):
                for i, f in sums.get(t, ()):
                    combine(i, f)
                up, down = banks[0], banks[2 + t % 2]
                pe.wait_ge(b1_in[t % 2], 16 * (t // 2 + 1))
                pe.matmul(up[:, 0:HE], g.slot_of[:, :], b1[:, t % 2, :], start=True, stop=False, skip_group_check=True)
                pe.wait_ge(e.w1_in[t % 2], 16 * PR * (t // 2 + 1))
                for v in range(2):
                    for k in range(KD):
                        for q in range(PR):
                            ins = pe.matmul(up[32 * q:32 * q + 32, 0:HE],
                                            xT[v][:, k, t * P + 32 * q:t * P + 32 * q + 32],
                                            w1[t % 2][:, q, v, k, :], start=False,
                                            stop=(v == 1 and k == KD - 1), skip_group_check=True)
                ins.then_inc(up_done, 1)
                combine_transposes(2 * t)
                pe.wait_ge(gelu_ready, t + 1)
                if t:
                    pe.wait_ge(hT_ready, 2 * t)
                for m in range(MH):
                    ins = pe.transpose(banks[4][:, m * P:(m + 1) * P], hg[:, t % 2, m:HE:MH], g.ident[:, :])
                ins.then_inc(h_turned, 1)
                combine_transposes(2 * t + 1)
                pe.wait_ge(hT_ready, 2 * (t + 1))
                if t >= 2:
                    pe.wait_ge(ys_ready, t - 1)
                pe.wait_ge(b2_in[t % 2], 16 * (t // 2 + 1))
                pe.wait_ge(e.w2_in[t % 2], 16 * PR * (t // 2 + 1))
                pe.matmul(down[:, 0:D], g.slot_of[:, :], b2[:, t % 2, :], start=True, stop=False, skip_group_check=True)
                for v in range(2):
                    for m in range(MH):
                        for q in range(PR):
                            ins = pe.matmul(down[32 * q:32 * q + 32, 0:D], hT[v][:, m, 32 * q:32 * q + 32],
                                            w2[t % 2][:, q, v, m, :], start=False,
                                            stop=(v == 1 and m == MH - 1), skip_group_check=True)
                ins.then_inc(down_done, 1)
            for i, f in sums[ST]:
                combine(i, f)

        @block.scalar
        def _(act):
            act.preload_act_table(ACT.Gelu)
            for t in range(ST):
                act.wait_ge(up_done, t + 1)
                if t >= 2:
                    act.wait_ge(h_turned, t - 1)
                act.activation(hg[:, t % 2, :], banks[0][:, 0:HE], ACT.Gelu).then_inc(gelu_ready, 1)
                act.wait_ge(down_done, t + 1)
                act.activation(ys[:, t, :], banks[2 + t % 2][:, 0:D], ACT.Copy).then_inc(ys_ready, 1)

        @block.vector
        def _(dve):
            dve.wait_ge(zeroed, 4)
            n = 0
            for k in range(KD):
                for f in range(2):
                    dve.wait_ge(turned, 2 * k + f + 1)
                    if n >= 2:
                        dve.wait_ge(slots_ready, 2 * (n - 1))
                    tv = tmp[:, n % 2, :].rearrange("p (n q) -> p n q", q=SL)
                    gn = slice(f * NE // 2, (f + 1) * NE // 2)
                    dve.tensor_tensor(tv, banks[2 * k + f][0:DP, :].rearrange("p (n q) -> p n q", q=SL),
                                      e.lnT[:, 0, k, gn].unsqueeze(2).broadcast_to([DP, NE // 2, SL]),
                                      ALU.mult).then_inc(scaled, 1)
                    dve.wait_ge(scaled, n + 1)
                    for v in range(2):
                        xv = xT[v][:, k, f * CH:(f + 1) * CH].rearrange("p (n q) -> p n q", q=SL)[:, v:NE // 2:2, :]
                        bn = e.lnT[:, 1, k, f * NE // 2 + v:(f + 1) * NE // 2:2]
                        dve.tensor_tensor(xv, tv[:, v:NE // 2:2, :],
                                          bn.unsqueeze(2).broadcast_to([DP, NE // 4, SL]),
                                          ALU.add).then_inc(slots_ready, 1)
                    n += 1

            def add(i, f):
                n = order.index((i, f))
                dve.wait_ge(y_done, n + 1)
                if f:
                    dve.wait_ge(added, order.index((i, f - 1)) + 1)
                dve.scalar_tensor_tensor(out=g.x[:, i, :], in0=banks[1 + 4 * (n % 2)][:, 0:D], scalar=rr[:, i:i + 1],
                                         in1=g.x[:, i, :], op0=ALU.mult, op1=ALU.add).then_inc(added, 1)

            def combine_copy(i):
                dve.wait_ge(c_turned, i + 1)
                for f in range(2):
                    dve.tensor_copy(e.lg[:, i, f * CH:(f + 1) * CH], banks[6 + f][:, :]).then_inc(c_ready, 1)

            for t in range(ST):
                for i, f in sums.get(t, ()):
                    add(i, f)
                combine_copy(2 * t)
                dve.wait_ge(h_turned, t + 1)
                if t:
                    dve.wait_ge(down_done, t)
                src = banks[4][:, 0:MH * P].rearrange("p (m q v s) -> p m q v s", m=MH, v=2, s=SL)
                for v in range(2):
                    for_v = hT[v][:, :, :].rearrange("p m (q v s) -> p m q v s", v=2, s=SL)
                    dve.tensor_copy(for_v[:, :, :, v, :], src[:, :, :, v, :]).then_inc(hT_ready, 1)
                combine_copy(2 * t + 1)
                if t == 0:
                    dve.reciprocal(rr[:, :], e.csum[:, :]).then_inc(c_recip, 1)
                    dve.wait_ge(c_recip, 1)
            for i, f in sums[ST]:
                add(i, f)


def store_out(nc, g, src):
    s_out, = sems(nc, g, "rows_out")
    with nc.Block() as block:
        @block.sync
        def _(sp):
            sp.dma_start(g.out.rearrange("a (i p) d -> p (a i) d", p=P), src[:, :, :]).then_inc(s_out, 16)
            sp.wait_ge(s_out, 16)


def lm_tower(nc, ins, out, upto=9):
    g = Core()
    g.live = []
    g.out = out
    g.ids = ins["x"]
    g.tok = {k[7:]: v for k, v in ins.items() if k.startswith("L0_tok_")}
    g.attn = {k[8:]: v for k, v in ins.items() if k.startswith("L0_attn_")}
    g.ffn = {k[7:]: v for k, v in ins.items() if k.startswith("L0_ffn_")}
    g.ctx = ExitStack()
    with g.ctx as ctx:
        def sb(name, shape, dt=F32):
            return ctx.enter_context(nc.sbuf_tensor(name, shape, dt))
        g.x = sb("x_rows", [P, NT, D])
        g.ident = sb("ident", [P, P])
        g.causal = sb("causal", [P, P])
        g.ones = sb("ones", [P, P])
        g.slot_of = sb("slot_of", [EG, P])
        g.head_of = sb("head_of", [DP, HK])
        with ExitStack() as mamba:
            def mb(name, shape, dt=F32):
                return mamba.enter_context(nc.sbuf_tensor(name, shape, dt))
            g.sel = mb("sel", [3 * NX, NX, P], BF16)
            g.w_in = mb("w_in", [DP, KD, 2 * DI])
            g.norm_w_c = mb("norm_w_c", [DP, NL, KD])
            g.conv_wc = mb("conv_wc", [P, NL, MI, TAPS])
            g.conv_bc = mb("conv_bc", [P, NL, MI])
            g.w_x = mb("w_x", [P, NL, MI, NX + RK])
            g.w_dt = mb("w_dt", [RK, NL, DI])
            g.dt_bc = mb("dt_bc", [P, NL, MI])
            g.a_neg = mb("a_neg", [P, NL, MI, NS])
            g.d_c = mb("d_c", [P, NL, MI])
            g.w_out = mb("w_out", [P, NL, MI, D])
            g.xr = mb("xr", [P, MI, L + TAPS - 1])
            g.sres = mb("sres", [P, MI, L])
            g.u = mb("u", [P, MI, L])
            g.delta = mb("delta", [P, MI, L])
            g.du = mb("du", [P, MI, L])
            g.bcp = mb("bcp", [3 * NX, L + CH], BF16)
            load_and_gather(nc, g)
            for l in range(NL if upto > 1 else upto):
                mamba_front(nc, g, l)
                mamba_scan(nc, g, l)
                retire_semaphores(nc, g)
        if upto > 2:
            with ExitStack() as attn:
                a = Core()
                def ab(name, shape, dt=F32):
                    return attn.enter_context(nc.sbuf_tensor(name, shape, dt))
                a.xa = ab("xa", [P, NT, D])
                a.xs = ab("xs_attn", [P, NT, D])
                a.w_o = ab("w_o", [DP, KD, D])
                a.proj_blocks = ab("proj_blocks", [DP, HK, M])
                a.neg_kmax = ab("neg_kmax", [P, 1])
                normalize_rows(nc, g, "norm0", g.x, a.xa, 1e-5)
                with ExitStack() as qkv:
                    def qb(name, shape, dt=F32):
                        return qkv.enter_context(nc.sbuf_tensor(name, shape, dt))
                    a.qk = qb("qk_T", [DP, 2, KD, L])
                    a.qk2 = qb("qk_squares_T", [DP, 2, KD, L])
                    a.v1 = qb("v_rows", [P, NT, H, DH + 1])
                    with nc.Block() as block:
                        @block.gpsimd
                        def _(pool):
                            pool.memset(a.proj_blocks[:, :, :], 0.0)
                    normalize_rows(nc, g, "norm1", a.xa, a.xs, 1e-5)
                    attn_project(nc, g, a)
                    a.kdd = qb("k_dd", [P, NT, KD, HK, M])
                    attn_key_logits(nc, g, a)
                    a.o = a.xs
                    attention(nc, g, a)
                attn_output(nc, g, a)
                normalize_rows(nc, g, "norm2", a.xa, a.xs, 1e-5)
                attn_mlp(nc, g, a)
                retire_semaphores(nc, g)
        if upto > 3:
            with ExitStack() as moe:
                e = Core()
                def eb(name, shape, dt=F32):
                    return moe.enter_context(nc.sbuf_tensor(name, shape, dt))
                e.lg = eb("logits", [P, NT, S])
                e.rmax = eb("neg_rmax", [P, NT])
                e.csum = eb("combine_sum", [P, NT])
                e.lnT = eb("expert_ln_T", [DP, 2, KD, NE])
                e.xs = eb("slot_rows", [P, ST, D])
                w1 = eb("expert_w1", [DP, PR, 2, KD, HE])
                w2 = eb("expert_w2", [P, PR, 2, MH, D])
                e.w_place = eb("expert_w_odd", [P, W1C + W2C])
                e.w1 = (w1, e.w_place[0:DP, 0:W1C].rearrange("p (q v k h) -> p q v k h", q=PR, v=2, k=KD))
                e.w2 = (w2, e.w_place[:, W1C:W1C + W2C].rearrange("p (q v m d) -> p q v m d", q=PR, v=2, m=MH))
                e.w1_in = sems(nc, g, "expert_w1_in_even expert_w1_in_odd")
                e.w2_in = sems(nc, g, "expert_w2_in_even expert_w2_in_odd")
                with ExitStack() as rows:
                    e.xm = rows.enter_context(nc.sbuf_tensor("moe_rows", [P, NT, D + 1], F32))
                    e.cmax = rows.enter_context(nc.sbuf_tensor("cmax", [P, S], F32))
                    with nc.Block() as block:
                        @block.gpsimd
                        def _(pool):
                            pool.memset(e.xm[:, :, D:D + 1], 1.0)
                    normalize_rows(nc, g, "norm3", g.x, e.xm, 1e-5)
                    moe_logits(nc, g, e)
                    moe_gather_slots(nc, g, e)
                normalize_rows(nc, g, "norm4", e.xs, e.xs, 1e-5)
                moe_experts(nc, g, e)
        else:
            store_out(nc, g, g.x)


_INS = ["x"] + ["L0_tok_" + n for n in (
    "emb", "norm_w", "in_proj_w", "conv_w", "conv_b", "x_proj_w", "dt_proj_w", "dt_proj_b", "A_log", "D",
    "out_proj_w")] + ["L0_attn_" + n for n in (
        "ln1_g", "ln1_b", "Wq", "bq", "Wk", "bk", "Wv", "bv", "Wo", "bo", "proj", "ln2_g", "ln2_b", "W1", "b1",
        "W2", "b2")] + ["L0_ffn_" + n for n in ("phi", "ln_g", "ln_b", "w1", "b1", "w2", "b2")]


def kernel(**inputs):
    import numpy as _np
    import concourse.bacc as _bacc
    from concourse import mybir as _mybir
    from concourse.bass_utils import run_bass_kernel_spmd as _run

    nc = _bacc.Bacc("TRN2", target_bir_lowering=False, num_devices=1)
    arrays, ins = {}, {}
    for name in _INS:
        a = _np.ascontiguousarray(inputs[name])
        arrays[f"in_{name}_dram"] = a
        ins[name] = nc.dram_tensor(f"in_{name}_dram", a.shape, _mybir.dt.from_np(a.dtype), kind="ExternalInput").ap()
    out = nc.dram_tensor("out_0_dram", (1, L, D), _mybir.dt.float32, kind="ExternalOutput").ap()
    lm_tower(nc, ins, out)
    r = _run(nc, [arrays], core_ids=[0])
    return r.results[0]["out_0_dram"]
```

```python
from contextlib import ExitStack

import numpy as np

import concourse.bass as bass
from concourse import mybir

F32 = mybir.dt.float32
BF16 = mybir.dt.bfloat16
I32 = mybir.dt.int32
ALU = mybir.AluOpType
ACT = mybir.ActivationFunctionType
AX = mybir.AxisListType

P = 128
L = 2048
NT = L // P
D = 192
KD = 2
DP = D // KD
CH = 512
NCH = L // CH
TPC = CH // P
V = 8000
NL = 2
DI = 384
MI = DI // P
NS = 16
RK = 12
NX = 2 * NS
TAPS = 4
H = 12
DH = 16
HK = H // KD
M = 44
MP = 64
HP = H // 2
VE = 32
HQ = P // VE
HG = H // HQ
FF = 768
MF = FF // P
NE = 64
SL = 16
S = NE * SL
ST = S // P
EG = P // SL
HE = 384
MH = HE // P
PR = EG // 2
W1C = PR * 2 * KD * HE
W2C = PR * 2 * MH * D
A_LOG_MAX = 80.0
LN2 = 0.6931471


class Core:
    pass


def sems(nc, g, names):
    made = [nc.alloc_semaphore(name=n) for n in names.split()]
    g.live += made
    return made


def retire_semaphores(nc, g):
    nc.clear_and_free_semaphores(g.live)
    nc.all_engine_barrier()
    g.live = []


def ks(w):
    return w.rearrange("(k p) n -> p k n", p=DP)


def col(v, p):
    return v.rearrange("(k p) -> p k", p=p)


def load_and_gather(nc, g):
    s_ids, g.s_w, s_gather, s_cst, s_idx = sems(nc, g, "ids_in mamba_weights_in rows_in identity_made indices_made")
    with ExitStack() as local, nc.allow_non_contiguous_dma(reason="small weights"):
        ids = local.enter_context(nc.sbuf_tensor("ids", [P, NT], I32))
        wrap = local.enter_context(nc.sbuf_tensor("wrap", [P, NT], F32))
        idsf = local.enter_context(nc.sbuf_tensor("idsf", [P, NT], F32))
        idx = local.enter_context(nc.sbuf_tensor("idx", [P, NT], I32))
        block = local.enter_context(nc.Block())

        @block.sync
        def _(sp):
            sp.dma_start(ids[:, :], g.ids.rearrange("a (i p) -> p (a i)", p=P)).then_inc(s_ids, 16)
            sp.dma_start(g.w_in[:, :, :], ks(g.tok["in_proj_w"][0])).then_inc(g.s_w, 16)
            n = 16
            for l in range(NL):
                for dst, src in (
                    (g.norm_w_c[:, l, :], col(g.tok["norm_w"][l], DP)),
                    (g.conv_wc[:, l, :, :], g.tok["conv_w"][l].rearrange("(m p) a k -> p m (a k)", p=P)),
                    (g.conv_bc[:, l, :], col(g.tok["conv_b"][l], P)),
                    (g.w_x[:, l, :, 0:NX], g.tok["x_proj_w"][l].rearrange("(m p) n -> p m n", p=P)[:, :, RK:RK + NX]),
                    (g.w_x[:, l, :, NX:NX + RK], g.tok["x_proj_w"][l].rearrange("(m p) n -> p m n", p=P)[:, :, 0:RK]),
                    (g.w_dt[:, l, :], g.tok["dt_proj_w"][l]),
                    (g.dt_bc[:, l, :], col(g.tok["dt_proj_b"][l], P)),
                    (g.a_neg[:, l, :, :], g.tok["A_log"][l].rearrange("(m p) n -> p m n", p=P)),
                    (g.d_c[:, l, :], col(g.tok["D"][l], P)),
                    (g.w_out[:, l], g.tok["out_proj_w"][l].rearrange("(m p) n -> p m n", p=P)),
                ):
                    sp.dma_start(dst, src).then_inc(g.s_w, 16)
                    n += 16
            sp.wait_ge(s_gather, 16 * NT)
            sp.wait_ge(g.s_w, n)

        @block.vector
        def _(dve):
            dve.wait_ge(s_ids, 16)
            dve.tensor_scalar(wrap[:, :], ids[:, :], 0.0, float(V), ALU.is_lt, ALU.mult).then_inc(s_idx, 1)
            dve.wait_ge(s_idx, 1)
            dve.tensor_tensor(idsf[:, :], ids[:, :], wrap[:, :], ALU.add).then_inc(s_idx, 1)
            dve.wait_ge(s_idx, 2)
            dve.tensor_scalar(idx[:, :], idsf[:, :], 0.0, float(V - 1), ALU.max, ALU.min).then_inc(s_idx, 1)
            dve.wait_ge(g.s_w, g_total_w(g))
            dve.tensor_scalar(g.a_neg[:, :, :, :], g.a_neg[:, :, :, :], A_LOG_MAX, None, ALU.min).then_inc(s_idx, 1)
            dve.wait_ge(s_idx, 5)
            dve.tensor_scalar(g.a_neg[:, :, :, :], g.a_neg[:, :, :, :], -1.0, None, ALU.mult).then_inc(s_idx, 1)

        @block.scalar
        def _(act):
            act.wait_ge(s_idx, 4)
            act.activation(g.a_neg[:, :, :, :], g.a_neg[:, :, :, :], ACT.Exp).then_inc(s_idx, 1)

        @block.gpsimd
        def _(pool):
            pool.memset(g.ident[:, :], 0.0).then_inc(s_cst, 1)
            pool.wait_ge(s_cst, 1)
            pool.affine_select(out=g.ident[:, :], in_=g.ident[:, :], compare_op=ALU.not_equal, fill=1.0,
                               base=0, pattern=[[-1, P]], channel_multiplier=1).then_inc(s_cst, 1)
            pool.wait_ge(s_idx, 3)
            for i in range(NT):
                pool.indirect_dma_start(g.x[:, i, :], None, g.tok["emb"],
                                        bass.IndirectOffsetOnAxis(ap=idx[:, i:i + 1], axis=0)).then_inc(s_gather, 16)
            pool.wait_ge(s_cst, 2)


def make_constants(pool, g, made):
    pool.memset(g.sel[:, :, :], 0.0).then_inc(made, 1)
    pool.memset(g.bcp[:, L:L + CH], 0.0).then_inc(made, 1)
    pool.memset(g.causal[:, :], 1.0).then_inc(made, 1)
    pool.memset(g.ones[:, :], 1.0).then_inc(made, 1)
    pool.memset(g.slot_of[:, :], 1.0).then_inc(made, 1)
    pool.memset(g.head_of[:, :], 0.5).then_inc(made, 1)
    pool.wait_ge(made, 6)
    for a in range(3):
        pool.affine_select(out=g.sel[:, :, :], in_=g.sel[:, :, :], compare_op=ALU.not_equal, fill=1.0,
                           base=-NX * a, pattern=[[-1, NX], [0, P]], channel_multiplier=1).then_inc(made, 1)
        pool.wait_ge(made, 7 + a)
    pool.affine_select(out=g.causal[:, :], in_=g.causal[:, :], compare_op=ALU.is_ge, fill=0.0,
                       base=0, pattern=[[1, P]], channel_multiplier=-1).then_inc(made, 1)
    for out, n, a in ((g.head_of, HK, -DH), (g.slot_of, P, 1)):
        cm = 1 if a < 0 else -SL
        pool.affine_select(out=out[:, :], in_=out[:, :], compare_op=ALU.is_ge, fill=0.0,
                           base=0, pattern=[[a, n]], channel_multiplier=cm).then_inc(made, 1)
    pool.wait_ge(made, 12)
    for out, n, a in ((g.head_of, HK, DH), (g.slot_of, P, -1)):
        cm = -1 if a > 0 else SL
        pool.affine_select(out=out[:, :], in_=out[:, :], compare_op=ALU.is_ge, fill=0.0,
                           base=DH - 1, pattern=[[a, n]], channel_multiplier=cm).then_inc(made, 1)
    pool.wait_ge(made, 14)


def g_total_w(g):
    return 16 * (10 * NL + 1)


def mamba_front(nc, g, l):
    (sumsq, meansq, rms, rstd_done, xs_ready, tr_done, xT_ready, proj_done, xr_ready, res_ready, conv_step,
     conv_done, u_ready, xp_done, bc_ready, dtT_ready, split_step, dt_done, abs_done, exp_done, ln_done,
     sp_step, relu_done, delta_done, du_done, last_delta_done, last_du_done,
     constants_made) = sems(nc, g, " ".join(f"{n}{l}" for n in (
        "sumsq meansq rms rstd_done xs_ready transposed xT_ready projected xr_ready res_ready conv_step "
        "conv_done u_ready x_projected bc_ready dtT_ready split_step dt_projected abs_done exp_done ln_done "
        "softplus_step relu_done delta_done delta_u_done last_delta_done "
        "last_delta_u_done constants_made").split()))
    with ExitStack() as local:
        def sb(name, shape, dt=F32):
            return local.enter_context(nc.sbuf_tensor(f"{name}{l}", shape, dt))
        ss = sb("ss", [P, NT])
        rstd = sb("rstd", [P, NT])
        ax = sb("ax", [P, 2, MI, CH])
        dd = sb("dd", [P, 2, MI, CH])
        cv = sb("cv", [P, MI, CH])
        bcf = sb("bcf", [NX, 2, CH])
        mid = sb("mid", [NX, CH], BF16)
        dtT = sb("dtT", [RK, 2, CH])
        xs = g.delta[:, :, :].rearrange("p m t -> p (m t)")[:, 0:NT * D].rearrange("p (i d) -> p i d", d=D)
        xT = g.du[0:DP, :, :].rearrange("p m t -> p (m t)")[:, 0:KD * L].rearrange("p (k t) -> p k t", k=KD)
        banks = [local.enter_context(nc.psum_tensor(f"fb{l}_{i}", [P, CH], F32)) for i in range(8)]
        block = local.enter_context(nc.Block())

        def finish(engine, c, delta_done, du_done, n):
            cc = slice(c * CH, (c + 1) * CH)
            engine.tensor_tensor(g.delta[:, :, cc], g.delta[:, :, cc], dd[:, c % 2, :, :],
                                 ALU.add).then_inc(delta_done, 1)
            engine.wait_ge(delta_done, n)
            engine.tensor_tensor(g.du[:, :, cc], g.delta[:, :, cc], g.u[:, :, cc], ALU.mult).then_inc(du_done, 1)

        @block.gpsimd
        def _(pool):
            if l == 0:
                make_constants(pool, g, constants_made)
            for c in range(NCH - 1):
                pool.wait_ge(sp_step, 4 * (c + 1))
                pool.wait_ge(relu_done, MI * (c + 1))
                finish(pool, c, delta_done, du_done, c + 1)

        @block.scalar
        def _(act):
            for i in range(NT):
                act.activation(xs[:, i, :], g.x[:, i, :], ACT.Square, accum_out=ss[:, i:i + 1]).then_inc(sumsq, 1)
            act.wait_ge(meansq, 1)
            act.activation(ss[:, :], ss[:, :], ACT.Sqrt).then_inc(rms, 1)
            for c in range(NCH):
                for k in range(KD):
                    act.wait_ge(tr_done, KD * c + k + 1)
                    act.activation(xT[:, k, c * CH:(c + 1) * CH], banks[(c % 2) * KD + k][0:DP, :], ACT.Copy,
                                   scale=g.norm_w_c[:, l, k:k + 1]).then_inc(xT_ready, 1)
            for c in range(NCH):
                for m in range(MI):
                    j = c * 2 * MI + 2 * m + 1
                    act.wait_ge(proj_done, j + 1)
                    act.activation(g.sres[:, m, c * CH:(c + 1) * CH], banks[4 + j % 4][:, :],
                                   ACT.Silu).then_inc(res_ready, 1)
                for m in range(MI):
                    act.wait_ge(conv_done, MI * c + m + 1)
                    act.activation(g.u[:, m, c * CH:(c + 1) * CH], cv[:, m, :], ACT.Silu,
                                   bias=g.conv_bc[:, l, m:m + 1]).then_inc(u_ready, 1)
            for c in range(NCH):
                act.wait_ge(xp_done, c + 1)
                if c >= 2:
                    act.wait_ge(split_step, 5 * (c - 1))
                    act.wait_ge(dt_done, MI * (c - 1))
                act.activation(bcf[:, c % 2, :], banks[c % 2][0:NX, :], ACT.Copy).then_inc(bc_ready, 1)
                act.activation(dtT[:, c % 2, :], banks[c % 2][NX:NX + RK, :], ACT.Copy).then_inc(dtT_ready, 1)
                for m in range(MI):
                    j = MI * c + m
                    act.wait_ge(dt_done, j + 1)
                    if m == 0 and c >= 2:
                        act.wait_ge(sp_step, 4 * (c - 1))
                    act.activation(ax[:, c % 2, m, :], banks[2 + j % 4][:, :], ACT.Abs,
                                   bias=g.dt_bc[:, l, m:m + 1]).then_inc(abs_done, 1)
                act.wait_ge(abs_done, MI * (c + 1))
                act.activation(ax[:, c % 2, :, :], ax[:, c % 2, :, :], ACT.Exp, scale=-1.0).then_inc(exp_done, 1)
                act.wait_ge(exp_done, c + 1)
                if c >= 2:
                    act.wait_ge(delta_done, c - 1)
                act.activation(dd[:, c % 2, :, :], ax[:, c % 2, :, :], ACT.Ln, bias=1.0).then_inc(ln_done, 1)

        @block.vector
        def _(dve):
            dve.wait_ge(sumsq, NT)
            dve.tensor_scalar(ss[:, :], ss[:, :], 1.0 / D, 1e-5, ALU.mult, ALU.add).then_inc(meansq, 1)
            dve.wait_ge(rms, 1)
            dve.reciprocal(rstd[:, :], ss[:, :]).then_inc(rstd_done, 1)
            dve.wait_ge(rstd_done, 1)
            for i in range(NT):
                dve.tensor_scalar(xs[:, i, :], g.x[:, i, :], rstd[:, i:i + 1], None, ALU.mult).then_inc(xs_ready, 1)
            dve.memset(g.xr[:, :, 0:TAPS - 1], 0.0).then_inc(conv_step, 1)
            steps = 1
            for c in range(NCH):
                for m in range(MI):
                    j = c * 2 * MI + 2 * m
                    dve.wait_ge(proj_done, j + 1)
                    dve.tensor_copy(g.xr[:, m, TAPS - 1 + c * CH:TAPS - 1 + (c + 1) * CH],
                                    banks[4 + j % 4][:, :]).then_inc(xr_ready, 1)
                dve.wait_ge(xr_ready, MI * (c + 1))
                if c:
                    dve.wait_ge(u_ready, MI * c)
                for k in range(TAPS):
                    dve.wait_ge(conv_step, steps)
                    for m in range(MI):
                        src = g.xr[:, m, c * CH + k:c * CH + k + CH]
                        w = g.conv_wc[:, l, m, k:k + 1]
                        if k == 0:
                            ins = dve.tensor_scalar(cv[:, m, :], src, w, None, ALU.mult)
                        else:
                            ins = dve.scalar_tensor_tensor(out=cv[:, m, :], in0=src, scalar=w, in1=cv[:, m, :],
                                                           op0=ALU.mult, op1=ALU.add)
                        if k < TAPS - 1:
                            ins.then_inc(conv_step, 1)
                            steps += 1
                        else:
                            ins.then_inc(conv_done, 1)
            n = 0
            for c in range(NCH):
                cc = slice(c * CH, (c + 1) * CH)
                for m in range(MI):
                    j = MI * c + m
                    dve.wait_ge(abs_done, j + 1)
                    dve.tensor_scalar(g.delta[:, m, cc], banks[2 + j % 4][:, :], g.dt_bc[:, l, m:m + 1], 0.0,
                                      ALU.add, ALU.max).then_inc(relu_done, 1)
                dve.wait_ge(bc_ready, c + 1)
                b = bcf[:, c % 2, :]
                for out, i0, i1 in ((g.bcp[0:NX, cc], b, None), (b, b, g.bcp[0:NX, cc]),
                                    (mid[:, :], b, None), (g.bcp[NX:2 * NX, cc], mid[:, :], None),
                                    (g.bcp[2 * NX:3 * NX, cc], b, mid[:, :])):
                    if i1 is None:
                        ins = dve.tensor_copy(out, i0)
                    else:
                        ins = dve.tensor_tensor(out, i0, i1, ALU.subtract)
                    ins.then_inc(split_step, 1)
                    n += 1
                    dve.wait_ge(split_step, n)
                dve.wait_ge(ln_done, c + 1)
                e, ln = ax[:, c % 2, :, :], dd[:, c % 2, :, :]
                r = cv
                k0 = 4 * c
                dve.tensor_scalar(r[:, :, :], e, 1.0, -1.0, ALU.add, ALU.add).then_inc(sp_step, 1)
                dve.wait_ge(sp_step, k0 + 1)
                dve.tensor_tensor(r[:, :, :], e, r[:, :, :], ALU.subtract).then_inc(sp_step, 1)
                dve.wait_ge(sp_step, k0 + 2)
                dve.tensor_tensor(ln, r[:, :, :], ln, ALU.add).then_inc(sp_step, 1)
                dve.wait_ge(sp_step, k0 + 3)
                dve.scalar_tensor_tensor(out=ln, in0=e, scalar=LN2, in1=ln, op0=ALU.mult,
                                         op1=ALU.max).then_inc(sp_step, 1)
            dve.wait_ge(sp_step, 4 * NCH)
            finish(dve, NCH - 1, last_delta_done, last_du_done, 1)
            dve.wait_ge(last_du_done, 1)

        @block.tensor
        def _(pe):
            for c in range(NCH):
                pe.wait_ge(xs_ready, TPC * (c + 1))
                for k in range(KD):
                    if c >= 2:
                        pe.wait_ge(xT_ready, KD * (c - 2) + k + 1)
                    for i in range(TPC):
                        ins = pe.transpose(banks[(c % 2) * KD + k][0:DP, i * P:(i + 1) * P],
                                           xs[:, c * TPC + i, k * DP:(k + 1) * DP], g.ident[:, :])
                    ins.then_inc(tr_done, 1)
            for c in range(NCH):
                pe.wait_ge(xT_ready, KD * (c + 1))
                for j6 in range(2 * MI):
                    j = c * 2 * MI + j6
                    m = j6 // 2 + MI * (j6 % 2)
                    if j >= 4:
                        pe.wait_ge(res_ready if j % 2 else xr_ready, (j - 4) // 2 + 1)
                    for k in range(KD):
                        ins = pe.matmul(banks[4 + j % 4][:, :], g.w_in[:, k, m * P:(m + 1) * P],
                                        xT[:, k, c * CH:(c + 1) * CH], start=(k == 0), stop=(k == KD - 1))
                    ins.then_inc(proj_done, 1)
            pe.wait_ge(xr_ready, MI * NCH)
            pe.wait_ge(res_ready, MI * NCH)
            for c in range(NCH):
                pe.wait_ge(u_ready, MI * (c + 1))
                if c >= 2:
                    pe.wait_ge(dtT_ready, c - 1)
                for m in range(MI):
                    ins = pe.matmul(banks[c % 2][0:NX + RK, :], g.w_x[:, l, m, :], g.u[:, m, c * CH:(c + 1) * CH],
                                    start=(m == 0), stop=(m == MI - 1))
                ins.then_inc(xp_done, 1)
                pe.wait_ge(dtT_ready, c + 1)
                for m in range(MI):
                    j = MI * c + m
                    if j >= 4:
                        pe.wait_ge(relu_done, j - 3)
                    pe.matmul(banks[2 + j % 4][:, :], g.w_dt[:, l, m * P:(m + 1) * P], dtT[:, c % 2, :],
                              start=True, stop=True).then_inc(dt_done, 1)


def mamba_scan(nc, g, l):
    JP = 2 * MI
    NP2 = NS // 2
    (b_rep, c_rep, b_copied, decay_ready, in_ready, scanned, carried, weighted, hc_free,
     gated, diag_made, out_done, added, pool_turns, dve_turns,
     w_in_loaded) = sems(nc, g, " ".join(f"{n}{l}" for n in (
        "b_replicated c_replicated b_copied decay_ready input_ready scanned carried "
        "weighted hc_free gated diag_made out_projected x_added pool_turns dve_turns w_in_loaded").split()))
    with ExitStack() as local:
        def sb(name, shape, dt=F32):
            return local.enter_context(nc.sbuf_tensor(f"{name}{l}", shape, dt))
        brep = sb("brep", [P, 2, CH])
        decay = sb("decay", [P, MI, CH])
        inp = sb("inp", [P, JP, CH])
        hst = sb("hst", [P, JP, CH])
        carry = sb("carry", [P, NS * MI])
        diag = sb("diag", [P, MI, P])
        psy = [local.enter_context(nc.psum_tensor(f"psy{l}_{m}", [P, CH], F32)) for m in range(MI)]
        psa = [local.enter_context(nc.psum_tensor(f"psa{l}_{m}", [P, CH], F32)) for m in range(2)]
        psc = [local.enter_context(nc.psum_tensor(f"psc{l}_{m}", [P, CH], F32)) for m in range(2)]
        psb = local.enter_context(nc.psum_tensor(f"psb{l}", [P, CH], F32))
        y = g.xr[:, :, 0:CH]
        hc = [g.xr[:, :, (1 + e) * CH:(2 + e) * CH] for e in range(2)]
        block = local.enter_context(nc.Block())

        @block.sync
        def _(sp):
            if l + 1 < NL:
                sp.dma_start(g.w_in[:, :, :], ks(g.tok["in_proj_w"][l + 1])).then_inc(w_in_loaded, 16)
                sp.wait_ge(w_in_loaded, 16)

        @block.tensor
        def _(pe):
            def replicate_b(c, n, q):
                pe.wait_ge(b_copied, q + 1)
                pe.matmul(psb[:, :], g.sel[:, n, :], g.bcp[:, bass.ds(c * CH, CH)], start=True,
                          stop=True).then_inc(b_rep, 1)

            def replicate_c(c, n, e):
                pe.matmul(psc[e][:, :], g.sel[:, n + NS, :], g.bcp[:, bass.ds(c * CH, CH)], start=True,
                          stop=True).then_inc(c_rep, 1)

            def accumulate(n, e, stop):
                pe.wait_ge(weighted, n + 3)
                for m in range(MI):
                    ins = pe.matmul(psy[m][:, :], g.ident[:, :], hc[e][:, m, :], start=False, stop=stop,
                                    skip_group_check=True)
                ins.then_inc(hc_free, 1)

            pe.sem_inc(hc_free, 2)
            for e in range(2):
                pe.wait_ge(b_copied, e + 1)
                pe.matmul(psb[:, :], g.sel[:, e, :], g.bcp[:, 0:CH], start=True, stop=True).then_inc(b_rep, 1)
                pe.matmul(psc[e][:, :], g.sel[:, e + NS, :], g.bcp[:, 0:CH], start=True, stop=True).then_inc(c_rep, 1)
            pe.wait_ge(b_copied, 3)
            pe.matmul(psb[:, :], g.sel[:, 2, :], g.bcp[:, 0:CH], start=True, stop=True).then_inc(b_rep, 1)
            pe.wait_ge(diag_made, MI)

            def project(q, bank):
                for m in range(MI):
                    ins = pe.matmul(bank[:, 0:D], y[:, m, q * P:(q + 1) * P], g.w_out[:, l, m, :],
                                    start=(m == 0), stop=(m == MI - 1))
                ins.then_inc(out_done, 1)

            def chunk(c, first):
                pe.wait_ge(gated, MI * c + MI)
                for m in range(MI):
                    pe.matmul(psy[m][:, :], diag[:, m, :], g.u[:, m, bass.ds(c * CH, CH)], start=True, stop=False,
                              skip_group_check=True)
                for n in range(NS):
                    replicate_b(c + (n + 3) // NS, (n + 3) % NS, c * NS + (n + 3))
                    accumulate(c * NS + n, n % 2, n == NS - 1)
                    if n % TPC == 0 and not first:
                        pe.wait_ge(added, (c - 1) * TPC + (n // TPC + 1))
                        project(n // TPC, psa[0])
                    replicate_c(c + (n + 2) // NS, (n + 2) % NS, n % 2)

            chunk(0, True)
            with pe.Fori(1, NCH) as c:
                chunk(c, False)
            pe.wait_ge(gated, MI * (NCH + 1))
            for i in range(NT - TPC, NT):
                if i != NT - TPC + 1:
                    pe.wait_ge(added, i + 1 if i == NT - TPC else i)
                project(i % TPC, psa[i % 2])

        @block.scalar
        def _(act):
            act.sem_inc(b_copied, 1)

            def copy_b(e, q):
                act.wait_ge(b_rep, q + 1)
                act.wait_ge(in_ready, q * MI)
                act.activation(brep[:, e, :], psb[:, :], ACT.Copy).then_inc(b_copied, 1)

            act.wait_ge(b_rep, 1)
            act.activation(brep[:, 0, :], psb[:, :], ACT.Copy).then_inc(b_copied, 1)
            act.preload_act_table(ACT.Exp)
            with act.Fori(0, NCH) as c:
                with act.Fori(0, NP2) as p:
                    for e in range(2):
                        for m in range(MI):
                            j = MI * e + m
                            act.wait_ge(scanned, (c * NP2 + p) * JP + (j + JP - MI + 1))
                            act.activation(decay[:, m, :], g.delta[:, m, bass.ds(c * CH, CH)], ACT.Exp,
                                           scale=g.a_neg[:, l, m, bass.ds(p * 2 + e, 1)]).then_inc(decay_ready, 1)
                            if m == 1:
                                copy_b(1 - e, c * NS + p * 2 + (e + 1))
            copy_b(1, NCH * NS + 1)

        @block.gpsimd
        def _(pool):
            pool.sem_inc(in_ready, MI)
            with pool.Fori(0, NCH) as c:
                with pool.Fori(0, NP2) as p:
                    for e in range(2):
                        pool.wait_ge(b_copied, c * NS + p * 2 + e + 2)
                        for m in range(MI):
                            j = MI * e + m
                            pool.wait_ge(scanned, (c * NP2 + p) * JP + j + 1)
                            pool.sem_inc(pool_turns, 1)
                            pool.tensor_tensor(inp[:, j, :], g.du[:, m, bass.ds(c * CH, CH)], brep[:, e, :],
                                               ALU.mult).then_inc(in_ready, 1)

        @block.vector
        def _(dve):
            dve.sem_inc(gated, MI)
            dve.sem_inc(added, 1)
            dve.sem_inc(scanned, JP)
            dve.sem_inc(weighted, 2)
            dve.memset(carry[:, :], 0.0).then_inc(carried, 2)
            for m in range(MI):
                dve.tensor_scalar(diag[:, m, :], g.ident[:, :], g.d_c[:, l, m:m + 1], None,
                                  ALU.mult).then_inc(diag_made, 1)

            def scan(c, p, j):
                k, n = (c * NP2 + p) * JP + j, c * NS + p * 2 + j // MI
                dve.wait_ge(decay_ready, k + 1)
                dve.wait_ge(in_ready, k + (MI + 1))
                if j % MI == 0:
                    dve.wait_ge(carried, n + 1)
                    dve.wait_ge(weighted, n + 1)
                dve.tensor_tensor_scan(hst[:, j, :], decay[:, j % MI, :], inp[:, j, :],
                                       carry[:, bass.ds(p * JP + j, 1)], ALU.mult, ALU.add).then_inc(scanned, 1)

            def weight(c, p, e):
                n = c * NS + p * 2 + e
                items = slice(MI * e, MI * (e + 1))
                dve.wait_ge(scanned, n * MI + (MI + JP))
                dve.sem_inc(dve_turns, 1)
                dve.tensor_copy(carry[:, bass.ds(p * JP + MI * e, MI)], hst[:, items, CH - 1]).then_inc(carried, 1)
                dve.wait_ge(c_rep, n + 1)
                dve.wait_ge(hc_free, n + 1)
                dve.tensor_tensor(hc[e], hst[:, items, :], psc[e][:, :].unsqueeze(1).broadcast_to([P, MI, CH]),
                                  ALU.mult).then_inc(weighted, 1)

            def gate(c):
                dve.wait_ge(hc_free, c * NS + (NS + 2))
                for m in range(MI):
                    dve.tensor_tensor(y[:, m, :], g.sres[:, m, bass.ds(c * CH, CH)], psy[m][:, :],
                                      ALU.mult).then_inc(gated, 1)

            def pair(c, p, before):
                for e in range(2):
                    scan(c, p, MI * e)
                    if e:
                        weight(c, p, 0)
                        if before == "chunk":
                            gate(c - 1)
                    elif before == "chunk":
                        weight(c - 1, NP2 - 1, 1)
                    elif before == "pair":
                        weight(c, p - 1, 1)
                    scan(c, p, MI * e + 1)
                    scan(c, p, MI * e + 2)

            def add(i, bank):
                dve.wait_ge(out_done, i + 1)
                xi = g.x[:, bass.ds(i, 1), :].rearrange("p i d -> p (i d)")
                dve.tensor_tensor(xi, xi, bank[:, 0:D], ALU.add).then_inc(added, 1)

            def chunk(c, first):
                pair(c, 0, None if first else "chunk")
                pair(c, 1, "pair")
                if not first:
                    add((c - 1) * TPC, psa[0])
                with dve.Fori(1, TPC) as q:
                    pair(c, q * 2, "pair")
                    pair(c, q * 2 + 1, "pair")
                    if not first:
                        add((c - 1) * TPC + q, psa[0])

            chunk(0, True)
            with dve.Fori(1, NCH) as c:
                chunk(c, False)
            weight(NCH - 1, NP2 - 1, 1)
            gate(NCH - 1)
            for i in range(NT - TPC, NT):
                add(i, psa[i % 2])
            dve.wait_ge(added, NT + 1)


def norm_sems(nc, g, name):
    v = Core()
    v.stats, v.mean_var, v.root, v.recip, v.rows = sems(nc, g, " ".join(
        f"{name}_{n}" for n in "stats mean_var root reciprocal rows".split()))
    return v


def row_stats(dve, g, v, src, i):
    dve.bn_stats(g.nst[:, i, :], src[:, i, 0:D]).then_inc(v.stats, 1)
    dve.wait_ge(v.stats, i + 1)
    dve.bn_aggr(g.nmv[:, i, :], g.nst[:, i, :]).then_inc(v.mean_var, 1)


def scale_rows(dve, g, v, src, dst, n, eps, counted=True):
    rs = g.nrs[:, 0:n]
    if counted:
        dve.wait_ge(v.mean_var, n)
    dve.tensor_scalar(rs, g.nmv[:, 0:n, 1], eps, None, ALU.add).then_inc(v.mean_var, 1)
    dve.wait_ge(v.root, 1)
    dve.reciprocal(rs, rs).then_inc(v.recip, 1)
    dve.wait_ge(v.recip, 1)
    for i in range(n):
        dve.tensor_scalar(dst[:, i, 0:D], src[:, i, 0:D], g.nmv[:, i, 0:1], g.nrs[:, i:i + 1],
                          ALU.subtract, ALU.mult).then_inc(v.rows, 1)


def row_root(act, g, v, n, counted=True):
    act.wait_ge(v.mean_var, n + 1 if counted else 1)
    act.activation(g.nrs[:, 0:n], g.nrs[:, 0:n], ACT.Sqrt).then_inc(v.root, 1)


def normalize_rows(nc, g, name, src, dst, eps, loads=None, after=None):
    v = norm_sems(nc, g, name)
    n = src.shape[1]
    with nc.Block() as block:
        if loads is not None:
            @block.sync
            def _(sp):
                with nc.allow_non_contiguous_dma(reason="small weights"):
                    loads(sp, g)

        @block.vector
        def _(dve):
            for i in range(n):
                row_stats(dve, g, v, src, i)
            scale_rows(dve, g, v, src, dst, n, eps)
            if after is not None:
                for i in range(n):
                    dve.wait_ge(v.rows, i + 1)
                    row_stats(dve, g, after, dst, i)
            dve.wait_ge(v.rows, n)

        @block.scalar
        def _(act):
            row_root(act, g, v, n)


def transpose_rows(pe, g, banks, src, c, k, done):
    for i in range(TPC):
        ins = pe.transpose(banks[(c % 2) * KD + k][0:DP, i * P:(i + 1) * P],
                           src[:, c * TPC + i, k * DP:(k + 1) * DP], g.ident[:, :])
    ins.then_inc(done, 1)


def load_attention(sp, g):
    a, I = g.a, g.attn
    w = a.w_qkv
    for dst, src in ((a.ln1_gb[:, 0, :], col(I["ln1_g"], DP)), (a.ln1_gb[:, 1, :], col(I["ln1_b"], DP)),
                     (w[:, 0], ks(I["Wq"])), (w[:, 1], ks(I["Wk"])), (w[:, 2], ks(I["Wv"])),
                     (a.qk_bias[:, 0, :], col(I["bq"], DP)), (a.qk_bias[:, 1, :], col(I["bk"], DP)),
                     (a.bv[:, :], I["bv"].partition_broadcast(P)),
                     (a.bo[:, :], I["bo"].partition_broadcast(P)),
                     *((a.w_o[VE * q:VE * q + DH, :, :],
                        I["Wo"].rearrange("(h q e) n -> q e h n", q=HQ, e=DH)[q]) for q in range(HQ)),
                     *((a.proj_blocks[DH * j:DH * (j + 1), j, :], I["proj"].rearrange("m d -> d m"))
                       for j in range(HK))):
        sp.dma_start(dst, src).then_inc(a.w_in, 16)


def load_phi(sp, g):
    sp.dma_start(g.e.phi, g.ffn["phi"].rearrange("(a b) q d -> (b q) a d", b=EG)).then_inc(g.e.phi_in, 16)
    sp.dma_start(g.e.lng[:, 0, :], g.ffn["ln_g"]).then_inc(g.e.phi_in, 16)
    sp.dma_start(g.e.lng[:, 1, :], g.ffn["ln_b"]).then_inc(g.e.phi_in, 16)


def attn_project(nc, g, a):
    tr_done, hT_ready, qk_done, qk_ready, v_done, v_ready, halved, ones_set, bias_in = sems(
        nc, g, "attn_transposed attn_hT_ready qk_projected qk_ready v_projected v_ready "
        "biases_scaled v_ones_set xa_biased")
    with ExitStack() as local, nc.allow_non_contiguous_dma(reason="small weights"):
        def sb(name, shape, dt=F32):
            return local.enter_context(nc.sbuf_tensor(name, shape, dt))
        hT = sb("hT", [DP, KD, L])
        w, gb, qkb, bv, bo = a.w_qkv, a.ln1_gb, a.qk_bias, a.bv, a.bo
        banks = [local.enter_context(nc.psum_tensor(f"pb{i}", [P, CH], F32)) for i in range(8)]
        block = local.enter_context(nc.Block())
        w_in, NW = a.w_in, a.n_w_in

        @block.gpsimd
        def _(pool):
            pool.memset(a.v[:, :, :, DH:DH + 1], 1.0).then_inc(ones_set, 1)
            pool.memset(a.v[:, :, :, DH + 1:VE], 0.0).then_inc(ones_set, 1)
            pool.wait_ge(w_in, NW)
            for i in range(NT):
                pool.wait_ge(a.norm1.rows, i + 1)
                pool.tensor_tensor(a.xa[:, i, :], a.xa[:, i, :], bo[:, :], ALU.add).then_inc(bias_in, 1)
            pool.wait_ge(bias_in, NT)

        @block.tensor
        def _(pe):
            for c in range(NCH):
                pe.wait_ge(a.norm1.rows, TPC * (c + 1))
                for k in range(KD):
                    if c >= 2:
                        pe.wait_ge(hT_ready, KD * (c - 2) + k + 1)
                    transpose_rows(pe, g, banks, a.xs, c, k, tr_done)
            pe.wait_ge(w_in, NW)
            for c in range(NCH):
                pe.wait_ge(hT_ready, KD * (c + 1))
                for qk in range(2):
                    for m in range(KD):
                        j = (c * 2 + qk) * KD + m
                        if j >= 2:
                            pe.wait_ge(qk_ready, 2 * (j - 1))
                        for k in range(KD):
                            ins = pe.matmul(banks[4 + j % 2][0:DP, :], w[:, qk, k, m * DP:(m + 1) * DP],
                                            hT[:, k, c * CH:(c + 1) * CH], start=(k == 0), stop=(k == KD - 1))
                        ins.then_inc(qk_done, 1)
                for i in range(c * TPC, (c + 1) * TPC):
                    if i >= 2:
                        pe.wait_ge(v_ready, i - 1)
                    for k in range(KD):
                        ins = pe.matmul(banks[6 + i % 2][:, 0:D], hT[:, k, i * P:(i + 1) * P], w[:, 2, k, :],
                                        start=(k == 0), stop=(k == KD - 1))
                    ins.then_inc(v_done, 1)

        @block.scalar
        def _(act):
            row_root(act, g, a.norm1, NT)
            act.wait_ge(w_in, NW)
            for c in range(NCH):
                for k in range(KD):
                    act.wait_ge(tr_done, KD * c + k + 1)
                    act.activation(hT[:, k, c * CH:(c + 1) * CH], banks[(c % 2) * KD + k][0:DP, :], ACT.Identity,
                                   scale=gb[:, 0, k:k + 1], bias=gb[:, 1, k:k + 1]).then_inc(hT_ready, 1)
            act.wait_ge(halved, 1)
            for c in range(NCH):
                for qk in range(2):
                    for m in range(KD):
                        j = (c * 2 + qk) * KD + m
                        act.wait_ge(qk_done, j + 1)
                        for out, f in ((a.qk[qk][:, m, c * CH:(c + 1) * CH], ACT.Identity),
                                       (a.qk2[qk][:, m, c * CH:(c + 1) * CH], ACT.Square)):
                            act.activation(out, banks[4 + j % 2][0:DP, :], f, scale=DH ** -0.25,
                                           bias=qkb[:, qk, m:m + 1]).then_inc(qk_ready, 1)

        @block.vector
        def _(dve):
            scale_rows(dve, g, a.norm1, a.xa, a.xs, NT, 1e-5)
            dve.wait_ge(w_in, NW)
            dve.tensor_scalar(qkb[:, :, :], qkb[:, :, :], DH ** -0.25, None, ALU.mult).then_inc(halved, 1)
            for i in range(NT):
                dve.wait_ge(v_done, i + 1)
                dve.tensor_tensor(a.v[:, i, :, 0:DH], banks[6 + i % 2][:, 0:D].rearrange("p (h e) -> p h e", e=DH),
                                  bv[:, :].rearrange("p (h e) -> p h e", e=DH), ALU.add).then_inc(v_ready, 1)


def attn_key_logits(nc, g, a):
    dd_done, diag_copied, kdd_ready, kmax_ready, gmax = sems(
        nc, g, "k_dd_done k_diag_copied k_dd_ready k_max_ready k_global_max")
    with ExitStack() as local:
        def sb(name, shape, dt=F32):
            return local.enter_context(nc.sbuf_tensor(name, shape, dt))
        kd = sb("k_diag", [P, NT, KD, HK])
        km = sb("k_max", [P, NT, KD])
        km1 = sb("k_max1", [P, 1])
        row = sb("k_max_row", [1, 2])
        banks = [local.enter_context(nc.psum_tensor(f"kb{i}", [P, CH], F32)) for i in range(8)]
        block = local.enter_context(nc.Block())
        W = HK * M

        @block.tensor
        def _(pe):
            for i in range(NT):
                if i >= 4:
                    pe.wait_ge(kdd_ready, KD * (i - 3))
                    pe.wait_ge(kmax_ready, KD * (i - 3))
                for k in range(KD):
                    b = banks[(i % 4) * KD + k]
                    t = slice(i * P, (i + 1) * P)
                    pe.matmul(b[:, 0:W], a.qk[1][:, k, t], a.proj_blocks[:, :, :], start=True, stop=True)
                    pe.matmul(b[:, W:W + HK], a.qk2[1][:, k, t], g.head_of[:, :], start=True,
                              stop=True).then_inc(dd_done, 1)
            pe.wait_ge(gmax, 1)
            pe.transpose(banks[0][0:1, 0:P], km1[:, :], g.ident[:, :]).then_inc(gmax, 1)
            pe.wait_ge(gmax, 3)
            pe.matmul(banks[1][:, 0:1], g.ones[0:1, :], row[:, 0:1], start=True, stop=True).then_inc(gmax, 1)

        @block.scalar
        def _(act):
            for i in range(NT):
                for k in range(KD):
                    act.wait_ge(dd_done, KD * i + k + 1)
                    act.activation(kd[:, i, k, :], banks[(i % 4) * KD + k][:, W:W + HK],
                                   ACT.Copy).then_inc(diag_copied, 1)

        @block.vector
        def _(dve):
            for i in range(NT):
                for k in range(KD):
                    dd = banks[(i % 4) * KD + k][:, 0:W]
                    dve.wait_ge(diag_copied, KD * i + k + 1)
                    dve.tensor_reduce(km[:, i, k:k + 1], dd, AX.X, ALU.max).then_inc(kmax_ready, 1)
                    dve.tensor_tensor(a.kdd[:, i, k, :, :], dd.rearrange("p (h m) -> p h m", m=M),
                                      kd[:, i, k, :].unsqueeze(2).broadcast_to([P, HK, M]),
                                      ALU.subtract).then_inc(kdd_ready, 1)
            dve.wait_ge(kmax_ready, KD * NT)
            dve.tensor_reduce(km1[:, :], km[:, :, :], AX.XY, ALU.max).then_inc(gmax, 1)
            dve.wait_ge(gmax, 2)
            dve.tensor_reduce(row[:, 0:1], banks[0][0:1, 0:P], AX.X, ALU.max).then_inc(gmax, 1)
            dve.wait_ge(gmax, 4)
            dve.tensor_scalar(a.neg_kmax[:, :], banks[1][:, 0:1], -1.0, None, ALU.mult).then_inc(gmax, 1)


def attention(nc, g, a):
    (qdd_done, qdiag_ready, qmax_ready, qbias_ready, qarg_ready, qexp_ready, qp_ready, kexp_ready, kp_ready,
     turned, turned_copied, at_done, masked, state_done, out_done, state_ready, recip, o_ready, padded) = sems(
         nc, g, " ".join("at_" + n for n in (
             "qdd_done qdiag_ready qmax_ready qbias_ready qarg_ready qexp_ready qp_ready kexp_ready kp_ready "
             "turned turned_copied products_done masked state_done out_done state_ready recip o_ready padded").split()))
    with ExitStack() as local:
        def sb(name, shape, dt=F32):
            return local.enter_context(nc.sbuf_tensor(name, shape, dt))
        qd = sb("q_diag", [P, 2, H])
        qm = sb("q_max", [P, 2, H])
        qarg = sb("q_arg", [P, 2, H, M])
        kexp = sb("k_exp", [P, 2, H, M])
        qp = sb("q_feat", [P, 2, H, MP])
        kp = sb("k_feat", [P, 3, H, MP])
        kT = sb("k_feat_T", [P, 2, HP, P])
        qT = a.xs[:, :, :].rearrange("p i d -> p (i d)").rearrange("p (n j s t) -> p n j s t", n=2, s=2, t=P)
        am = sb("masked_products", [P, H, P])
        st = sb("state", [P, 2, HP, VE])
        zt = sb("feature_sums", [P, 2, HP, VE])
        rc = sb("recip_den", [P, HG, P])
        ones = sb("ones_by_32", [P, VE])
        zero = sb("zeros", [P, CH], BF16)
        banks = [local.enter_context(nc.psum_tensor(f"ab{i}", [P, CH], F32)) for i in range(8)]
        block = local.enter_context(nc.Block())
        W = HK * M
        PADS = 7

        def copied(n):
            return 6 * (n // 3) + (1, 4, 6)[n % 3]
        ratio = M ** -0.5

        @block.gpsimd
        def _(pool):
            pool.memset(qp[:, :, :, M:MP], 0.0).then_inc(padded, 1)
            pool.memset(kp[:, :, :, M:MP], 0.0).then_inc(padded, 1)
            pool.memset(qT[:, :, :, :, :], 0.0).then_inc(padded, 1)
            pool.memset(st[:, 0, :, :], 0.0).then_inc(padded, 1)
            pool.memset(zt[:, 0, :, :], 1e-6).then_inc(padded, 1)
            pool.memset(ones[:, :], 1.0).then_inc(padded, 1)
            pool.memset(zero[:, :], 0.0).then_inc(padded, 1)
            pool.wait_ge(padded, PADS)
            for i in range(NT):
                if i >= 3:
                    pool.wait_ge(out_done, i - 2)
                pool.wait_ge(kexp_ready, i + 1)
                pool.tensor_scalar(kp[:, i % 3, :, 0:M], kexp[:, i % 2, :, :], 1e-4, ratio, ALU.add,
                                   ALU.mult).then_inc(kp_ready, 1)
                if i >= 2:
                    pool.wait_ge(turned, 3 * (i - 1))
                pool.wait_ge(qexp_ready, i + 1)
                pool.tensor_scalar(qp[:, i % 2, :, 0:M], qarg[:, i % 2, :, :], 1e-4, ratio, ALU.add,
                                   ALU.mult).then_inc(qp_ready, 1)

        @block.scalar
        def _(act):
            def features(i):
                if i >= 2:
                    act.wait_ge(kp_ready, i - 1)
                act.activation(kexp[:, i % 2, :, :], a.kdd[:, i, :, :, :].rearrange("p k h m -> p (k h) m"), ACT.Exp,
                               bias=a.neg_kmax[:, :]).then_inc(kexp_ready, 1)
                for k in range(KD):
                    act.wait_ge(qdd_done, KD * i + k + 1)
                    if i >= 2 and k == 0:
                        act.wait_ge(qbias_ready, i - 1)
                    act.activation(qd[:, i % 2, k * HK:(k + 1) * HK], banks[k][:, W:W + HK],
                                   ACT.Identity).then_inc(qdiag_ready, 1)
                act.wait_ge(qarg_ready, KD * (i + 1))
                act.activation(qarg[:, i % 2, :, :], qarg[:, i % 2, :, :], ACT.Exp).then_inc(qexp_ready, 1)

            def copy_turned(i):
                if i >= 2:
                    act.wait_ge(out_done, i - 1)
                for b in range(3):
                    act.wait_ge(turned, 3 * i + b + 1)
                    src = banks[2 + (3 * i + b) % 2][:, :].rearrange("p (s t) -> p s t", t=P)
                    nk = min(max(HP - 4 * b, 0), 4)
                    if nk:
                        act.activation(kT[:, i % 2, 4 * b:4 * b + nk, :], src[:, 0:nk, :],
                                       ACT.Identity).then_inc(turned_copied, 1)
                    if nk < 4:
                        j = 4 * b + nk - HP
                        for s in range(2):
                            q = slice(MP * s, MP * (s + 1))
                            act.activation(qT[q, i % 2, j:j + 4 - nk, s, :], src[q, nk:4, :],
                                           ACT.Identity).then_inc(turned_copied, 1)

            act.wait_ge(padded, PADS)
            features(0)
            features(1)
            copy_turned(0)
            for i in range(NT):
                if i + 1 < NT:
                    copy_turned(i + 1)
                if i + 2 < NT:
                    features(i + 2)

        @block.vector
        def _(dve):
            def features(i):
                for k in range(KD):
                    dve.wait_ge(qdiag_ready, KD * i + k + 1)
                    dve.tensor_reduce(qm[:, i % 2, k * HK:(k + 1) * HK],
                                      banks[k][:, 0:W].rearrange("p (h m) -> p h m", m=M), AX.X,
                                      ALU.max).then_inc(qmax_ready, 1)
                dve.wait_ge(qmax_ready, KD * (i + 1))
                dve.tensor_tensor(qm[:, i % 2, :], qm[:, i % 2, :], qd[:, i % 2, :], ALU.add).then_inc(qbias_ready, 1)
                dve.wait_ge(qbias_ready, i + 1)
                if i >= 2:
                    dve.wait_ge(qp_ready, i - 1)
                for k in range(KD):
                    dve.tensor_tensor(qarg[:, i % 2, k * HK:(k + 1) * HK, :],
                                      banks[k][:, 0:W].rearrange("p (h m) -> p h m", m=M),
                                      qm[:, i % 2, k * HK:(k + 1) * HK].unsqueeze(2).broadcast_to([P, HK, M]),
                                      ALU.subtract).then_inc(qarg_ready, 1)

            def mask(i, b):
                dve.wait_ge(at_done, 3 * i + b + 1)
                dve.tensor_tensor(am[:, HQ * b:HQ * (b + 1), :],
                                  banks[5 + b % 2][:, :].rearrange("p (h t) -> p h t", t=P),
                                  g.causal[:, :].unsqueeze(1).broadcast_to([P, HQ, P]), ALU.mult).then_inc(masked, 1)

            def divide(i):
                dve.wait_ge(out_done, i + 1)
                dve.reciprocal(rc[:, :, :], banks[4][:, 0:HG * P].rearrange("p (h t) -> p h t", t=P)).then_inc(recip, 1)
                dve.wait_ge(recip, i + 1)
                dve.tensor_tensor(a.oT[:, :, i * P:(i + 1) * P], banks[7][:, 0:HG * P].rearrange("p (h t) -> p h t", t=P),
                                  rc[:, :, :], ALU.mult).then_inc(o_ready, 1)

            features(0)
            features(1)
            dve.wait_ge(padded, PADS)
            for i in range(NT):
                if i:
                    dve.wait_ge(out_done, i)
                mask(i, 0)
                mask(i, 1)
                if i:
                    divide(i - 1)
                mask(i, 2)
                if i + 2 < NT:
                    features(i + 2)
                dve.wait_ge(state_done, i + 1)
                if i:
                    dve.wait_ge(state_ready, 4 * i)
                sp = banks[6][:, 0:H * VE].rearrange("p (j s e) -> p j s e", s=2, e=VE)
                for s in range(2):
                    q = slice(MP * s, MP * (s + 1))
                    dve.tensor_tensor(st[q, (i + 1) % 2, :, :], st[q, i % 2, :, :], sp[q, :, s, :],
                                      ALU.add).then_inc(state_ready, 1)
                    dve.tensor_tensor(zt[q, (i + 1) % 2, :, :], zt[q, i % 2, :, :],
                                      sp[q, :, s, DH:DH + 1].broadcast_to([MP, HP, VE]), ALU.add).then_inc(state_ready, 1)
            divide(NT - 1)
            dve.wait_ge(state_ready, 4 * NT)
            dve.wait_ge(o_ready, NT)

        @block.tensor
        def _(pe):
            def logits(i):
                if i:
                    pe.wait_ge(qarg_ready, KD * i)
                for k in range(KD):
                    t = slice(i * P, (i + 1) * P)
                    pe.matmul(banks[k][:, 0:W], a.qk[0][:, k, t], a.proj_blocks[:, :, :], start=True, stop=True)
                    pe.matmul(banks[k][:, W:W + HK], a.qk2[0][:, k, t], g.head_of[:, :], start=True,
                              stop=True).then_inc(qdd_done, 1)

            def turn(i, b):
                n = 3 * i + b
                if n >= 2:
                    pe.wait_ge(turned_copied, copied(n - 2))
                for s in range(4 * b, 4 * b + 4):
                    f, m, j = (kp, 3, s) if s < HP else (qp, 2, s - HP)
                    if s == 0:
                        pe.wait_ge(kp_ready, i + 1)
                    if s == HP:
                        pe.wait_ge(qp_ready, i + 1)
                    ins = pe.transpose(banks[2 + n % 2][:, (s % 4) * P:(s % 4 + 1) * P],
                                       f[:, i % m, 2 * j:2 * j + 2, :].rearrange("p h m -> p (h m)"), g.ident[:, :])
                ins.then_inc(turned, 1)

            def products(i, b):
                if b == 0:
                    pe.wait_ge(turned_copied, copied(3 * i + 2))
                    if i:
                        pe.wait_ge(masked, 3 * i)
                if b == 1 and i:
                    pe.wait_ge(state_ready, 4 * i)
                if b == 2:
                    pe.wait_ge(masked, 3 * i + 1)
                for j in range(2):
                    ins = pe.matmul(banks[5 + b % 2][:, 2 * j * P:2 * (j + 1) * P], kT[:, i % 2, 2 * b + j, :],
                                    qT[:, i % 2, 2 * b + j, :, :].rearrange("p s t -> p (s t)"), start=True, stop=True)
                ins.then_inc(at_done, 1)

            def state(i):
                pe.wait_ge(masked, 3 * i + 2)
                for j in range(HP):
                    ins = pe.matmul(banks[6][:, 2 * VE * j:2 * VE * (j + 1)],
                                    kp[:, i % 3, 2 * j:2 * j + 2, :].rearrange("p h m -> p (h m)"),
                                    a.v[:, i, 2 * j:2 * j + 2, :].rearrange("p h e -> p (h e)"), start=True, stop=True)
                ins.then_inc(state_done, 1)

            def outputs(i):
                pe.wait_ge(masked, 3 * i + 3)
                if i:
                    pe.wait_ge(o_ready, i)
                for bank in (7, 4):
                    pe.matmul(banks[bank][:, 0:HG * P], zero[:, 0:P], zero[:, 0:HG * P], start=True, stop=False,
                              skip_group_check=True)
                for bank, now, before in ((7, None, st), (4, ones, zt)):
                    for h0 in range(0, H, HQ):
                        for h in range(h0, h0 + HQ):
                            q, t = VE * (h % HQ), slice(h // HQ * P, (h // HQ + 1) * P)
                            pe.matmul(banks[bank][q:q + VE, t], before[:, i % 2, h // 2, :],
                                      qT[:, i % 2, h // 2, h % 2, :], start=False, stop=False, skip_group_check=True)
                        for h in range(h0, h0 + HQ):
                            q, t = VE * (h % HQ), slice(h // HQ * P, (h // HQ + 1) * P)
                            ins = pe.matmul(banks[bank][q:q + VE, t], a.v[:, i, h, :] if now is None else now[:, :],
                                            am[:, h, :], start=False, stop=True, skip_group_check=True)
                ins.then_inc(out_done, 1)

            pe.wait_ge(padded, PADS)
            logits(0)
            logits(1)
            for b in range(3):
                turn(0, b)
            for i in range(NT):
                products(i, 0)
                products(i, 1)
                if i + 1 < NT:
                    turn(i + 1, 0)
                    turn(i + 1, 1)
                products(i, 2)
                if i + 1 < NT:
                    turn(i + 1, 2)
                state(i)
                if i + 2 < NT:
                    logits(i + 2)
                outputs(i)


def attn_output(nc, g, a):
    wo_done, xa_ready, a.mlp_w_in = sems(nc, g, "wo_done xa_ready mlp_w_in")
    with ExitStack() as local, nc.allow_non_contiguous_dma(reason="small weights"):
        banks = [local.enter_context(nc.psum_tensor(f"ob{i}", [P, CH], F32)) for i in range(4)]
        block = local.enter_context(nc.Block())

        @block.sync
        def _(sp):
            I = g.attn
            w1, w2, gb, b1, b2 = a.mlp_w
            for dst, src in ((gb[:, 0, :], col(I["ln2_g"], DP)), (gb[:, 1, :], col(I["ln2_b"], DP)),
                             (w1[:, :, :], ks(I["W1"])), (w2[:, :, :], I["W2"].rearrange("(m p) n -> p m n", p=P)),
                             (b1[:, :], col(I["b1"], P)), (b2[:, :], I["b2"].partition_broadcast(P))):
                sp.dma_start(dst, src).then_inc(a.mlp_w_in, 16)

        @block.tensor
        def _(pe):
            for i in range(NT):
                if i >= 4:
                    pe.wait_ge(xa_ready, i - 3)
                for k in range(HG):
                    ins = pe.matmul(banks[i % 4][:, 0:D], a.oT[:, k, i * P:(i + 1) * P], a.w_o[:, k, :],
                                    start=(k == 0), stop=(k == HG - 1))
                ins.then_inc(wo_done, 1)

        @block.vector
        def _(dve):
            for i in range(NT):
                dve.wait_ge(wo_done, i + 1)
                dve.tensor_tensor(a.xa[:, i, :], a.xa[:, i, :], banks[i % 4][:, 0:D], ALU.add).then_inc(xa_ready, 1)
                dve.wait_ge(xa_ready, i + 1)
                row_stats(dve, g, a.norm2, a.xa, i)


def attn_mlp(nc, g, a):
    tr_done, hT_ready, up_done, gelu_ready, down_done, biased, added = sems(
        nc, g, "mlp_transposed mlp_hT_ready mlp_up_done gelu_ready mlp_down_done mlp_biased mlp_added")
    with ExitStack() as local, nc.allow_non_contiguous_dma(reason="small weights"):
        def sb(name, shape, dt=F32):
            return local.enter_context(nc.sbuf_tensor(name, shape, dt))
        hT = sb("mlp_hT", [DP, KD, L])
        gT = sb("gelu_T", [P, MF, L])
        w1, w2, gb, b1, b2 = a.mlp_w
        banks = [local.enter_context(nc.psum_tensor(f"mb{i}", [P, CH], F32)) for i in range(8)]
        block = local.enter_context(nc.Block())
        w_in, NW = a.mlp_w_in, 16 * 6

        @block.gpsimd
        def _(pool):
            pool.wait_ge(w_in, NW)
            for i in range(NT):
                pool.wait_ge(a.norm2.rows, i + 1)
                pool.tensor_tensor(a.xa[:, i, :], a.xa[:, i, :], b2[:, :], ALU.add).then_inc(biased, 1)
                pool.wait_ge(biased, 2 * i + 1)
                pool.tensor_tensor(g.x[:, i, :], g.x[:, i, :], a.xa[:, i, :], ALU.add).then_inc(biased, 1)

        @block.tensor
        def _(pe):
            for c in range(NCH):
                pe.wait_ge(a.norm2.rows, TPC * (c + 1))
                for k in range(KD):
                    if c >= 2:
                        pe.wait_ge(hT_ready, KD * (c - 2) + k + 1)
                    transpose_rows(pe, g, banks, a.xs, c, k, tr_done)
            pe.wait_ge(w_in, NW)
            for c in range(NCH + 1):
                if c < NCH:
                    pe.wait_ge(hT_ready, KD * (c + 1))
                    for m in range(MF):
                        j = c * MF + m
                        if j >= 2:
                            pe.wait_ge(gelu_ready, j - 1)
                        for k in range(KD):
                            ins = pe.matmul(banks[4 + j % 2][:, :], w1[:, k, m * P:(m + 1) * P],
                                            hT[:, k, c * CH:(c + 1) * CH], start=(k == 0), stop=(k == KD - 1))
                        ins.then_inc(up_done, 1)
                if c:
                    pe.wait_ge(gelu_ready, MF * c)
                    for i in range((c - 1) * TPC, c * TPC):
                        if i >= 2:
                            pe.wait_ge(added, i - 1)
                        for m in range(MF):
                            ins = pe.matmul(banks[6 + i % 2][:, 0:D], gT[:, m, i * P:(i + 1) * P], w2[:, m, :],
                                            start=(m == 0), stop=(m == MF - 1))
                        ins.then_inc(down_done, 1)

        @block.scalar
        def _(act):
            row_root(act, g, a.norm2, NT)
            act.wait_ge(w_in, NW)
            for c in range(NCH):
                for k in range(KD):
                    act.wait_ge(tr_done, KD * c + k + 1)
                    act.activation(hT[:, k, c * CH:(c + 1) * CH], banks[(c % 2) * KD + k][0:DP, :], ACT.Identity,
                                   scale=gb[:, 0, k:k + 1], bias=gb[:, 1, k:k + 1]).then_inc(hT_ready, 1)
            for j in range(NCH * MF):
                c, m = j // MF, j % MF
                act.wait_ge(up_done, j + 1)
                act.activation(gT[:, m, c * CH:(c + 1) * CH], banks[4 + j % 2][:, :], ACT.Gelu,
                               bias=b1[:, m:m + 1]).then_inc(gelu_ready, 1)

        @block.vector
        def _(dve):
            scale_rows(dve, g, a.norm2, a.xa, a.xs, NT, 1e-5)
            for i in range(NT):
                dve.wait_ge(down_done, i + 1)
                dve.wait_ge(biased, 2 * (i + 1))
                dve.tensor_tensor(g.x[:, i, :], g.x[:, i, :], banks[6 + i % 2][:, 0:D], ALU.add).then_inc(added, 1)
                dve.wait_ge(added, i + 1)
                row_stats(dve, g, g.norm3, g.x, i)


def moe_logits(nc, g, e):
    (phi_turned, phi_ready, square_ready, norm_step, phiT_ready, x_turned, xT_ready, lg_done, lg_ready,
     rmax_ready, cmax_step, cmax_turned, cmax_col, cmax_diag, cmax_rep, cmax_ready, wT_turned, wT_ready) = sems(
         nc, g, " ".join("moe_" + n for n in (
             "phi_turned phi_ready square_ready norm_step phiT_ready x_turned xT_ready logits_done "
             "logits_ready rmax_ready cmax_step cmax_turned cmax_col cmax_diag cmax_replicated cmax_ready "
             "ln_turned ln_ready").split()))
    with ExitStack() as local, nc.allow_non_contiguous_dma(reason="small weights"):
        def sb(name, shape, dt=F32):
            return local.enter_context(nc.sbuf_tensor(name, shape, dt))
        phi = e.phi
        n0 = ST * D
        phiT, sq = (e.w_place[0:DP, n0 + v * KD * S:n0 + (v + 1) * KD * S].rearrange("p (k s) -> p k s", k=KD)
                    for v in range(2))
        n0 += 2 * KD * S
        xT = e.w_place[0:DP, n0:n0 + KD * L].rearrange("p (k t) -> p k t", k=KD)
        rn = sb("phi_norm", [DP, KD, SL])
        cm = sb("tile_cmax", [P, S])
        cc = sb("cmax_cols", [P, ST])
        dg = sb("cmax_diag", [P, ST, P])
        lng = e.lng
        banks = [local.enter_context(nc.psum_tensor(f"eb{i}", [P, CH], F32)) for i in range(8)]
        block = local.enter_context(nc.Block())
        I = g.ffn

        @block.sync
        def _(sp):
            load_up(sp, g, e, 0)
            load_down(sp, g, e, 0)

        @block.tensor
        def _(pe):
            pe.wait_ge(e.phi_in, 48)
            for k in range(KD):
                for f in range(2):
                    for s in range(ST // 2):
                        ins = pe.transpose(banks[2 * k + f][0:DP, s * P:(s + 1) * P],
                                           phi[:, f * ST // 2 + s, k * DP:(k + 1) * DP], g.ident[:, :])
                    ins.then_inc(phi_turned, 1)
            for v in range(2):
                for k in range(KD):
                    ins = pe.transpose(banks[4][0:DP, (2 * v + k) * NE:(2 * v + k + 1) * NE],
                                       lng[:, v, k * DP:(k + 1) * DP], g.ident[0:NE, 0:NE])
            ins.then_inc(wT_turned, 1)
            pe.wait_ge(square_ready, 2 * KD)
            pe.wait_ge(phi_ready, 2 * KD)
            for c in range(NCH):
                pe.wait_ge(e.norm3.rows, TPC * (c + 1))
                for k in range(KD):
                    if c >= 2:
                        pe.wait_ge(xT_ready, KD * (c - 2) + k + 1)
                    transpose_rows(pe, g, banks, e.xm, c, k, x_turned)
            pe.wait_ge(phiT_ready, KD)
            pe.wait_ge(wT_ready, 1)
            for j in range(2 * NT):
                i, f = j // 2, j % 2
                pe.wait_ge(xT_ready, KD * (i // TPC + 1))
                if j >= 4:
                    pe.wait_ge(lg_ready, j - 3)
                for k in range(KD):
                    ins = pe.matmul(banks[4 + j % 4][:, :], xT[:, k, i * P:(i + 1) * P],
                                    phiT[:, k, f * CH:(f + 1) * CH], start=(k == 0), stop=(k == KD - 1))
                ins.then_inc(lg_done, 1)
            pe.wait_ge(cmax_step, NT)
            for s in range(ST):
                ins = pe.transpose(banks[s // 4][:, (s % 4) * P:(s % 4 + 1) * P], cm[:, s * P:(s + 1) * P], g.ident[:, :])
            ins.then_inc(cmax_turned, 1)
            for s in range(ST):
                pe.wait_ge(cmax_diag, s + 1)
                ins = pe.matmul(banks[2 + s // 4][:, (s % 4) * P:(s % 4 + 1) * P], g.ones[:, :], dg[:, s, :],
                                start=True, stop=True)
            ins.then_inc(cmax_rep, 1)

        @block.scalar
        def _(act):
            row_root(act, g, e.norm3, NT, counted=False)
            for k in range(KD):
                for f in range(2):
                    act.wait_ge(phi_turned, 2 * k + f + 1)
                    src = banks[2 * k + f][0:DP, :]
                    act.activation(sq[:, k, f * CH:(f + 1) * CH], src, ACT.Square).then_inc(square_ready, 1)
                    act.activation(phiT[:, k, f * CH:(f + 1) * CH], src, ACT.Copy).then_inc(phi_ready, 1)
            act.wait_ge(wT_turned, 1)
            act.activation(e.lnT[:, :, :, :], banks[4][0:DP, 0:4 * NE].rearrange("p (v k n) -> p v k n", v=2, k=KD),
                           ACT.Copy).then_inc(wT_ready, 1)
            act.wait_ge(norm_step, KD + 1)
            act.activation(rn[:, :, :], rn[:, :, :], ACT.Sqrt).then_inc(norm_step, 1)
            for c in range(NCH):
                for k in range(KD):
                    act.wait_ge(x_turned, KD * c + k + 1)
                    act.activation(xT[:, k, c * CH:(c + 1) * CH], banks[(c % 2) * KD + k][0:DP, :],
                                   ACT.Copy).then_inc(xT_ready, 1)
            for j in range(2 * NT):
                act.wait_ge(lg_done, j + 1)
                act.activation(e.lg[:, j // 2, (j % 2) * CH:(j % 2 + 1) * CH], banks[4 + j % 4][:, :],
                               ACT.Copy).then_inc(lg_ready, 1)
            act.wait_ge(cmax_rep, 1)
            for f in range(2):
                act.activation(e.cmax[:, f * CH:(f + 1) * CH], banks[2 + f][:, :], ACT.Copy).then_inc(cmax_ready, 1)

        @block.vector
        def _(dve):
            scale_rows(dve, g, e.norm3, g.x, e.xm, NT, 1e-5, counted=False)
            dve.wait_ge(square_ready, 2 * KD)
            for k in range(KD):
                dve.tensor_reduce(rn[:, k, :], sq[:, k, :].rearrange("p (n q) -> p q n", q=SL), AX.X,
                                  ALU.add).then_inc(norm_step, 1)
            dve.wait_ge(norm_step, KD)
            dve.tensor_scalar(rn[:, :, :], rn[:, :, :], 1e-6, None, ALU.add).then_inc(norm_step, 1)
            dve.wait_ge(norm_step, KD + 2)
            dve.reciprocal(rn[:, :, :], rn[:, :, :]).then_inc(norm_step, 1)
            dve.wait_ge(norm_step, KD + 3)
            dve.wait_ge(phi_ready, 2 * KD)
            for k in range(KD):
                v = phiT[:, k, :].rearrange("p (n q) -> p n q", q=SL)
                dve.tensor_tensor(v, v, rn[:, k, :].unsqueeze(1).broadcast_to([DP, NE, SL]),
                                  ALU.mult).then_inc(phiT_ready, 1)
            for i in range(NT):
                dve.wait_ge(lg_ready, 2 * (i + 1))
                dve.tensor_reduce(e.rmax[:, i:i + 1], e.lg[:, i, :], AX.X, ALU.max,
                                  negate=True).then_inc(rmax_ready, 1)
                if i:
                    dve.wait_ge(cmax_step, i)
                    dve.tensor_tensor(cm[:, :], cm[:, :], e.lg[:, i, :], ALU.max).then_inc(cmax_step, 1)
                else:
                    dve.tensor_copy(cm[:, :], e.lg[:, i, :]).then_inc(cmax_step, 1)
            dve.wait_ge(cmax_turned, 1)
            for f in range(2):
                dve.tensor_reduce(cc[:, 4 * f:4 * f + 4], banks[f][:, :].rearrange("p (s t) -> p s t", t=P), AX.X,
                                  ALU.max).then_inc(cmax_col, 1)
            dve.wait_ge(cmax_col, 2)
            for s in range(ST):
                dve.tensor_scalar(dg[:, s, :], g.ident[:, :], cc[:, s:s + 1], None, ALU.mult).then_inc(cmax_diag, 1)
            dve.wait_ge(cmax_ready, 2)
            dve.wait_ge(rmax_ready, NT)
            dve.wait_ge(e.norm3.rows, NT)


def moe_gather_slots(nc, g, e):
    arg_ready, exp_ready, used, sum_done, recip, rows_ready, c_exp = sems(
        nc, g, "slot_arg_ready slot_exp_ready slot_exp_used slot_sum_done slot_recip slot_rows_ready combine_exp")
    with ExitStack() as local:
        def sb(name, shape, dt=F32):
            return local.enter_context(nc.sbuf_tensor(name, shape, dt))
        ed = sb("dispatch", [P, 3, S])
        rc = sb("dispatch_recip", [P, ST])
        banks = [local.enter_context(nc.psum_tensor(f"db{i}", [P, CH], F32)) for i in range(4)]
        block = local.enter_context(nc.Block())
        D1 = D + 1

        @block.sync
        def _(sp):
            load_up(sp, g, e, 1)
            load_down(sp, g, e, 1)

        @block.vector
        def _(dve):
            for i in range(NT):
                if i >= 3:
                    dve.wait_ge(used, i - 2)
                dve.tensor_tensor(ed[:, i % 3, :], e.lg[:, i, :], e.cmax[:, :], ALU.subtract).then_inc(arg_ready, 1)
            dve.wait_ge(sum_done, 1)
            for s in range(ST):
                b = banks[s // 2][:, (s % 2) * D1:(s % 2 + 1) * D1]
                dve.reciprocal(rc[:, s:s + 1], b[:, D:D1]).then_inc(recip, 1)
            for s in range(ST):
                b = banks[s // 2][:, (s % 2) * D1:(s % 2 + 1) * D1]
                dve.wait_ge(recip, s + 1)
                dve.tensor_scalar(e.xs[:, s, :], b[:, 0:D], rc[:, s:s + 1], None, ALU.mult).then_inc(rows_ready, 1)
            dve.wait_ge(rows_ready, ST)

        @block.scalar
        def _(act):
            for i in range(NT):
                act.wait_ge(arg_ready, i + 1)
                act.activation(ed[:, i % 3, :], ed[:, i % 3, :], ACT.Exp).then_inc(exp_ready, 1)
                act.activation(e.lg[:, i, :], e.lg[:, i, :], ACT.Exp, bias=e.rmax[:, i:i + 1],
                               accum_out=e.csum[:, i:i + 1]).then_inc(c_exp, 1)
            act.wait_ge(c_exp, NT)

        @block.tensor
        def _(pe):
            for i in range(NT):
                pe.wait_ge(exp_ready, i + 1)
                for s in range(ST):
                    ins = pe.matmul(banks[s // 2][:, (s % 2) * D1:(s % 2 + 1) * D1], ed[:, i % 3, s * P:(s + 1) * P],
                                    e.xm[:, i, :], start=(i == 0 and s % 2 == 0), stop=(i == NT - 1),
                                    skip_group_check=True)
                ins.then_inc(used, 1)
            pe.matmul(banks[3][0:1, 2 * D1:2 * D1 + 2], g.ident[:, 0:1], g.ident[:, 0:2], start=False, stop=True,
                      skip_group_check=True).then_inc(sum_done, 1)


def load_up(sp, g, e, t):
    for q in range(PR):
        n = EG * t + 2 * q
        sp.dma_start(e.w1[t % 2][:, q], g.ffn["w1"][n:n + 2].rearrange("e (k p) h -> p e k h", p=DP)) \
          .then_inc(e.w1_in[t % 2], 16)


def load_down(sp, g, e, t):
    for q in range(PR):
        n = EG * t + 2 * q
        sp.dma_start(e.w2[t % 2][:, q], g.ffn["w2"][n:n + 2].rearrange("e (p m) d -> p e m d", m=MH)) \
          .then_inc(e.w2_in[t % 2], 16)


def moe_experts(nc, g, e):
    (zeroed, turned, scaled, slots_ready, up_done, gelu_ready, h_turned, hT_ready, down_done, ys_ready,
     c_turned, c_ready, y_done, c_recip, added, s_out) = sems(nc, g, " ".join("ex_" + n for n in (
         "zeroed slots_turned slots_scaled slots_ready up_done gelu_ready h_turned hT_ready "
         "down_done results_ready combine_turned combine_ready y_done combine_recip added "
         "rows_out").split()))
    b1_in = sems(nc, g, "ex_b1_in_even ex_b1_in_odd")
    b2_in = sems(nc, g, "ex_b2_in_even ex_b2_in_odd")
    with ExitStack() as local, nc.allow_non_contiguous_dma(reason="small weights"):
        def sb(name, shape, dt=F32):
            return local.enter_context(nc.sbuf_tensor(name, shape, dt))
        w1, w2 = e.w1, e.w2
        b1 = sb("ex_b1", [EG, 2, HE])
        b2 = sb("ex_b2", [EG, 2, D])
        xT = [sb(f"slots_T{v}", [DP, KD, S]) for v in range(2)]
        tmp = sb("slots_scaled", [DP, 2, CH])
        hg = sb("gelu_rows", [P, 2, HE])
        hT = [sb(f"gelu_T{v}", [P, MH, P]) for v in range(2)]
        ys = sb("slot_results", [P, ST, D])
        rr = sb("combine_recip", [P, NT])
        banks = [local.enter_context(nc.psum_tensor(f"xb{i}", [P, CH], F32)) for i in range(8)]
        block = local.enter_context(nc.Block())
        I = g.ffn
        PARTS = ((0, ST // 2), (ST // 2, ST))
        order = [(i, f) for f in range(len(PARTS)) for i in range(NT)]
        cuts = (0, 5, 10, 14)
        sums = {5 + k: order[cuts[k]:cuts[k + 1]] for k in range(3)}
        sums[ST] = order[cuts[-1]:]

        @block.sync
        def _(sp):
            for t in range(ST):
                if t >= 2:
                    sp.wait_ge(up_done, t - 1)
                sp.dma_start(b1[:, t % 2, :], I["b1"][EG * t:EG * (t + 1), :]).then_inc(b1_in[t % 2], 16)
                if t >= 2:
                    load_up(sp, g, e, t)
                    sp.wait_ge(down_done, t - 1)
                sp.dma_start(b2[:, t % 2, :], I["b2"][EG * t:EG * (t + 1), :]).then_inc(b2_in[t % 2], 16)
                if t >= 2:
                    load_down(sp, g, e, t)
            for i in range(NT):
                sp.wait_ge(added, (len(PARTS) - 1) * NT + i + 1)
                sp.dma_start(g.out[0, i * P:(i + 1) * P, :], g.x[:, i, :]).then_inc(s_out, 16)
            sp.wait_ge(s_out, 16 * NT)

        @block.gpsimd
        def _(pool):
            for v in range(2):
                pool.memset(xT[v][:, :, :], 0.0).then_inc(zeroed, 1)
                pool.memset(hT[v][:, :, :], 0.0).then_inc(zeroed, 1)

        @block.tensor
        def _(pe):
            def combine_transposes(i):
                if i:
                    pe.wait_ge(c_ready, 2 * i)
                for s in range(ST):
                    ins = pe.transpose(banks[6 + s // 4][:, (s % 4) * P:(s % 4 + 1) * P],
                                       e.lg[:, i, s * P:(s + 1) * P], g.ident[:, :])
                ins.then_inc(c_turned, 1)

            def combine(i, f):
                n = order.index((i, f))
                s0, s1 = PARTS[f]
                pe.wait_ge(c_ready, 2 * (i + 1))
                pe.wait_ge(ys_ready, s1)
                if n >= 2:
                    pe.wait_ge(added, n - 1)
                for s in range(s0, s1):
                    ins = pe.matmul(banks[1 + 4 * (n % 2)][:, 0:D], e.lg[:, i, s * P:(s + 1) * P], ys[:, s, :],
                                    start=(s == s0), stop=(s == s1 - 1))
                ins.then_inc(y_done, 1)

            for k in range(KD):
                for f in range(2):
                    for s in range(ST // 2):
                        ins = pe.transpose(banks[2 * k + f][0:DP, s * P:(s + 1) * P],
                                           e.xs[:, f * ST // 2 + s, k * DP:(k + 1) * DP], g.ident[:, :])
                    ins.then_inc(turned, 1)
            pe.wait_ge(zeroed, 4)
            pe.wait_ge(slots_ready, 4 * KD)
            for t in range(ST):
                for i, f in sums.get(t, ()):
                    combine(i, f)
                up, down = banks[0], banks[2 + t % 2]
                pe.wait_ge(b1_in[t % 2], 16 * (t // 2 + 1))
                pe.matmul(up[:, 0:HE], g.slot_of[:, :], b1[:, t % 2, :], start=True, stop=False, skip_group_check=True)
                pe.wait_ge(e.w1_in[t % 2], 16 * PR * (t // 2 + 1))
                for v in range(2):
                    for k in range(KD):
                        for q in range(PR):
                            ins = pe.matmul(up[32 * q:32 * q + 32, 0:HE],
                                            xT[v][:, k, t * P + 32 * q:t * P + 32 * q + 32],
                                            w1[t % 2][:, q, v, k, :], start=False,
                                            stop=(v == 1 and k == KD - 1), skip_group_check=True)
                ins.then_inc(up_done, 1)
                combine_transposes(2 * t)
                pe.wait_ge(gelu_ready, t + 1)
                if t:
                    pe.wait_ge(hT_ready, 2 * t)
                for m in range(MH):
                    ins = pe.transpose(banks[4][:, m * P:(m + 1) * P], hg[:, t % 2, m:HE:MH], g.ident[:, :])
                ins.then_inc(h_turned, 1)
                combine_transposes(2 * t + 1)
                pe.wait_ge(hT_ready, 2 * (t + 1))
                if t >= 2:
                    pe.wait_ge(ys_ready, t - 1)
                pe.wait_ge(b2_in[t % 2], 16 * (t // 2 + 1))
                pe.wait_ge(e.w2_in[t % 2], 16 * PR * (t // 2 + 1))
                pe.matmul(down[:, 0:D], g.slot_of[:, :], b2[:, t % 2, :], start=True, stop=False, skip_group_check=True)
                for v in range(2):
                    for m in range(MH):
                        for q in range(PR):
                            ins = pe.matmul(down[32 * q:32 * q + 32, 0:D], hT[v][:, m, 32 * q:32 * q + 32],
                                            w2[t % 2][:, q, v, m, :], start=False,
                                            stop=(v == 1 and m == MH - 1), skip_group_check=True)
                ins.then_inc(down_done, 1)
            for i, f in sums[ST]:
                combine(i, f)

        @block.scalar
        def _(act):
            act.preload_act_table(ACT.Gelu)
            for t in range(ST):
                act.wait_ge(up_done, t + 1)
                if t >= 2:
                    act.wait_ge(h_turned, t - 1)
                act.activation(hg[:, t % 2, :], banks[0][:, 0:HE], ACT.Gelu).then_inc(gelu_ready, 1)
                act.wait_ge(down_done, t + 1)
                act.activation(ys[:, t, :], banks[2 + t % 2][:, 0:D], ACT.Copy).then_inc(ys_ready, 1)

        @block.vector
        def _(dve):
            dve.wait_ge(zeroed, 4)
            n = 0
            for k in range(KD):
                for f in range(2):
                    dve.wait_ge(turned, 2 * k + f + 1)
                    if n >= 2:
                        dve.wait_ge(slots_ready, 2 * (n - 1))
                    tv = tmp[:, n % 2, :].rearrange("p (n q) -> p n q", q=SL)
                    gn = slice(f * NE // 2, (f + 1) * NE // 2)
                    dve.tensor_tensor(tv, banks[2 * k + f][0:DP, :].rearrange("p (n q) -> p n q", q=SL),
                                      e.lnT[:, 0, k, gn].unsqueeze(2).broadcast_to([DP, NE // 2, SL]),
                                      ALU.mult).then_inc(scaled, 1)
                    dve.wait_ge(scaled, n + 1)
                    for v in range(2):
                        xv = xT[v][:, k, f * CH:(f + 1) * CH].rearrange("p (n q) -> p n q", q=SL)[:, v:NE // 2:2, :]
                        bn = e.lnT[:, 1, k, f * NE // 2 + v:(f + 1) * NE // 2:2]
                        dve.tensor_tensor(xv, tv[:, v:NE // 2:2, :],
                                          bn.unsqueeze(2).broadcast_to([DP, NE // 4, SL]),
                                          ALU.add).then_inc(slots_ready, 1)
                    n += 1

            def add(i, f):
                n = order.index((i, f))
                dve.wait_ge(y_done, n + 1)
                if f:
                    dve.wait_ge(added, order.index((i, f - 1)) + 1)
                dve.scalar_tensor_tensor(out=g.x[:, i, :], in0=banks[1 + 4 * (n % 2)][:, 0:D], scalar=rr[:, i:i + 1],
                                         in1=g.x[:, i, :], op0=ALU.mult, op1=ALU.add).then_inc(added, 1)

            def combine_copy(i):
                dve.wait_ge(c_turned, i + 1)
                for f in range(2):
                    dve.tensor_copy(e.lg[:, i, f * CH:(f + 1) * CH], banks[6 + f][:, :]).then_inc(c_ready, 1)

            for t in range(ST):
                for i, f in sums.get(t, ()):
                    add(i, f)
                combine_copy(2 * t)
                dve.wait_ge(h_turned, t + 1)
                if t:
                    dve.wait_ge(down_done, t)
                src = banks[4][:, 0:MH * P].rearrange("p (m q v s) -> p m q v s", m=MH, v=2, s=SL)
                for v in range(2):
                    for_v = hT[v][:, :, :].rearrange("p m (q v s) -> p m q v s", v=2, s=SL)
                    dve.tensor_copy(for_v[:, :, :, v, :], src[:, :, :, v, :]).then_inc(hT_ready, 1)
                combine_copy(2 * t + 1)
                if t == 0:
                    dve.reciprocal(rr[:, :], e.csum[:, :]).then_inc(c_recip, 1)
                    dve.wait_ge(c_recip, 1)
            for i, f in sums[ST]:
                add(i, f)


def lm_tower(nc, ins, out):
    g = Core()
    g.live = []
    g.out = out
    g.ids = ins["x"]
    g.tok = {k[7:]: v for k, v in ins.items() if k.startswith("L0_tok_")}
    g.attn = {k[8:]: v for k, v in ins.items() if k.startswith("L0_attn_")}
    g.ffn = {k[7:]: v for k, v in ins.items() if k.startswith("L0_ffn_")}
    g.ctx = ExitStack()
    with g.ctx as ctx:
        def sb(name, shape, dt=F32):
            return ctx.enter_context(nc.sbuf_tensor(name, shape, dt))
        g.x = sb("x_rows", [P, NT, D])
        g.ident = sb("ident", [P, P])
        g.nst = sb("norm_stats", [P, NT, 6])
        g.nmv = sb("norm_mean_var", [P, NT, 2])
        g.nrs = sb("norm_scale", [P, NT])
        g.causal = sb("causal", [P, P])
        g.ones = sb("ones", [P, P])
        g.slot_of = sb("slot_of", [EG, P])
        g.head_of = sb("head_of", [DP, HK])
        with ExitStack() as mamba:
            def mb(name, shape, dt=F32):
                return mamba.enter_context(nc.sbuf_tensor(name, shape, dt))
            g.sel = mb("sel", [3 * NX, NX, P], BF16)
            g.w_in = mb("w_in", [DP, KD, 2 * DI])
            g.norm_w_c = mb("norm_w_c", [DP, NL, KD])
            g.conv_wc = mb("conv_wc", [P, NL, MI, TAPS])
            g.conv_bc = mb("conv_bc", [P, NL, MI])
            g.w_x = mb("w_x", [P, NL, MI, NX + RK])
            g.w_dt = mb("w_dt", [RK, NL, DI])
            g.dt_bc = mb("dt_bc", [P, NL, MI])
            g.a_neg = mb("a_neg", [P, NL, MI, NS])
            g.d_c = mb("d_c", [P, NL, MI])
            g.w_out = mb("w_out", [P, NL, MI, D])
            g.xr = mb("xr", [P, MI, L + TAPS - 1])
            g.sres = mb("sres", [P, MI, L])
            g.u = mb("u", [P, MI, L])
            g.delta = mb("delta", [P, MI, L])
            g.du = mb("du", [P, MI, L])
            g.bcp = mb("bcp", [3 * NX, L + CH], BF16)
            load_and_gather(nc, g)
            for l in range(NL):
                mamba_front(nc, g, l)
                mamba_scan(nc, g, l)
                retire_semaphores(nc, g)
        with ExitStack() as attn:
            a = g.a = Core()
            def ab(name, shape, dt=F32):
                return attn.enter_context(nc.sbuf_tensor(name, shape, dt))
            a.xa = ab("xa", [P, NT, D])
            a.xs = ab("xs_attn", [P, NT, D])
            place = ab("keys_or_outputs", [P, 2 * KD * L])
            k_cols = [place[0:DP, v * KD * L:(v + 1) * KD * L].rearrange("p (k t) -> p k t", k=KD)
                      for v in range(2)]
            a.oT = place[:, 0:HG * L].rearrange("p (h t) -> p h t", h=HG)
            a.w_o = ab("w_o", [P, HG, D])
            a.proj_blocks = ab("proj_blocks", [DP, HK, M])
            a.neg_kmax = ab("neg_kmax", [P, 1])
            with ExitStack() as qkv:
                def qb(name, shape, dt=F32):
                    return qkv.enter_context(nc.sbuf_tensor(name, shape, dt))
                a.qk = (qb("q_T", [DP, KD, L]), k_cols[0])
                a.qk2 = (qb("q_squares_T", [DP, KD, L]), k_cols[1])
                a.v = qb("v_rows", [P, NT, H, VE])
                with ExitStack() as proj:
                    def pb(name, shape, dt=F32):
                        return proj.enter_context(nc.sbuf_tensor(name, shape, dt))
                    a.w_qkv = pb("w_qkv", [DP, 3, KD, D])
                    a.ln1_gb = pb("ln1_gb", [DP, 2, KD])
                    a.qk_bias = pb("qk_bias", [DP, 2, KD])
                    a.bv = pb("bv_rows", [P, D])
                    a.bo = pb("bo_rows", [P, D])
                    with nc.Block() as block:
                        @block.gpsimd
                        def _(pool):
                            pool.memset(a.proj_blocks[:, :, :], 0.0)
                            pool.memset(a.w_o[:, :, :], 0.0)
                    a.w_in, = sems(nc, g, "attn_w_in")
                    a.n_w_in = 16 * (9 + HQ + HK)
                    a.norm1 = norm_sems(nc, g, "norm1")
                    normalize_rows(nc, g, "norm0", g.x, a.xa, 1e-5, load_attention, a.norm1)
                    attn_project(nc, g, a)
                a.kdd = qb("k_dd", [P, NT, KD, HK, M])
                attn_key_logits(nc, g, a)
                attention(nc, g, a)
            a.mlp_w = (ab("mlp_w1", [DP, KD, FF]), ab("mlp_w2", [P, MF, D]), ab("ln2_gb", [DP, 2, KD]),
                       ab("mlp_b1", [P, MF]), ab("mlp_b2_rows", [P, D]))
            a.norm2 = norm_sems(nc, g, "norm2")
            attn_output(nc, g, a)
            g.norm3 = norm_sems(nc, g, "norm3")
            attn_mlp(nc, g, a)
            retire_semaphores(nc, g)
        with ExitStack() as moe:
            e = g.e = Core()
            def eb(name, shape, dt=F32):
                return moe.enter_context(nc.sbuf_tensor(name, shape, dt))
            e.lg = eb("logits", [P, NT, S])
            e.rmax = eb("neg_rmax", [P, NT])
            e.csum = eb("combine_sum", [P, NT])
            e.lnT = eb("expert_ln_T", [DP, 2, KD, NE])
            e.xs = eb("slot_rows", [P, ST, D])
            w1 = eb("expert_w1", [DP, PR, 2, KD, HE])
            w2 = eb("expert_w2", [P, PR, 2, MH, D])
            e.w_place = eb("expert_w_odd", [P, W1C + W2C])
            e.w1 = (w1, e.w_place[0:DP, 0:W1C].rearrange("p (q v k h) -> p q v k h", q=PR, v=2, k=KD))
            e.w2 = (w2, e.w_place[:, W1C:W1C + W2C].rearrange("p (q v m d) -> p q v m d", q=PR, v=2, m=MH))
            e.w1_in = sems(nc, g, "expert_w1_in_even expert_w1_in_odd")
            e.w2_in = sems(nc, g, "expert_w2_in_even expert_w2_in_odd")
            with ExitStack() as rows:
                e.xm = rows.enter_context(nc.sbuf_tensor("moe_rows", [P, NT, D + 1], F32))
                e.cmax = rows.enter_context(nc.sbuf_tensor("cmax", [P, S], F32))
                e.lng = rows.enter_context(nc.sbuf_tensor("expert_ln", [NE, 2, D], F32))
                e.phi = e.w_place[:, 0:ST * D].rearrange("p (a d) -> p a d", d=D)
                e.phi_in, = sems(nc, g, "phi_in")
                with nc.Block() as block:
                    @block.gpsimd
                    def _(pool):
                        pool.memset(e.xm[:, :, D:D + 1], 1.0)

                    @block.sync
                    def _(sp):
                        load_phi(sp, g)
                e.norm3 = norm_sems(nc, g, "norm3_scale")
                moe_logits(nc, g, e)
                moe_gather_slots(nc, g, e)
            normalize_rows(nc, g, "norm4", e.xs, e.xs, 1e-5)
            moe_experts(nc, g, e)


_INS = ["x"] + ["L0_tok_" + n for n in (
    "emb", "norm_w", "in_proj_w", "conv_w", "conv_b", "x_proj_w", "dt_proj_w", "dt_proj_b", "A_log", "D",
    "out_proj_w")] + ["L0_attn_" + n for n in (
        "ln1_g", "ln1_b", "Wq", "bq", "Wk", "bk", "Wv", "bv", "Wo", "bo", "proj", "ln2_g", "ln2_b", "W1", "b1",
        "W2", "b2")] + ["L0_ffn_" + n for n in ("phi", "ln_g", "ln_b", "w1", "b1", "w2", "b2")]


def kernel(**inputs):
    import numpy as _np
    import concourse.bacc as _bacc
    from concourse import mybir as _mybir
    from concourse.bass_utils import run_bass_kernel_spmd as _run

    nc = _bacc.Bacc("TRN2", target_bir_lowering=False, num_devices=1)
    arrays, ins = {}, {}
    for name in _INS:
        a = _np.ascontiguousarray(inputs[name])
        arrays[f"in_{name}_dram"] = a
        ins[name] = nc.dram_tensor(f"in_{name}_dram", a.shape, _mybir.dt.from_np(a.dtype), kind="ExternalInput").ap()
    out = nc.dram_tensor("out_0_dram", (1, L, D), _mybir.dt.float32, kind="ExternalOutput").ap()
    lm_tower(nc, ins, out)
    r = _run(nc, [arrays], core_ids=[0])
    return r.results[0]["out_0_dram"]
```
